# Optimizing a Trainium2 kernel written in Bass

```python
import numpy as np
import jax
import jax.numpy as jnp

def _softmax(x, axis=-1):
    return jax.nn.softmax(x, axis=axis)

def _gelu(x):
    return jax.nn.gelu(x, approximate=True)

def _silu(x):
    return jax.nn.silu(x)

def _sigmoid(x):
    return jax.nn.sigmoid(x)

def _layernorm(x, axis=-1, eps=1e-05):
    m = jnp.mean(x, axis=axis, keepdims=True)
    v = jnp.var(x, axis=axis, keepdims=True)
    return (x - m) / jnp.sqrt(v + eps)

def _scatter_add(tgt, idx, src, axis=0):
    return tgt.at[idx].add(src)

def _segment_sum(src, seg, n):
    return jax.ops.segment_sum(src, seg, n)
kernel_name = 'mk_xattn_ffn_d4_seqx_r8_6b7468'

def setup_inputs(seed: int=0):
    np.random.seed(seed)
    _w = jnp.asarray

    def _rec_inputs():
        import jax
        import jax.numpy as jnp
        _rk = jax.random.key(seed)
        x = -0.0002928 + 1 * jax.random.normal(jax.random.fold_in(_rk, 1), (16, 256, 128), jnp.float32)
        _lenS = 256 - jax.random.randint(jax.random.fold_in(_rk, 7), (16,), 0, max(1, 256 // 4) + 1, jnp.int32)
        _lenS2 = 64 - jax.random.randint(jax.random.fold_in(_rk, 8), (16,), 0, max(1, 64 // 4) + 1, jnp.int32)
        _ctx_1024P = jax.random.normal(jax.random.fold_in(_rk, 11), (16, 16, 128), jnp.float32)
        _ctx_1024c = jax.random.dirichlet(jax.random.fold_in(_rk, 511), 0.3 * jnp.ones((16,), jnp.float32), (16, 64))
        _ctx_1024t = jnp.einsum('bsk,bkd->bsd', _ctx_1024c, _ctx_1024P)
        _ctx_1024t = _ctx_1024t * jax.lax.rsqrt(jnp.mean(jnp.square(_ctx_1024t)) + 1e-12) * 0.953939
        ctx_1024 = -1.39393e-06 + 0.999914 * (_ctx_1024t + 0.3 * jax.random.normal(jax.random.fold_in(_rk, 611), (16, 64, 128), jnp.float32))
        _validS = jnp.arange(256)[None, :] < _lenS[:, None]
        _validS2 = jnp.arange(64)[None, :] < _lenS2[:, None]
        _causal = jnp.tril(jnp.ones((256, 256), dtype=bool))
        mask_Bx1xSxS2_ik1 = jnp.where(jnp.broadcast_to(_validS2[:, None, None, :], (16, 1, 256, 64)), 1, 0).astype(jnp.int32)
        return (x, ctx_1024, mask_Bx1xSxS2_ik1)
    x, ctx_1024, mask_Bx1xSxS2_ik1 = _rec_inputs()

    def _L0_xattn_setup():
        import jax, jax.numpy as jnp
        import numpy as np
        B, N, D_MODEL, H, DH = (2, 256, 128, 16, 64)
        SCALE = DH ** (-0.5)
        key = jax.random.key(seed)
        ks = jax.random.split(key, 6)

        def lin(k, fan_in, shape):
            return jax.random.normal(k, shape, dtype=jnp.float32) / np.sqrt(fan_in)
        return {'x': jax.random.normal(ks[0], (B, N, D_MODEL), dtype=jnp.float32), 'context': jax.random.normal(ks[1], (B, N, D_MODEL), dtype=jnp.float32), 'Wq': lin(ks[2], D_MODEL, (D_MODEL, H * DH)), 'Wk': lin(ks[3], D_MODEL, (D_MODEL, H * DH)), 'Wv': lin(ks[4], D_MODEL, (D_MODEL, H * DH)), 'Wo': lin(ks[5], H * DH, (H * DH, D_MODEL)), 'bo': jnp.zeros((D_MODEL,), dtype=jnp.float32)}
    _L0_xattn_all = _L0_xattn_setup()
    _L0_xattn_in = {k: v for k, v in _L0_xattn_all.items() if k in ('Wq', 'Wk', 'Wv', 'Wo', 'bo')}
    del _L0_xattn_all

    def _L0_ffn_setup():
        import jax, jax.numpy as jnp
        import numpy as np
        B, S, D, H, E = (64, 128, 128, 64, 8)
        EPS = 1e-05
        key = jax.random.key(seed)
        ks = jax.random.split(key, 8)
        x = jax.random.normal(ks[0], (B, S, D), jnp.float32)
        return {'x': x, 'ln_g': jnp.ones((D,), jnp.float32), 'ln_b': jnp.zeros((D,), jnp.float32), 'bn_g': jnp.ones((D,), jnp.float32), 'bn_b': jnp.zeros((D,), jnp.float32), 'bn_mean': jax.random.normal(ks[1], (D,), jnp.float32) * 0.01, 'bn_var': jnp.ones((D,), jnp.float32), 'Wr': jax.random.normal(ks[2], (D, E), jnp.float32) * 0.02, 'br': jnp.zeros((E,), jnp.float32), 'W_down': jax.random.normal(ks[3], (E, D, H), jnp.float32) * 0.02, 'b_down': jnp.zeros((E, H), jnp.float32), 'W_up': jax.random.normal(ks[4], (E, H, D), jnp.float32) * 0.02, 'b_up': jnp.zeros((E, D), jnp.float32)}
    _L0_ffn_all = _L0_ffn_setup()
    _L0_ffn_in = {k: v for k, v in _L0_ffn_all.items() if k in ('ln_g', 'ln_b', 'bn_g', 'bn_b', 'bn_mean', 'bn_var', 'Wr', 'br', 'W_down', 'b_down', 'W_up', 'b_up')}
    del _L0_ffn_all

    def _L1_xattn_setup():
        import jax, jax.numpy as jnp
        import numpy as np
        HEADS = 16
        key = jax.random.key(seed)
        k1, k2, k3, k4 = jax.random.split(key, 4)
        B, T, S, W = (2, 256, 256, 128)
        x = jax.random.normal(k1, (B, T, W), dtype=jnp.float32)
        cond_k = jax.random.normal(k2, (B, S, W), dtype=jnp.float32)
        cond_v = jax.random.normal(k3, (B, S, W), dtype=jnp.float32)
        w_proj = jax.random.normal(k4, (W, W), dtype=jnp.float32) * 0.02
        b_proj = jnp.zeros((W,), dtype=jnp.float32)
        return {'x': x, 'cond_k': cond_k, 'cond_v': cond_v, 'w_proj': w_proj, 'b_proj': b_proj}
    _L1_xattn_all = _L1_xattn_setup()
    _L1_xattn_in = {k: v for k, v in _L1_xattn_all.items() if k in ('w_proj', 'b_proj')}
    del _L1_xattn_all

    def _L1_ffn_setup():
        import jax, jax.numpy as jnp
        import numpy as np
        from jax import lax
        D = 128
        H = 176
        E = 8
        K = 2
        ROUTER_SCALE = 1.0

        def _expert(x, w1, b1, w3, b3, w2, b2):
            h = jax.nn.silu((x @ w1 + b1) * (x @ w3 + b3))
            return h @ w2 + b2
        key = jax.random.key(seed)
        ks = jax.random.split(key, 16)
        s = 0.02
        inp = {'x': jax.random.normal(ks[0], (2, 256, D), dtype=jnp.float32), 'gate_w': jax.random.normal(ks[1], (E, D), dtype=jnp.float32) * s, 'gate_b': jax.random.normal(ks[2], (E,), dtype=jnp.float32) * s, 'w1': jax.random.normal(ks[3], (E, D, H), dtype=jnp.float32) * s, 'b1': jax.random.normal(ks[4], (E, H), dtype=jnp.float32) * s, 'w3': jax.random.normal(ks[5], (E, D, H), dtype=jnp.float32) * s, 'b3': jax.random.normal(ks[6], (E, H), dtype=jnp.float32) * s, 'w2': jax.random.normal(ks[7], (E, H, D), dtype=jnp.float32) * s, 'b2': jax.random.normal(ks[8], (E, D), dtype=jnp.float32) * s, 'sw1': jax.random.normal(ks[9], (D, H), dtype=jnp.float32) * s, 'sb1': jax.random.normal(ks[10], (H,), dtype=jnp.float32) * s, 'sw3': jax.random.normal(ks[11], (D, H), dtype=jnp.float32) * s, 'sb3': jax.random.normal(ks[12], (H,), dtype=jnp.float32) * s, 'sw2': jax.random.normal(ks[13], (H, D), dtype=jnp.float32) * s, 'sb2': jax.random.normal(ks[14], (D,), dtype=jnp.float32) * s}
        return inp
    _L1_ffn_all = _L1_ffn_setup()
    _L1_ffn_in = {k: v for k, v in _L1_ffn_all.items() if k in ('gate_w', 'gate_b', 'w1', 'b1', 'w3', 'b3', 'w2', 'b2', 'sw1', 'sb1', 'sw3', 'sb3', 'sw2', 'sb2')}
    del _L1_ffn_all

    def _L2_xattn_setup():
        import jax, jax.numpy as jnp
        import numpy as np
        import math
        HEAD = 16
        D_MODEL = 128
        HEAD_DIM = D_MODEL // HEAD
        B, S = (2, 256)
        key = jax.random.key(seed)
        ks = jax.random.split(key, 9)
        sc = 1.0 / math.sqrt(D_MODEL)
        return {'q': jax.random.normal(ks[0], (B, S, D_MODEL), dtype=jnp.float32), 'k': jax.random.normal(ks[1], (B, S, D_MODEL), dtype=jnp.float32), 'v': jax.random.normal(ks[2], (B, S, D_MODEL), dtype=jnp.float32), 'mask': jax.random.randint(ks[3], (B, 1, S, S), 0, 2, dtype=jnp.int32), 'wq': jax.random.normal(ks[4], (D_MODEL, D_MODEL), dtype=jnp.float32) * sc, 'wk': jax.random.normal(ks[5], (D_MODEL, D_MODEL), dtype=jnp.float32) * sc, 'wv': jax.random.normal(ks[6], (D_MODEL, D_MODEL), dtype=jnp.float32) * sc, 'wo': jax.random.normal(ks[7], (D_MODEL, D_MODEL), dtype=jnp.float32) * sc, 'bo': jax.random.normal(ks[8], (D_MODEL,), dtype=jnp.float32) * 0.01}
    _L2_xattn_all = _L2_xattn_setup()
    _L2_xattn_in = {k: v for k, v in _L2_xattn_all.items() if k in ('wq', 'wk', 'wv', 'wo', 'bo')}
    del _L2_xattn_all

    def _L2_ffn_setup():
        import jax, jax.numpy as jnp
        import numpy as np
        import math
        HID, HD, E, MIN_E = (128, 128, 16, 2)
        B, T = (4, 256)
        IS_CAUSAL = True

        def _l2norm(x, axis):
            return x / jnp.sqrt(jnp.sum(x * x, axis=axis, keepdims=True) + 1e-12)

        def _gating(hidden_states, sim_matrix, gates):
            b, t, c = hidden_states.shape
            flat = hidden_states.reshape(b * t, c)
            logits = _l2norm(flat, -1) @ _l2norm(sim_matrix, 0) - jax.nn.sigmoid(gates)
            gated = jax.nn.relu(logits)
            mask = (gated > 0).astype(gated.dtype)
            inactive = jnp.sum(mask, axis=1) == 0
            _, top_idx = jax.lax.top_k(logits, MIN_E)
            fb = jnp.sum(jax.nn.one_hot(top_idx, E, dtype=mask.dtype), axis=1)
            mask = mask + inactive[:, None].astype(mask.dtype) * fb
            masked = jnp.where(mask > 0, gated, -jnp.inf)
            probs = jax.nn.softmax(masked, axis=-1)
            return probs
        key = jax.random.key(seed)
        ks = jax.random.split(key, 6)
        a_qkv = math.sqrt(6.0 / (HID + HD))
        a_o = math.sqrt(6.0 / (HD + HID))
        return {'hidden_states': jax.random.normal(ks[0], (B, T, HID), jnp.float32), 'sim_matrix': jax.random.normal(ks[1], (HID, E), jnp.float32), 'gates': jnp.zeros((E,), jnp.float32), 'q_proj': jax.random.uniform(ks[2], (E, HID, HD), jnp.float32, -a_qkv, a_qkv), 'k_proj': jax.random.uniform(ks[3], (E, HID, HD), jnp.float32, -a_qkv, a_qkv), 'v_proj': jax.random.uniform(ks[4], (E, HID, HD), jnp.float32, -a_qkv, a_qkv), 'o_proj': jax.random.uniform(ks[5], (E, HD, HID), jnp.float32, -a_o, a_o)}
    _L2_ffn_all = _L2_ffn_setup()
    _L2_ffn_in = {k: v for k, v in _L2_ffn_all.items() if k in ('sim_matrix', 'gates', 'q_proj', 'k_proj', 'v_proj', 'o_proj')}
    del _L2_ffn_all

    def _L3_xattn_setup():
        import jax, jax.numpy as jnp
        import numpy as np
        H = 16
        DIM = 128
        DK = DIM // H
        key = jax.random.key(seed)
        ks = jax.random.split(key, 11)
        B, S = (4, 256)
        scale = 1.0 / np.sqrt(DIM)
        return {'q': jax.random.normal(ks[0], (B, S, DIM), jnp.float32), 'k': jax.random.normal(ks[1], (B, S, DIM), jnp.float32), 'v': jax.random.normal(ks[2], (B, S, DIM), jnp.float32), 'Wq': jax.random.normal(ks[3], (DIM, DIM), jnp.float32) * scale, 'bq': jnp.zeros((DIM,), jnp.float32), 'Wk': jax.random.normal(ks[4], (DIM, DIM), jnp.float32) * scale, 'bk': jnp.zeros((DIM,), jnp.float32), 'Wv': jax.random.normal(ks[5], (DIM, DIM), jnp.float32) * scale, 'bv': jnp.zeros((DIM,), jnp.float32), 'Wo': jax.random.normal(ks[6], (DIM, DIM), jnp.float32) * scale, 'bo': jnp.zeros((DIM,), jnp.float32)}
    _L3_xattn_all = _L3_xattn_setup()
    _L3_xattn_in = {k: v for k, v in _L3_xattn_all.items() if k in ('Wq', 'bq', 'Wk', 'bk', 'Wv', 'bv', 'Wo', 'bo')}
    del _L3_xattn_all

    def _L3_ffn_setup():
        import jax, jax.numpy as jnp
        import numpy as np
        BLOCK = 32
        W_BITS = 4
        ACT_BITS = 16

        def act_qdq(x):
            qmax = 2.0 ** (ACT_BITS - 1) - 1.0
            scale = jnp.maximum(jnp.max(jnp.abs(x)) / qmax, 1e-12)
            return jnp.clip(jnp.round(x / scale), -qmax - 1.0, qmax) * scale

        def fixed_qdq_u16(x):
            scale = 1.0 / 65536.0
            return jnp.clip(jnp.round(x / scale), 0.0, 65535.0) * scale

        def lpbq_dequant(w):
            O, I = w.shape
            qmax = 2.0 ** (W_BITS - 1) - 1.0
            wb = w.reshape(O, I // BLOCK, BLOCK)
            s = jnp.maximum(jnp.max(jnp.abs(wb), axis=-1, keepdims=True) / qmax, 1e-12)
            wq = jnp.clip(jnp.round(wb / s), -qmax - 1.0, qmax) * s
            return wq.reshape(O, I)
        key = jax.random.key(seed)
        k1, k2, k3, k4 = jax.random.split(key, 4)
        B, S, H, I = (2, 512, 128, 384)
        x = jax.random.normal(k1, (B, S, H), jnp.float32)
        w_gate = jax.random.normal(k2, (I, H), jnp.float32) * 0.02
        w_up = jax.random.normal(k3, (I, H), jnp.float32) * 0.02
        w_down = jax.random.normal(k4, (H, I), jnp.float32) * 0.02
        return {'x': x, 'w_gate': w_gate, 'w_up': w_up, 'w_down': w_down}
    _L3_ffn_all = _L3_ffn_setup()
    _L3_ffn_in = {k: v for k, v in _L3_ffn_all.items() if k in ('w_gate', 'w_up', 'w_down')}
    del _L3_ffn_all
    return {'x': x, 'ctx_1024': ctx_1024, 'mask_Bx1xSxS2_ik1': mask_Bx1xSxS2_ik1, 'L0_xattn_Wq': _L0_xattn_in['Wq'], 'L0_xattn_Wk': _L0_xattn_in['Wk'], 'L0_xattn_Wv': _L0_xattn_in['Wv'], 'L0_xattn_Wo': _L0_xattn_in['Wo'], 'L0_xattn_bo': _L0_xattn_in['bo'], 'L0_ffn_ln_g': _L0_ffn_in['ln_g'], 'L0_ffn_ln_b': _L0_ffn_in['ln_b'], 'L0_ffn_bn_g': _L0_ffn_in['bn_g'], 'L0_ffn_bn_b': _L0_ffn_in['bn_b'], 'L0_ffn_bn_mean': _L0_ffn_in['bn_mean'], 'L0_ffn_bn_var': _L0_ffn_in['bn_var'], 'L0_ffn_Wr': _L0_ffn_in['Wr'], 'L0_ffn_br': _L0_ffn_in['br'], 'L0_ffn_W_down': _L0_ffn_in['W_down'], 'L0_ffn_b_down': _L0_ffn_in['b_down'], 'L0_ffn_W_up': _L0_ffn_in['W_up'], 'L0_ffn_b_up': _L0_ffn_in['b_up'], 'L1_xattn_w_proj': _L1_xattn_in['w_proj'], 'L1_xattn_b_proj': _L1_xattn_in['b_proj'], 'L1_ffn_gate_w': _L1_ffn_in['gate_w'], 'L1_ffn_gate_b': _L1_ffn_in['gate_b'], 'L1_ffn_w1': _L1_ffn_in['w1'], 'L1_ffn_b1': _L1_ffn_in['b1'], 'L1_ffn_w3': _L1_ffn_in['w3'], 'L1_ffn_b3': _L1_ffn_in['b3'], 'L1_ffn_w2': _L1_ffn_in['w2'], 'L1_ffn_b2': _L1_ffn_in['b2'], 'L1_ffn_sw1': _L1_ffn_in['sw1'], 'L1_ffn_sb1': _L1_ffn_in['sb1'], 'L1_ffn_sw3': _L1_ffn_in['sw3'], 'L1_ffn_sb3': _L1_ffn_in['sb3'], 'L1_ffn_sw2': _L1_ffn_in['sw2'], 'L1_ffn_sb2': _L1_ffn_in['sb2'], 'L2_xattn_wq': _L2_xattn_in['wq'], 'L2_xattn_wk': _L2_xattn_in['wk'], 'L2_xattn_wv': _L2_xattn_in['wv'], 'L2_xattn_wo': _L2_xattn_in['wo'], 'L2_xattn_bo': _L2_xattn_in['bo'], 'L2_ffn_sim_matrix': _L2_ffn_in['sim_matrix'], 'L2_ffn_gates': _L2_ffn_in['gates'], 'L2_ffn_q_proj': _L2_ffn_in['q_proj'], 'L2_ffn_k_proj': _L2_ffn_in['k_proj'], 'L2_ffn_v_proj': _L2_ffn_in['v_proj'], 'L2_ffn_o_proj': _L2_ffn_in['o_proj'], 'L3_xattn_Wq': _L3_xattn_in['Wq'], 'L3_xattn_bq': _L3_xattn_in['bq'], 'L3_xattn_Wk': _L3_xattn_in['Wk'], 'L3_xattn_bk': _L3_xattn_in['bk'], 'L3_xattn_Wv': _L3_xattn_in['Wv'], 'L3_xattn_bv': _L3_xattn_in['bv'], 'L3_xattn_Wo': _L3_xattn_in['Wo'], 'L3_xattn_bo': _L3_xattn_in['bo'], 'L3_ffn_w_gate': _L3_ffn_in['w_gate'], 'L3_ffn_w_up': _L3_ffn_in['w_up'], 'L3_ffn_w_down': _L3_ffn_in['w_down']}

def reference(x, ctx_1024, mask_Bx1xSxS2_ik1, L0_xattn_Wq, L0_xattn_Wk, L0_xattn_Wv, L0_xattn_Wo, L0_xattn_bo, L0_ffn_ln_g, L0_ffn_ln_b, L0_ffn_bn_g, L0_ffn_bn_b, L0_ffn_bn_mean, L0_ffn_bn_var, L0_ffn_Wr, L0_ffn_br, L0_ffn_W_down, L0_ffn_b_down, L0_ffn_W_up, L0_ffn_b_up, L1_xattn_w_proj, L1_xattn_b_proj, L1_ffn_gate_w, L1_ffn_gate_b, L1_ffn_w1, L1_ffn_b1, L1_ffn_w3, L1_ffn_b3, L1_ffn_w2, L1_ffn_b2, L1_ffn_sw1, L1_ffn_sb1, L1_ffn_sw3, L1_ffn_sb3, L1_ffn_sw2, L1_ffn_sb2, L2_xattn_wq, L2_xattn_wk, L2_xattn_wv, L2_xattn_wo, L2_xattn_bo, L2_ffn_sim_matrix, L2_ffn_gates, L2_ffn_q_proj, L2_ffn_k_proj, L2_ffn_v_proj, L2_ffn_o_proj, L3_xattn_Wq, L3_xattn_bq, L3_xattn_Wk, L3_xattn_bk, L3_xattn_Wv, L3_xattn_bv, L3_xattn_Wo, L3_xattn_bo, L3_ffn_w_gate, L3_ffn_w_up, L3_ffn_w_down):
    import jax
    import jax.numpy as jnp

    def _L0_xattn_ref(x, context, Wq, Wk, Wv, Wo, bo):
        import jax, jax.numpy as jnp
        import numpy as np
        B, N, D_MODEL, H, DH = (2, 256, 128, 16, 64)
        SCALE = DH ** (-0.5)
        b, n, _ = x.shape
        m = context.shape[1]
        q = (x @ Wq).reshape(b, n, H, DH)
        k = (context @ Wk * SCALE).reshape(b, m, H, DH)
        v = (context @ Wv).reshape(b, m, H, DH)
        scores = jnp.einsum('bihd,bjhd->bhij', q, k)
        attn = jax.nn.softmax(scores, axis=-1)
        out = jnp.einsum('bhij,bjhd->bihd', attn, v)
        out = out.reshape(b, n, H * DH)
        return out @ Wo + bo

    def _L0_ffn_ref(x, ln_g, ln_b, bn_g, bn_b, bn_mean, bn_var, Wr, br, W_down, b_down, W_up, b_up):
        import jax, jax.numpy as jnp
        import numpy as np
        B, S, D, H, E = (64, 128, 128, 64, 8)
        EPS = 1e-05
        mu = jnp.mean(x, axis=-1, keepdims=True)
        var = jnp.var(x, axis=-1, keepdims=True)
        z = (x - mu) * jax.lax.rsqrt(var + EPS) * ln_g + ln_b
        z_sent = jnp.mean(z, axis=1)
        z_bn = (z_sent - bn_mean) * jax.lax.rsqrt(bn_var + EPS) * bn_g + bn_b
        probs = jax.nn.softmax(z_bn @ Wr + br, axis=-1)
        idx = jnp.argmax(probs, axis=-1)
        gate = jnp.take_along_axis(probs, idx[:, None], axis=1)[:, 0]
        h = jax.nn.relu(jnp.einsum('bsd,bdh->bsh', z, W_down[idx]) + b_down[idx][:, None, :])
        y = jnp.einsum('bsh,bhd->bsd', h, W_up[idx]) + b_up[idx][:, None, :]
        return y * gate[:, None, None]

    def _L1_xattn_ref(x, cond_k, cond_v, w_proj, b_proj):
        import jax, jax.numpy as jnp
        import numpy as np
        HEADS = 16
        B, T, W = x.shape
        S = cond_k.shape[1]
        H = HEADS
        d = W // H
        scale = 1.0 / jnp.sqrt(jnp.sqrt(jnp.float32(d)))
        q = x.reshape(B, T, H, d) * scale
        k = cond_k.reshape(B, S, H, d) * scale
        v = cond_v.reshape(B, S, H, d)
        scores = jnp.einsum('bthd,bshd->bhts', q, k)
        w = jax.nn.softmax(scores.astype(jnp.float32), axis=-1).astype(scores.dtype)
        out = jnp.einsum('bhts,bshd->bthd', w, v).reshape(B, T, W)
        return out @ w_proj.T + b_proj

    def _L1_ffn_ref(x, gate_w, gate_b, w1, b1, w3, b3, w2, b2, sw1, sb1, sw3, sb3, sw2, sb2):
        import jax, jax.numpy as jnp
        import numpy as np
        from jax import lax
        D = 128
        H = 176
        E = 8
        K = 2
        ROUTER_SCALE = 1.0

        def _expert(x, w1, b1, w3, b3, w2, b2):
            h = jax.nn.silu((x @ w1 + b1) * (x @ w3 + b3))
            return h @ w2 + b2
        shape = x.shape
        xf = x.reshape(-1, D)
        T = xf.shape[0]
        scores = jax.nn.softmax(xf @ gate_w.T, axis=-1)
        biased = scores + gate_b
        _, idx = lax.top_k(biased, K)
        w = jnp.take_along_axis(scores, idx, axis=-1) * ROUTER_SCALE
        rw = jnp.zeros((T, E), dtype=xf.dtype).at[jnp.arange(T)[:, None], idx].add(w)
        h = jax.nn.silu((jnp.einsum('td,edh->teh', xf, w1) + b1) * (jnp.einsum('td,edh->teh', xf, w3) + b3))
        oe = jnp.einsum('teh,ehd->ted', h, w2) + b2
        y = jnp.einsum('te,ted->td', rw, oe)
        z = _expert(xf, sw1, sb1, sw3, sb3, sw2, sb2)
        return (y + z).reshape(shape)

    def _L2_xattn_ref(q, k, v, mask, wq, wk, wv, wo, bo):
        import jax, jax.numpy as jnp
        import numpy as np
        import math
        HEAD = 16
        D_MODEL = 128
        HEAD_DIM = D_MODEL // HEAD
        B, S = (2, 256)
        N, Lq, _ = q.shape
        Lk = k.shape[1]
        qh = (q @ wq).reshape(N, Lq, HEAD, HEAD_DIM)
        kh = (k @ wk).reshape(N, Lk, HEAD, HEAD_DIM)
        vh = (v @ wv).reshape(N, Lk, HEAD, HEAD_DIM)
        scores = jnp.einsum('nqha,nkha->nhqk', qh, kh)
        scores = jnp.where(mask == 0, jnp.float32(-10000000000.0), scores)
        attn = jax.nn.softmax(scores / math.sqrt(HEAD_DIM), axis=-1)
        out = jnp.einsum('nhqk,nkha->nqha', attn, vh).reshape(N, Lq, D_MODEL)
        return out @ wo + bo

    def _L2_ffn_ref(hidden_states, sim_matrix, gates, q_proj, k_proj, v_proj, o_proj):
        import jax, jax.numpy as jnp
        import numpy as np
        import math
        HID, HD, E, MIN_E = (128, 128, 16, 2)
        B, T = (4, 256)
        IS_CAUSAL = True

        def _l2norm(x, axis):
            return x / jnp.sqrt(jnp.sum(x * x, axis=axis, keepdims=True) + 1e-12)

        def _gating(hidden_states, sim_matrix, gates):
            b, t, c = hidden_states.shape
            flat = hidden_states.reshape(b * t, c)
            logits = _l2norm(flat, -1) @ _l2norm(sim_matrix, 0) - jax.nn.sigmoid(gates)
            gated = jax.nn.relu(logits)
            mask = (gated > 0).astype(gated.dtype)
            inactive = jnp.sum(mask, axis=1) == 0
            _, top_idx = jax.lax.top_k(logits, MIN_E)
            fb = jnp.sum(jax.nn.one_hot(top_idx, E, dtype=mask.dtype), axis=1)
            mask = mask + inactive[:, None].astype(mask.dtype) * fb
            masked = jnp.where(mask > 0, gated, -jnp.inf)
            probs = jax.nn.softmax(masked, axis=-1)
            return probs
        b, t, c = hidden_states.shape
        rw = _gating(hidden_states, sim_matrix, gates).reshape(b, t, E)
        q = jnp.einsum('btc,ech,bte->bth', hidden_states, q_proj, rw)
        k = jnp.einsum('btc,ech,bte->bth', hidden_states, k_proj, rw)
        v = jnp.einsum('btc,ech,bte->bth', hidden_states, v_proj, rw)
        scale = 1.0 / math.sqrt(HD)
        scores = jnp.einsum('bqh,bkh->bqk', q, k) * scale
        if IS_CAUSAL:
            causal = jnp.tril(jnp.ones((t, t), dtype=bool))
            scores = jnp.where(causal[None], scores, -jnp.inf)
        attn = jax.nn.softmax(scores, axis=-1)
        ao = jnp.einsum('bqk,bkh->bqh', attn, v)
        out = jnp.einsum('bth,ehc,bte->btc', ao, o_proj, rw)
        return out

    def _L3_xattn_ref(q, k, v, Wq, bq, Wk, bk, Wv, bv, Wo, bo):
        import jax, jax.numpy as jnp
        import numpy as np
        H = 16
        DIM = 128
        DK = DIM // H
        B, S, _ = q.shape

        def proj(x, W, b):
            y = x @ W.T + b
            return y.reshape(B, -1, H, DK).transpose(0, 2, 1, 3)
        qh = proj(q, Wq, bq)
        kh = proj(k, Wk, bk)
        vh = proj(v, Wv, bv)
        scores = jnp.einsum('bhqd,bhkd->bhqk', qh, kh) / np.sqrt(DK)
        a = jax.nn.softmax(scores, axis=-1)
        attn = jnp.einsum('bhqk,bhkd->bhqd', a, vh)
        concat = attn.transpose(0, 2, 1, 3).reshape(B, S, DIM)
        return concat @ Wo.T + bo

    def _L3_ffn_ref(x, w_gate, w_up, w_down):
        import jax, jax.numpy as jnp
        import numpy as np
        BLOCK = 32
        W_BITS = 4
        ACT_BITS = 16

        def act_qdq(x):
            qmax = 2.0 ** (ACT_BITS - 1) - 1.0
            scale = jnp.maximum(jnp.max(jnp.abs(x)) / qmax, 1e-12)
            return jnp.clip(jnp.round(x / scale), -qmax - 1.0, qmax) * scale

        def fixed_qdq_u16(x):
            scale = 1.0 / 65536.0
            return jnp.clip(jnp.round(x / scale), 0.0, 65535.0) * scale

        def lpbq_dequant(w):
            O, I = w.shape
            qmax = 2.0 ** (W_BITS - 1) - 1.0
            wb = w.reshape(O, I // BLOCK, BLOCK)
            s = jnp.maximum(jnp.max(jnp.abs(wb), axis=-1, keepdims=True) / qmax, 1e-12)
            wq = jnp.clip(jnp.round(wb / s), -qmax - 1.0, qmax) * s
            return wq.reshape(O, I)
        x = act_qdq(x)
        up = act_qdq(x @ lpbq_dequant(w_up).T)
        gate = act_qdq(x @ lpbq_dequant(w_gate).T)
        sig = fixed_qdq_u16(jax.nn.sigmoid(gate))
        gate = act_qdq(gate * sig)
        o = act_qdq(gate * up)
        return o @ lpbq_dequant(w_down).T
    x = x + _L0_xattn_ref(_layernorm(x, axis=-1), ctx_1024, L0_xattn_Wq, L0_xattn_Wk, L0_xattn_Wv, L0_xattn_Wo, L0_xattn_bo)
    x = x + _L0_ffn_ref(_layernorm(x, axis=-1), L0_ffn_ln_g, L0_ffn_ln_b, L0_ffn_bn_g, L0_ffn_bn_b, L0_ffn_bn_mean, L0_ffn_bn_var, L0_ffn_Wr, L0_ffn_br, L0_ffn_W_down, L0_ffn_b_down, L0_ffn_W_up, L0_ffn_b_up)
    x = x + _L1_xattn_ref(_layernorm(x, axis=-1), ctx_1024, ctx_1024, L1_xattn_w_proj, L1_xattn_b_proj)
    x = x + _L1_ffn_ref(_layernorm(x, axis=-1), L1_ffn_gate_w, L1_ffn_gate_b, L1_ffn_w1, L1_ffn_b1, L1_ffn_w3, L1_ffn_b3, L1_ffn_w2, L1_ffn_b2, L1_ffn_sw1, L1_ffn_sb1, L1_ffn_sw3, L1_ffn_sb3, L1_ffn_sw2, L1_ffn_sb2)
    x = x + _L2_xattn_ref(_layernorm(x, axis=-1), ctx_1024, ctx_1024, mask_Bx1xSxS2_ik1, L2_xattn_wq, L2_xattn_wk, L2_xattn_wv, L2_xattn_wo, L2_xattn_bo)
    x = x + _L2_ffn_ref(_layernorm(x, axis=-1), L2_ffn_sim_matrix, L2_ffn_gates, L2_ffn_q_proj, L2_ffn_k_proj, L2_ffn_v_proj, L2_ffn_o_proj)
    x = x + _L3_xattn_ref(_layernorm(x, axis=-1), ctx_1024, ctx_1024, L3_xattn_Wq, L3_xattn_bq, L3_xattn_Wk, L3_xattn_bk, L3_xattn_Wv, L3_xattn_bv, L3_xattn_Wo, L3_xattn_bo)
    x = x + _L3_ffn_ref(_layernorm(x, axis=-1), L3_ffn_w_gate, L3_ffn_w_up, L3_ffn_w_down)
    return x

_drawn_inputs = setup_inputs


def setup_inputs(seed=0):
    import zlib

    import numpy as np

    out = dict(_drawn_inputs(seed))
    spreads = {'L0_xattn_bo': (0.0, 0.1),
     'L0_ffn_ln_g': (1.0, 0.6),
     'L0_ffn_ln_b': (0.0, 0.471),
     'L0_ffn_bn_g': (1.0, 0.6),
     'L0_ffn_bn_b': (0.0, 0.511),
     'L0_ffn_bn_var': (1.0, 0.6),
     'L0_ffn_br': (0.0, 0.299),
     'L0_ffn_b_down': (0.0, 0.8),
     'L0_ffn_b_up': (0.0, 0.316),
     'L1_xattn_b_proj': (0.0, 0.1),
     'L2_ffn_gates': (0.0, 0.1),
     'L3_xattn_bq': (0.0, 0.458),
     'L3_xattn_bk': (0.0, 2.0),
     'L3_xattn_bv': (0.0, 0.1),
     'L3_xattn_bo': (0.0, 0.1)}
    factors = {'L0_ffn_bn_mean': 8.0,
     'L0_ffn_Wr': 3.028,
     'L0_ffn_W_down': 6.195,
     'L0_ffn_W_up': 5.815,
     'L1_ffn_gate_w': 6.814,
     'L1_ffn_gate_b': 8.0,
     'L1_ffn_w1': 8.0,
     'L1_ffn_b1': 8.0,
     'L1_ffn_w3': 8.0,
     'L1_ffn_b3': 8.0,
     'L1_ffn_w2': 8.0,
     'L1_ffn_b2': 5.171,
     'L1_ffn_sw1': 4.891,
     'L1_ffn_sb1': 8.0,
     'L1_ffn_sw3': 4.444,
     'L1_ffn_sb3': 8.0,
     'L1_ffn_sw2': 4.477,
     'L2_xattn_bo': 10.952,
     'L3_ffn_w_gate': 7.724,
     'L3_ffn_w_up': 7.631,
     'L3_ffn_w_down': 7.666,
     'L1_ffn_sb2': 5.051,
     'L2_ffn_q_proj': 3.523,
     'L2_ffn_k_proj': 3.555}
    for name, (base, spread) in spreads.items():
        noise = np.random.default_rng([zlib.crc32(name.encode()), seed]).standard_normal(out[name].shape)
        drawn = base * np.exp(spread * noise) if base else spread * noise
        out[name] = jnp.asarray(drawn.astype(out[name].dtype))
    for name, factor in factors.items():
        out[name] = (out[name] * factor).astype(out[name].dtype)
    return out
```

```python
from contextlib import ExitStack

import concourse.bass as bass
from concourse import mybir

F32 = mybir.dt.float32
BF16 = mybir.dt.bfloat16
I32 = mybir.dt.int32
ALU = mybir.AluOpType
ACT = mybir.ActivationFunctionType
AX = mybir.AxisListType

N_SUBLAYERS = 8

P = 128
B, S, SC = 16, 256, 64
TILES = B * S // P
TPI = 4
BPI = 2
ITERS = TILES // TPI
H = 16
PAIRS = H // 2
KEYS = H * SC
EPS = 1e-5
L1_E, L1_H = 8, 176
L1_ALL = (L1_E + 1) * L1_H
L1_CH = -(-L1_ALL // P)
L2_E = 16
L3_I = 384
BLK = 32
NEG = -float(2 ** 100)
MAGIC = 1.5 * 2.0 ** 23


class Signal:
    PRIME = 4

    def __init__(self, sem):
        self.sem, self.base = sem, Signal.PRIME

    def at(self, n):
        return n + self.base


class Steps:

    def __init__(self, eng, sig, i, per_iteration):
        self.eng, self.sig, self.i, self.n, self.k = eng, sig, i, per_iteration, 0

    def done(self, instruction):
        self.k += 1
        instruction.then_inc(self.sig.sem, 1)
        self.eng.wait_ge(self.sig.sem, self.sig.at(self.i * self.n + self.k))

    def end(self):
        assert self.k == self.n, (self.k, self.n)


class Program:

    def __init__(self, nc, ctx):
        self.nc, self.ctx, self.named = nc, ctx, {}

    def sig(self, name):
        if name not in self.named:
            self.named[name] = Signal(self.ctx.enter_context(self.nc.semaphore(name)))
        return self.named[name]

    def end_block(self, counts):
        for name, n in counts.items():
            self.named[name].base += n


SIGNALS = [
    "ln_var", "ln_rstd", "ln_out", "ln_T", "xT_ready", "bias_added", "x_added",
    "ctx_ready", "kv_proj", "kv_ready", "khat_ready", "q_proj", "q_ready", "mask_ready",
    "scores", "shifted", "shifted_T", "probs", "heads_out", "heads_norm", "heads_T", "headsT_ready", "attn_proj",
    "dve_steps", "pool_steps", "act_steps", "weights", "out_stored",
    "z_ready", "gate_logits", "gate_exp", "gate_ready", "gate_T", "gate_parts",
    "hidden", "hidden_b", "hidden_ready", "ffn_out", "ffn_outT", "ffn_outT_ready", "gate_bcast", "hidden_mul", "hidden_act",
    "scaled", "qkv", "qkv_ready", "vT", "v_ready", "maxed", "pT", "pT_ready", "ao", "ao_ready",
    "absmax", "gmax", "quant", "wraw",
]


def load_weights(eng, pr, pairs, count):
    for dst, src in pairs:
        eng.dma_start(dst, src).then_inc(pr.sig("weights").sem, 16)
        count += 16
    return count


def ln_buffers(sb):
    return dict(stats=sb("stats", [P, TPI, 6]), mv=sb("mv", [P, 4, TPI]), mean=sb("mean", [P, TPI]),
                vareps=sb("vareps", [P, TPI]), rstd=sb("rstd", [P, TPI]))


LN_STEPS = 3


def layernorm_vector(pr, dve, steps, i, w, x4, xn):
    nc = pr.nc
    for c in range(TPI):
        ins = nc.vector.bn_stats(w["stats"][:, c, :], x4[:, c, :])
    steps.done(ins)
    st, mv = w["stats"], w["mv"]
    nc.vector.tensor_tensor(mv[:, 0, :], st[:, :, 1], st[:, :, 4], ALU.add)
    nc.vector.scalar_tensor_tensor(mv[:, 2, :], st[:, :, 2], P * EPS, st[:, :, 5], ALU.add, ALU.add)
    steps.done(nc.vector.tensor_tensor(mv[:, 1, :], st[:, :, 1], st[:, :, 4], ALU.subtract))
    nc.vector.tensor_scalar(w["mean"][:], mv[:, 0, :], 0.5, None, ALU.mult)
    steps.done(nc.vector.scalar_tensor_tensor(mv[:, 3, :], mv[:, 1, :], 0.25, mv[:, 1, :], ALU.mult, ALU.mult))
    nc.vector.scalar_tensor_tensor(w["vareps"][:], mv[:, 2, :], 1.0 / P, mv[:, 3, :], ALU.mult, ALU.add)\
        .then_inc(pr.sig("ln_var").sem, 1)


def layernorm_apply(pr, dve, w, x4, xn):
    for c in range(TPI):
        ins = pr.nc.vector.tensor_scalar(xn[:, c, :], x4[:, c, :], w["mean"][:, c:c + 1], w["rstd"][:, c:c + 1],
                                         ALU.subtract, ALU.mult)
    return ins


def layernorm_pool(pr, pool, n, w):
    pool.wait_ge(pr.sig("ln_var").sem, pr.sig("ln_var").at(n))
    pr.nc.gpsimd.tensor_tensor(w["rstd"][:], w["vareps"][:], w["mhalf"][:, 0:TPI], ALU.pow).then_inc(pr.sig("ln_rstd").sem, 1)


def tile4(x_sb, i):
    return x_sb[:, bass.ds(i * TPI, TPI), :]


def context_attention(pr, x_sb, common, dram, layer):
    nc = pr.nc
    first = layer == 0
    masked = layer == 2
    dv = SC if first else P // H
    vw = 2 * (dv + 1)
    with ExitStack() as ctx:
        def sb(name, shape, dt=F32):
            return ctx.enter_context(nc.sbuf_tensor(f"{name}_a{layer}", shape, dt))
        w = dict(common)
        ident, ctxT = common["ident"], common["ctxT"]
        if first:
            wqT = sb("wqT", [P, PAIRS, P])
            wkT = sb("wkT", [P, PAIRS, P])
            wv = sb("wv", [P, H * dv])
            wo = sb("wo", [P, PAIRS, P])
            m = sb("m", [P, H, P])
            loads = [(wqT[:], dram["L0_wqT"]), (wkT[:], dram["L0_wkT"]), (wv[:], dram["L0_wv"]), (wo[:], dram["L0_wo"])]
        else:
            ws = sb("ws", [P, 4, P])
            cols = sb("cols", [P, 3])
            loads = [(ws[:], dram[f"L{layer}_w4"]), (cols[:], dram[f"L{layer}_cols"])]
            wq, wk, wv, wo = (ws[:, k, :] for k in range(4))
        bo = sb("bo", [P, P])
        loads.append((bo[:], dram[f"L{layer}_bo"].partition_broadcast(P)))
        if masked:
            maskf = sb("maskf", [P, TPI, SC], I32)
            maskb = sb("maskb", [P, TPI, SC], BF16)
        cb = sb("cb", [P, BPI, P])
        khat = sb("khat", [P, BPI, H, SC])
        kT = sb("kT", [P, BPI, SC])
        vb = sb("vb", [P, BPI, PAIRS, vw])
        xn = sb("xn", [P, TPI, P])
        xT = sb("xT", [P, TPI, P])
        qT = sb("qT", [P, TPI, P])
        shifted = sb("shifted", [P, TPI, KEYS])
        probs = sb("probs", [P, TPI, KEYS])
        smax = sb("smax", [P, TPI, H])
        rsum = sb("rsum", [P, TPI, H])
        w.update(ln_buffers(sb))
        PS = [ctx.enter_context(nc.psum_tensor(f"ps{c}_a{layer}", [P, 1024], F32)) for c in range(TPI)]
        heads = shifted if first else sb("heads", [P, TPI, P])
        headsT = probs if first else sb("headsT", [P, TPI, P])
        PH = 2 if first else 1
        nload = 16 * len(loads)
        block = ctx.enter_context(nc.Block())
        s = pr.sig

        @block.sync
        def _(sp):
            load_weights(sp, pr, loads, 0)
            if masked:
                with sp.Fori(0, ITERS) as i:
                    sp.wait_ge(s("mask_ready").sem, s("mask_ready").at(i))
                    sp.dma_start(maskf[:], dram["mask"][:, bass.ds(i * TPI, TPI), :]).then_inc(s("wraw").sem, 16)

        @block.gpsimd
        def _(pool):
            nc.gpsimd.memset(vb[:], 0.0).then_inc(s("pool_steps").sem, 1)
            pool.wait_ge(s("pool_steps").sem, s("pool_steps").at(1))
            for par in range(2):
                ins = nc.gpsimd.memset(vb[par * SC:(par + 1) * SC, :, :, par * (dv + 1) + dv:par * (dv + 1) + dv + 1], 1.0)
                ins.then_inc(s("pool_steps").sem, 1)
                pool.wait_ge(s("pool_steps").sem, s("pool_steps").at(2 + par))
            pool.wait_ge(s("weights").sem, s("weights").at(nload))
            with pool.Fori(0, ITERS) as i:
                pool.wait_ge(s("kv_proj").sem, s("kv_proj").at(i))
                ins = nc.gpsimd.tensor_copy(cb[:].rearrange("p b k -> p (b k)"), ctxT[:, bass.ds(i * (BPI * P), BPI * P)])
                ins.then_inc(s("ctx_ready").sem, 1)
                layernorm_pool(pr, pool, i + 1, w)
                if not first:
                    pool.wait_ge(s("kv_ready").sem, s("kv_ready").at(i + 1))
                    pool.wait_ge(s("scores").sem, s("scores").at(i * TPI))
                    for b in range(BPI):
                        ins = nc.gpsimd.tensor_tensor(khat[:, b, :, :], kT[:, b, :].unsqueeze(1).broadcast_to([P, H, SC]),
                                                      common["headmask"][:].unsqueeze(2).broadcast_to([P, H, SC]), ALU.mult)
                    ins.then_inc(s("khat_ready").sem, 1)
                pool.wait_ge(s("ln_out").sem, s("ln_out").at(i + 1))
                x4 = tile4(x_sb, i)
                nc.gpsimd.tensor_tensor(x4, x4, bo[:].unsqueeze(1).broadcast_to([P, TPI, P]), ALU.add)\
                    .then_inc(s("bias_added").sem, 1)

        @block.scalar
        def _(act):
            act.wait_ge(s("weights").sem, s("weights").at(nload))
            act.wait_ge(s("pool_steps").sem, s("pool_steps").at(3))
            if first:
                for j in range(2):
                    act.wait_ge(s("q_proj").sem, s("q_proj").at(j + 1))
                    nc.scalar.activation(m[:, j::2, :], PS[j][:].rearrange("p (h d) -> p h d", h=8), ACT.Copy)\
                        .then_inc(s("q_ready").sem, 1)
            with act.Fori(0, ITERS) as i:
                act.wait_ge(s("kv_proj").sem, s("kv_proj").at(i + 1))
                act.wait_ge(s("heads_out").sem, s("heads_out").at(i * TPI * PH))
                if not first:
                    act.wait_ge(s("khat_ready").sem, s("khat_ready").at(i))
                else:
                    act.wait_ge(s("scores").sem, s("scores").at(i * TPI))
                for b in range(BPI):
                    if first:
                        nc.scalar.activation(khat[:, b, :, :], PS[2 * b][:].rearrange("p (h k) -> p h k", h=H), ACT.Copy)
                        v = PS[2 * b + 1][:].rearrange("p (q a d) -> p q a d", a=2, d=dv)
                    else:
                        nc.scalar.activation(kT[:, b, :], PS[2 * b][:, 0:SC], ACT.Identity, bias=cols[:, 1:2])
                        v = PS[2 * b][:, 512:512 + P].rearrange("p (q a d) -> p q a d", a=2, d=dv)
                    for par in range(2):
                        r = slice(par * SC, (par + 1) * SC)
                        ins = nc.scalar.activation(vb[r, b, :, par * (dv + 1):par * (dv + 1) + dv], v[r, :, par, :], ACT.Copy)
                ins.then_inc(s("kv_ready").sem, 1)
                for c in range(TPI):
                    act.wait_ge(s("ln_T").sem, s("ln_T").at(i * TPI + c + 1))
                    nc.scalar.activation(xT[:, c, :], PS[c][:, 0:P], ACT.Copy).then_inc(s("xT_ready").sem, 1)
                if not first:
                    for c in range(TPI):
                        act.wait_ge(s("q_proj").sem, s("q_proj").at(i * TPI + c + 1))
                        nc.scalar.activation(qT[:, c, :], PS[c][:, 512:512 + P], ACT.Identity, bias=cols[:, 0:1])\
                            .then_inc(s("q_ready").sem, 1)
                for c in range(TPI):
                    act.wait_ge(s("shifted_T").sem, s("shifted_T").at(i * TPI + c + 1))
                    nc.scalar.activation(probs[:, c, :], PS[c][:], ACT.Exp, scale=float(dv) ** -0.5).then_inc(s("probs").sem, 1)
                for c in range(TPI):
                    act.wait_ge(s("heads_T").sem, s("heads_T").at(i * TPI + c + 1))
                    if first:
                        nc.scalar.activation(headsT[:, c, :], PS[c][:], ACT.Copy).then_inc(s("headsT_ready").sem, 1)
                    else:
                        nc.scalar.activation(headsT[:, c, :], PS[c][:, 512:512 + P], ACT.Identity, bias=cols[:, 2:3])\
                            .then_inc(s("headsT_ready").sem, 1)

        @block.tensor
        def _(pe):
            pe.wait_ge(s("weights").sem, s("weights").at(nload))
            if first:
                for h in range(H):
                    r = slice((h % 2) * SC, (h % 2 + 1) * SC)
                    ins = nc.tensor.matmul(PS[h % 2][:, (h // 2) * P:(h // 2 + 1) * P], wkT[r, h // 2, :], wqT[r, h // 2, :],
                                           start=True, stop=True)
                    if h >= H - 2:
                        ins.then_inc(s("q_proj").sem, 1)
                pe.wait_ge(s("q_ready").sem, s("q_ready").at(2))
            with pe.Fori(0, ITERS) as i:
                pe.wait_ge(s("ctx_ready").sem, s("ctx_ready").at(i + 1))
                pe.wait_ge(s("x_added").sem, s("x_added").at(i * TPI))
                for b in range(BPI):
                    if first:
                        for h in range(H):
                            nc.tensor.matmul(PS[2 * b][:, h * SC:(h + 1) * SC], m[:, h, :], cb[:, b, 0:SC], start=True, stop=True)
                        for j in range(2):
                            ins = nc.tensor.matmul(PS[2 * b + 1][:, j * 512:(j + 1) * 512], cb[:, b, :],
                                                   wv[:, j * 512:(j + 1) * 512], start=True, stop=True)
                    else:
                        nc.tensor.matmul(PS[2 * b][:, 0:SC], wk, cb[:, b, 0:SC], start=True, stop=True)
                        ins = nc.tensor.matmul(PS[2 * b][:, 512:512 + P], cb[:, b, :], wv, start=True, stop=True)
                ins.then_inc(s("kv_proj").sem, 1)
                pe.wait_ge(s("kv_ready").sem, s("kv_ready").at(i + 1))
                pe.wait_ge(s("ln_out").sem, s("ln_out").at(i + 1))
                for c in range(TPI):
                    nc.tensor.transpose(PS[c][:, 0:P], xn[:, c, :], ident[:]).then_inc(s("ln_T").sem, 1)
                if not first:
                    for c in range(TPI):
                        pe.wait_ge(s("xT_ready").sem, s("xT_ready").at(i * TPI + c + 1))
                        nc.tensor.matmul(PS[c][:, 512:512 + P], wq, xT[:, c, :], start=True, stop=True).then_inc(s("q_proj").sem, 1)
                    pe.wait_ge(s("khat_ready").sem, s("khat_ready").at(i + 1))
                if masked:
                    pe.wait_ge(s("mask_ready").sem, s("mask_ready").at(i + 1))
                for c in range(TPI):
                    src = xT if first else qT
                    if first:
                        pe.wait_ge(s("xT_ready").sem, s("xT_ready").at(i * TPI + c + 1))
                    else:
                        pe.wait_ge(s("q_ready").sem, s("q_ready").at(i * TPI + c + 1))
                    for j in range(2):
                        out = PS[c][:, j * 512:(j + 1) * 512]
                        if masked:
                            nc.tensor.matmul(out, common["identb"][:], maskb[:, c, :].unsqueeze(1).broadcast_to([P, 8, SC]),
                                             start=True, stop=False)
                        ins = nc.tensor.matmul(out, src[:, c, :], khat[:, c // 2, 8 * j:8 * j + 8, :], start=not masked, stop=True)
                    ins.then_inc(s("scores").sem, 1)
                for c in range(TPI):
                    pe.wait_ge(s("shifted").sem, s("shifted").at(i * TPI + c + 1))
                    for q in range(PAIRS):
                        ins = nc.tensor.transpose(PS[c][:, q * P:(q + 1) * P], shifted[:, c, q * P:(q + 1) * P], ident[:])
                    ins.then_inc(s("shifted_T").sem, 1)
                for ph in range(PH):
                    for c in range(TPI):
                        if ph == 0:
                            pe.wait_ge(s("probs").sem, s("probs").at(i * TPI + c + 1))
                        else:
                            pe.wait_ge(s("heads_norm").sem, s("heads_norm").at((i * PH + ph - 1) * TPI + c + 1))
                        for k in range(PAIRS // PH):
                            q = ph * (PAIRS // PH) + k
                            o = (k // 2) * 512 + (k % 2) * vw if first else k * vw
                            ins = nc.tensor.matmul(PS[c][:, o:o + vw], probs[:, c, q * P:(q + 1) * P], vb[:, c // 2, q, :],
                                                   start=True, stop=True)
                        ins.then_inc(s("heads_out").sem, 1)
                for c in range(TPI):
                    pe.wait_ge(s("heads_norm").sem, s("heads_norm").at((i * PH + PH - 1) * TPI + c + 1))
                    if first:
                        for q in range(PAIRS):
                            ins = nc.tensor.transpose(PS[c][:, q * P:(q + 1) * P], heads[:, c, q * P:(q + 1) * P], ident[:])
                    else:
                        ins = nc.tensor.transpose(PS[c][:, 512:512 + P], heads[:, c, :], ident[:])
                    ins.then_inc(s("heads_T").sem, 1)
                for c in range(TPI):
                    pe.wait_ge(s("headsT_ready").sem, s("headsT_ready").at(i * TPI + c + 1))
                    if first:
                        for q in range(PAIRS):
                            ins = nc.tensor.matmul(PS[c][:, 0:P], headsT[:, c, q * P:(q + 1) * P], wo[:, q, :],
                                                   start=q == 0, stop=q == PAIRS - 1)
                    else:
                        ins = nc.tensor.matmul(PS[c][:, 0:P], headsT[:, c, :], wo, start=True, stop=True)
                    ins.then_inc(s("attn_proj").sem, 1)

        @block.vector
        def _(dve):
            with dve.Fori(0, ITERS) as i:
                steps = Steps(dve, s("dve_steps"), i, LN_STEPS + TPI + TPI * PH)
                x4 = tile4(x_sb, i)
                layernorm_vector(pr, dve, steps, i, w, x4, xn)
                if masked:
                    dve.wait_ge(s("wraw").sem, s("wraw").at((i + 1) * 16))
                    dve.wait_ge(s("scores").sem, s("scores").at(i * TPI))
                    nc.vector.tensor_scalar(maskb[:], maskf[:], 0.0, NEG, ALU.is_equal, ALU.mult).then_inc(s("mask_ready").sem, 1)
                dve.wait_ge(s("ln_rstd").sem, s("ln_rstd").at(i + 1))
                layernorm_apply(pr, dve, w, x4, xn).then_inc(s("ln_out").sem, 1)
                for c in range(TPI):
                    dve.wait_ge(s("scores").sem, s("scores").at(i * TPI + c + 1))
                    sc = PS[c][:].rearrange("p (h k) -> p h k", h=H)
                    steps.done(nc.vector.tensor_reduce(smax[:, c, :], sc, axis=AX.X, op=ALU.max))
                    nc.vector.tensor_tensor(shifted[:, c, :].rearrange("p (h k) -> p h k", h=H), sc,
                                            smax[:, c, :].unsqueeze(2).broadcast_to([P, H, SC]), ALU.subtract)\
                        .then_inc(s("shifted").sem, 1)
                for ph in range(PH):
                    for c in range(TPI):
                        dve.wait_ge(s("heads_out").sem, s("heads_out").at((i * PH + ph) * TPI + c + 1))
                        if first:
                            o = PS[c][:].rearrange("p (g n) -> p g n", g=2)[:, :, 0:2 * vw].rearrange("p g (k d) -> p g k d", d=dv + 1)
                            hs = heads[:, c, ph * 512:(ph + 1) * 512].rearrange("p (g k d) -> p g k d", g=2, d=dv)
                            rs = rsum[:, c, ph * 8:ph * 8 + 8].rearrange("p (g k) -> p g k", g=2)
                            steps.done(nc.vector.reciprocal(rs, o[:, :, :, dv]))
                            ins = nc.vector.tensor_tensor(hs, o[:, :, :, 0:dv], rs.unsqueeze(3).broadcast_to([P, 2, 4, dv]), ALU.mult)
                        else:
                            o = PS[c][:, 0:H * (dv + 1)].rearrange("p (h d) -> p h d", h=H)
                            steps.done(nc.vector.reciprocal(rsum[:, c, :], o[:, :, dv]))
                            ins = nc.vector.tensor_tensor(heads[:, c, :].rearrange("p (h d) -> p h d", h=H), o[:, :, 0:dv],
                                                          rsum[:, c, :].unsqueeze(2).broadcast_to([P, H, dv]), ALU.mult)
                        ins.then_inc(s("heads_norm").sem, 1)
                dve.wait_ge(s("bias_added").sem, s("bias_added").at(i + 1))
                for c in range(TPI):
                    dve.wait_ge(s("attn_proj").sem, s("attn_proj").at(i * TPI + c + 1))
                    xc = x_sb[:, bass.ds(i * TPI + c, 1), :].rearrange("p a d -> p (a d)")
                    nc.vector.tensor_tensor(xc, xc, PS[c][:, 0:P], ALU.add).then_inc(s("x_added").sem, 1)
                steps.end()

    n4, n1 = ITERS * TPI, ITERS
    counts = dict(weights=nload, kv_proj=n1, ctx_ready=n1, ln_var=n1, ln_rstd=n1, kv_ready=n1, ln_out=n1, bias_added=n1,
                  ln_T=n4, xT_ready=n4, scores=n4, shifted=n4, shifted_T=n4, probs=n4, heads_out=n4 * PH, heads_norm=n4 * PH,
                  heads_T=n4, headsT_ready=n4, attn_proj=n4, x_added=n4, pool_steps=3, dve_steps=n1 * (LN_STEPS + TPI + TPI * PH))
    if first:
        counts.update(q_proj=2, q_ready=2)
    else:
        counts.update(khat_ready=n1, q_proj=n4, q_ready=n4)
    if masked:
        counts.update(mask_ready=n1, wraw=16 * n1)
    pr.end_block(counts)


def first_max(nc, steps, src, onehot, top, scratch, desc):
    shape = list(src.shape)
    steps.done(nc.vector.tensor_reduce(top, src, axis=AX.X, op=ALU.max))
    steps.done(nc.vector.tensor_tensor(scratch, src, top.unsqueeze(2).broadcast_to(shape), ALU.is_equal))
    steps.done(nc.vector.tensor_tensor(scratch, scratch, desc.unsqueeze(1).broadcast_to(shape), ALU.mult))
    steps.done(nc.vector.tensor_reduce(top, scratch, axis=AX.X, op=ALU.max))
    steps.done(nc.vector.tensor_tensor(onehot, desc.unsqueeze(1).broadcast_to(shape), top.unsqueeze(2).broadcast_to(shape),
                                       ALU.is_equal))


def three_parts(nc, steps, src, parts, hi, rest, mid, n):
    steps.done(nc.vector.tensor_copy(hi, src))
    nc.vector.tensor_copy(parts[:, :, 0:n], hi)
    steps.done(nc.vector.tensor_tensor(rest, src, hi, ALU.subtract))
    steps.done(nc.vector.tensor_copy(mid, rest))
    nc.vector.tensor_copy(parts[:, :, n:2 * n], mid)
    return nc.vector.tensor_tensor(parts[:, :, 2 * n:3 * n], rest, mid, ALU.subtract)


def xc_of(x_sb, i, c):
    return x_sb[:, bass.ds(i * TPI + c, 1), :].rearrange("p a d -> p (a d)")


def layer0_ffn(pr, x_sb, common, dram):
    nc, s = pr.nc, pr.sig
    E, CH = 8, 4
    with ExitStack() as ctx:
        def sb(name, shape, dt=F32):
            return ctx.enter_context(nc.sbuf_tensor(f"{name}_f0", shape, dt))
        w = dict(common)
        ident = common["ident"]
        wd, wu = sb("wd", [P, CH * P]), sb("wu", [P, CH, P])
        wr, br = sb("wr", [P, E]), sb("br", [P, E])
        bup, cols, desc = sb("bup", [E, P]), sb("cols", [P, 6 + CH]), sb("desc", [P, E])
        loads = [(wd[:], dram["F0_wd"]), (wu[:], dram["F0_wu"]), (wr[:], dram["F0_wr"]), (cols[:], dram["F0_cols"]),
                 (bup[:], dram["F0_bup"]), (br[:], dram["F0_br"].partition_broadcast(P)),
                 (desc[:], dram["desc8"].partition_broadcast(P))]
        nload = 16 * len(loads)
        bn = sb("bn", [P, 4])
        xn, zh, zT = sb("xn", [P, TPI, P]), sb("zh", [P, TPI, P]), sb("zT", [P, TPI, P])
        zsum, zs, zbn = sb("zsum", [P, TPI]), sb("zs", [P, BPI]), sb("zbn", [P, BPI, P])
        lg, ex, oh, tmp = (sb(n, [P, BPI, E]) for n in ("lg", "ex", "oh", "tmp"))
        top, gsum, gate = (sb(n, [P, BPI]) for n in ("top", "gsum", "gate"))
        sel, bsel = sb("sel", [P, BPI, CH]), sb("bsel", [P, BPI, CH])
        gd, gdb = sb("gd", [E, BPI]), sb("gdb", [E, BPI, P])
        hT = sb("hT", [P, BPI, CH, BPI * P])
        w.update(ln_buffers(sb))
        PS = [ctx.enter_context(nc.psum_tensor(f"ps{c}_f0", [P, 1024], F32)) for c in range(TPI)]
        NST = 2 * LN_STEPS + 1 + 1 + 2 + 2 + 5 + 1 + 1 + 1 + 1
        SETUP = 4
        block = ctx.enter_context(nc.Block())

        @block.sync
        def _(sp):
            load_weights(sp, pr, loads, 0)

        @block.gpsimd
        def _(pool):
            pool.wait_ge(s("act_steps").sem, s("act_steps").at(1))
            nc.gpsimd.tensor_tensor(bn[:, 1:2], bn[:, 0:1], common["mhalf"][:, 0:1], ALU.pow).then_inc(s("pool_steps").sem, 1)
            with pool.Fori(0, ITERS) as i:
                layernorm_pool(pr, pool, 2 * i + 1, w)
                layernorm_pool(pr, pool, 2 * i + 2, w)

        @block.scalar
        def _(act):
            act.wait_ge(s("weights").sem, s("weights").at(nload))
            nc.scalar.activation(bn[:, 0:1], cols[:, 0:1], ACT.Copy, bias=EPS).then_inc(s("act_steps").sem, 1)
            with act.Fori(0, ITERS) as i:
                act.wait_ge(s("hidden").sem, s("hidden").at(i * BPI))
                for c in range(TPI):
                    act.wait_ge(s("ln_T").sem, s("ln_T").at(i * TPI + c + 1))
                    nc.scalar.activation(zT[:, c, :], PS[c][:, 0:P], ACT.Identity, scale=cols[:, 4:5], bias=cols[:, 5:6],
                                         accum_out=zsum[:, c:c + 1]).then_inc(s("z_ready").sem, 1)
                act.wait_ge(s("gate_logits").sem, s("gate_logits").at(2 * i + 2))
                nc.scalar.activation(ex[:], lg[:], ACT.Exp).then_inc(s("gate_exp").sem, 1)
                act.wait_ge(s("gate_ready").sem, s("gate_ready").at(i + 1))
                for b in range(BPI):
                    act.wait_ge(s("hidden").sem, s("hidden").at(i * BPI + b + 1))
                    for j in range(CH):
                        ins = nc.scalar.activation(hT[:, b, j, :], PS[2 * b][:, j * BPI * P:(j + 1) * BPI * P], ACT.Relu,
                                                   scale=sel[:, b, j:j + 1], bias=bsel[:, b, j:j + 1])
                    ins.then_inc(s("hidden_ready").sem, 1)

        @block.tensor
        def _(pe):
            pe.wait_ge(s("weights").sem, s("weights").at(nload))
            with pe.Fori(0, ITERS) as i:
                pe.wait_ge(s("x_added").sem, s("x_added").at(i * TPI))
                pe.wait_ge(s("ln_out").sem, s("ln_out").at(i + 1))
                for c in range(TPI):
                    nc.tensor.transpose(PS[c][:, 0:P], zh[:, c, :], ident[:]).then_inc(s("ln_T").sem, 1)
                pe.wait_ge(s("scaled").sem, s("scaled").at(i + 1))
                for b in range(BPI):
                    ins = nc.tensor.matmul(PS[0][:, 512 + b * E:512 + (b + 1) * E], zbn[:, b, :], wr[:], start=True, stop=True)
                ins.then_inc(s("gate_logits").sem, 1)
                pe.wait_ge(s("gate_ready").sem, s("gate_ready").at(i + 1))
                for b in range(BPI):
                    for j in range(CH):
                        ins = nc.tensor.matmul(PS[2 * b][:, j * BPI * P:(j + 1) * BPI * P], wd[:, j * P:(j + 1) * P],
                                               zT[:, 2 * b:2 * b + 2, :], start=True, stop=True)
                    ins.then_inc(s("hidden").sem, 1)
                for b in range(BPI):
                    pe.wait_ge(s("hidden_ready").sem, s("hidden_ready").at(i * BPI + b + 1))
                    for t in range(2):
                        out = PS[2 * b + 1][:, t * 512:t * 512 + P]
                        for j in range(CH):
                            nc.tensor.matmul(out, hT[:, b, j, t * P:(t + 1) * P], wu[:, j, :], start=j == 0, stop=False)
                        nc.tensor.matmul(out, gdb[:, b, :], bup[:], start=False, stop=True).then_inc(s("ffn_out").sem, 1)

        @block.vector
        def _(dve):
            setup = Steps(dve, s("dve_steps"), 0, SETUP)
            dve.wait_ge(s("weights").sem, s("weights").at(nload))
            dve.wait_ge(s("pool_steps").sem, s("pool_steps").at(1))
            setup.done(nc.vector.tensor_tensor(bn[:, 1:2], bn[:, 1:2], cols[:, 1:2], ALU.mult))
            setup.done(nc.vector.tensor_scalar(bn[:, 2:3], bn[:, 1:2], 1.0 / S, None, ALU.mult))
            setup.done(nc.vector.tensor_tensor(bn[:, 3:4], bn[:, 1:2], cols[:, 3:4], ALU.mult))
            setup.done(nc.vector.tensor_tensor(bn[:, 3:4], cols[:, 2:3], bn[:, 3:4], ALU.subtract))
            setup.end()
            with dve.Fori(0, ITERS) as i:
                steps = Steps(dve, s("dve_steps"), i, NST)
                steps.k = SETUP
                x4 = tile4(x_sb, i)
                layernorm_vector(pr, dve, steps, i, w, x4, xn)
                dve.wait_ge(s("ln_rstd").sem, s("ln_rstd").at(2 * i + 1))
                steps.done(layernorm_apply(pr, dve, w, x4, xn))
                layernorm_vector(pr, dve, steps, i, w, xn, zh)
                dve.wait_ge(s("ln_rstd").sem, s("ln_rstd").at(2 * i + 2))
                layernorm_apply(pr, dve, w, xn, zh).then_inc(s("ln_out").sem, 1)
                dve.wait_ge(s("z_ready").sem, s("z_ready").at(i * TPI + TPI))
                z2 = zsum[:].rearrange("p (b t) -> p b t", t=2)
                steps.done(nc.vector.tensor_tensor(zs[:], z2[:, :, 0], z2[:, :, 1], ALU.add))
                nc.vector.tensor_scalar(zbn[:], zs[:].unsqueeze(2).broadcast_to([P, BPI, P]), bn[:, 2:3], bn[:, 3:4],
                                        ALU.mult, ALU.add).then_inc(s("scaled").sem, 1)
                dve.wait_ge(s("gate_logits").sem, s("gate_logits").at(2 * i + 1))
                lps = PS[0][:, 512:512 + BPI * E].rearrange("p (b e) -> p b e", e=E)
                steps.done(nc.vector.tensor_tensor(lg[:], lps, br[:].unsqueeze(1).broadcast_to([P, BPI, E]), ALU.add))
                steps.done(nc.vector.tensor_reduce(top[:], lg[:], axis=AX.X, op=ALU.max))
                nc.vector.tensor_tensor(lg[:], lg[:], top[:].unsqueeze(2).broadcast_to([P, BPI, E]), ALU.subtract)\
                    .then_inc(s("gate_logits").sem, 1)
                dve.wait_ge(s("gate_logits").sem, s("gate_logits").at(2 * i + 2))
                dve.wait_ge(s("gate_exp").sem, s("gate_exp").at(i + 1))
                steps.done(nc.vector.tensor_reduce(gsum[:], ex[:], axis=AX.X, op=ALU.add))
                steps.done(nc.vector.reciprocal(gate[:], gsum[:]))
                first_max(nc, steps, lg[:], oh[:], top[:], tmp[:], desc[:])
                steps.done(nc.vector.tensor_tensor(oh[:], oh[:], gate[:].unsqueeze(2).broadcast_to([P, BPI, E]), ALU.mult))
                ohp = oh[:].rearrange("p b (j a) -> p b j a", a=2)
                dve.wait_ge(s("hidden_ready").sem, s("hidden_ready").at(i * BPI))
                dve.wait_ge(s("ffn_out").sem, s("ffn_out").at(i * TPI))
                nc.vector.tensor_copy(sel[0:64, :, :], ohp[0:64, :, :, 0])
                nc.vector.tensor_tensor(tmp[0:E, :, :], oh[0:E, :, :], ident[0:E, 0:E].unsqueeze(1).broadcast_to([E, BPI, E]), ALU.mult)
                steps.done(nc.vector.tensor_copy(sel[64:128, :, :], ohp[64:128, :, :, 1]))
                steps.done(nc.vector.tensor_reduce(gd[:], tmp[0:E, :, :], axis=AX.X, op=ALU.add))
                steps.done(nc.vector.tensor_copy(gdb[:], gd[:].unsqueeze(2).broadcast_to([E, BPI, P])))
                nc.vector.tensor_tensor(bsel[:], sel[:], cols[:, 6:6 + CH].unsqueeze(1).broadcast_to([P, BPI, CH]), ALU.mult)\
                    .then_inc(s("gate_ready").sem, 1)
                for c in range(TPI):
                    dve.wait_ge(s("ffn_out").sem, s("ffn_out").at(i * TPI + c + 1))
                    xc = xc_of(x_sb, i, c)
                    nc.vector.tensor_tensor(xc, xc, PS[c - c % 2 + 1][:, (c % 2) * 512:(c % 2) * 512 + P], ALU.add)\
                        .then_inc(s("x_added").sem, 1)
                steps.n += SETUP
                steps.end()

    n1, n4 = ITERS, ITERS * TPI
    pr.end_block(dict(weights=nload, act_steps=1, pool_steps=1, dve_steps=SETUP + NST * n1, ln_var=2 * n1, ln_rstd=2 * n1,
                      ln_out=n1, ln_T=n4, z_ready=n4, scaled=n1, gate_logits=2 * n1, gate_exp=n1, gate_ready=n1,
                      hidden=n1 * BPI, hidden_ready=n1 * BPI, ffn_out=n4, x_added=n4))


def layer1_ffn(pr, x_sb, common, dram):
    nc, s = pr.nc, pr.sig
    E, NE, CH = L1_E, L1_E + 1, L1_CH
    T4 = TPI * P
    with ExitStack() as ctx:
        def sb(name, shape, dt=F32):
            return ctx.enter_context(nc.sbuf_tensor(f"{name}_f1", shape, dt))
        w = dict(common)
        ident = common["ident"]
        w1, w3, w2 = sb("w1", [P, L1_ALL]), sb("w3", [P, L1_ALL]), sb("w2", [P, CH, P])
        cols, gw, gb, desc = sb("cols", [P, 2 * CH]), sb("gw", [P, E]), sb("gb", [P, E]), sb("desc", [P, E])
        b2, self32, selb = sb("b2", [3 * NE, P]), sb("self32", [3 * NE, L1_ALL]), sb("selb", [3 * NE, L1_ALL], BF16)
        loads = [(gw[:], dram["F1_gw"]), (gb[:], dram["F1_gb"].partition_broadcast(P)), (desc[:], dram["desc8"].partition_broadcast(P)),
                 (cols[:], dram["F1_cols"]), (b2[:], dram["F1_b2"]), (self32[:], dram["F1_sel"]),
                 (w1[:], dram["F1_w1"]), (w3[:], dram["F1_w3"]), (w2[:], dram["F1_w2"])]
        nload = 16 * len(loads)
        xn, xT = sb("xn", [P, TPI, P]), sb("xT", [P, T4])
        lg, ex, bi, oh, oh2, tmp = (sb(n, [P, TPI, E]) for n in ("lg", "ex", "bi", "oh", "oh2", "tmp"))
        top, gs = sb("top", [P, TPI]), sb("gs", [P, TPI])
        rw, rest = sb("rw", [P, TPI, NE]), sb("rest", [P, TPI, NE])
        hi, mid = sb("hi", [P, TPI, NE], BF16), sb("mid", [P, TPI, NE], BF16)
        parts = sb("parts", [P, TPI, 3 * NE])
        rwT, rwTb = sb("rwT", [3 * NE, T4]), sb("rwTb", [3 * NE, T4], BF16)
        t3, g, sg, h = (sb(n, [P, 2, T4]) for n in ("t3", "g", "sg", "h"))
        oT = sb("oT", [P, T4])
        w.update(ln_buffers(sb))
        psU = [ctx.enter_context(nc.psum_tensor(f"psU{k}_f1", [P, 2, T4], F32)) for k in range(2)]
        psR = [ctx.enter_context(nc.psum_tensor(f"psR{k}_f1", [P, T4], F32)) for k in range(2)]
        psO = ctx.enter_context(nc.psum_tensor("psO_f1", [P, T4], F32))
        psM = ctx.enter_context(nc.psum_tensor("psM_f1", [P, T4], F32))
        NST = LN_STEPS + 1 + 1 + 1 + 1 + 1 + 5 + 1 + 5 + 1 + 1 + 3
        rows = [min(P, L1_ALL - k * P) for k in range(CH)]
        block = ctx.enter_context(nc.Block())

        @block.sync
        def _(sp):
            load_weights(sp, pr, loads, 0)

        @block.gpsimd
        def _(pool):
            pool.wait_ge(s("weights").sem, s("weights").at(nload))
            nc.gpsimd.tensor_copy(selb[:], self32[:]).then_inc(s("pool_steps").sem, 1)
            pool.wait_ge(s("pool_steps").sem, s("pool_steps").at(1))
            nc.gpsimd.memset(rw[:], 1.0).then_inc(s("pool_steps").sem, 1)
            with pool.Fori(0, ITERS) as i:
                layernorm_pool(pr, pool, i + 1, w)

        @block.scalar
        def _(act):
            act.wait_ge(s("weights").sem, s("weights").at(nload))
            with act.Fori(0, ITERS) as i:
                act.wait_ge(s("ln_T").sem, s("ln_T").at(i + 1))
                nc.scalar.activation(xT[:], psM[:], ACT.Copy).then_inc(s("xT_ready").sem, 1)
                act.wait_ge(s("gate_logits").sem, s("gate_logits").at(2 * i + 2))
                nc.scalar.activation(ex[:], lg[:], ACT.Exp).then_inc(s("gate_exp").sem, 1)
                act.wait_ge(s("gate_T").sem, s("gate_T").at(i + 1))
                nc.scalar.activation(rwT[:], psM[0:3 * NE, :], ACT.Copy)
                nc.scalar.activation(rwTb[:], psM[0:3 * NE, :], ACT.Copy).then_inc(s("gate_parts").sem, 1)

                def silu(k):
                    r = slice(0, rows[k])
                    act.wait_ge(s("hidden_mul").sem, s("hidden_mul").at(i * CH + k + 1))
                    nc.scalar.activation(sg[r, k % 2, :], g[r, k % 2, :], ACT.Silu).then_inc(s("hidden_act").sem, 1)
                for k in range(CH):
                    r = slice(0, rows[k])
                    act.wait_ge(s("hidden").sem, s("hidden").at(i * CH + k + 1))
                    nc.scalar.activation(t3[r, k % 2, :], psU[k % 2][r, 1, :], ACT.Identity, bias=cols[r, CH + k:CH + k + 1])\
                        .then_inc(s("hidden_b").sem, 1)
                    if k:
                        silu(k - 1)
                silu(CH - 1)
                act.wait_ge(s("ffn_out").sem, s("ffn_out").at(i + 1))
                nc.scalar.activation(oT[:], psO[:], ACT.Copy).then_inc(s("ffn_outT").sem, 1)

        @block.tensor
        def _(pe):
            pe.wait_ge(s("weights").sem, s("weights").at(nload))
            pe.wait_ge(s("pool_steps").sem, s("pool_steps").at(2))
            with pe.Fori(0, ITERS) as i:
                pe.wait_ge(s("x_added").sem, s("x_added").at(i * TPI))
                pe.wait_ge(s("ln_out").sem, s("ln_out").at(i + 1))
                for c in range(TPI):
                    ins = nc.tensor.transpose(psM[:, c * P:(c + 1) * P], xn[:, c, :], ident[:])
                ins.then_inc(s("ln_T").sem, 1)
                pe.wait_ge(s("xT_ready").sem, s("xT_ready").at(i + 1))
                for c in range(TPI):
                    ins = nc.tensor.matmul(psM[:, c * E:(c + 1) * E], xT[:, c * P:(c + 1) * P], gw[:], start=True, stop=True)
                ins.then_inc(s("gate_logits").sem, 1)

                def up(k):
                    cs = slice(k * P, k * P + rows[k])
                    r = slice(0, rows[k])
                    pe.wait_ge(s("hidden_mul").sem, s("hidden_mul").at(i * CH + k - 1))
                    nc.tensor.matmul(psU[k % 2][r, 0, :], w1[:, cs], xT[:], start=True, stop=True)
                    nc.tensor.matmul(psU[k % 2][r, 1, :], w3[:, cs], xT[:], start=True, stop=True).then_inc(s("hidden").sem, 1)

                def spread(k):
                    cs = slice(k * P, k * P + rows[k])
                    pe.wait_ge(s("hidden_ready").sem, s("hidden_ready").at(i * CH + k - 1))
                    nc.tensor.matmul(psR[k % 2][0:rows[k], :], selb[:, cs], rwTb[:], start=True, stop=True)\
                        .then_inc(s("gate_bcast").sem, 1)

                def down(k):
                    pe.wait_ge(s("hidden_ready").sem, s("hidden_ready").at(i * CH + k + 1))
                    return nc.tensor.matmul(psO[:], w2[0:rows[k], k, :], h[0:rows[k], k % 2, :], start=False, stop=k == CH - 1)
                up(0)
                up(1)
                pe.wait_ge(s("gate_ready").sem, s("gate_ready").at(i + 1))
                for c in range(TPI):
                    ins = nc.tensor.transpose(psM[0:3 * NE, c * P:(c + 1) * P], parts[:, c, :], ident[:])
                ins.then_inc(s("gate_T").sem, 1)
                pe.wait_ge(s("gate_parts").sem, s("gate_parts").at(i + 1))
                pe.wait_ge(s("ffn_outT").sem, s("ffn_outT").at(i))
                nc.tensor.matmul(psO[:], b2[:], rwT[:], start=True, stop=False)
                for k in range(CH):
                    spread(k)
                    if k >= 1:
                        down(k - 1)
                        if k + 1 < CH:
                            up(k + 1)
                down(CH - 1).then_inc(s("ffn_out").sem, 1)
                pe.wait_ge(s("ffn_outT").sem, s("ffn_outT").at(i + 1))
                for c in range(TPI):
                    ins = nc.tensor.transpose(psM[:, c * P:(c + 1) * P], oT[:, c * P:(c + 1) * P], ident[:])
                ins.then_inc(s("ffn_outT_ready").sem, 1)

        @block.vector
        def _(dve):
            dve.wait_ge(s("weights").sem, s("weights").at(nload))
            dve.wait_ge(s("pool_steps").sem, s("pool_steps").at(2))
            with dve.Fori(0, ITERS) as i:
                steps = Steps(dve, s("dve_steps"), i, NST)
                x4 = tile4(x_sb, i)
                layernorm_vector(pr, dve, steps, i, w, x4, xn)
                dve.wait_ge(s("ln_rstd").sem, s("ln_rstd").at(i + 1))
                layernorm_apply(pr, dve, w, x4, xn).then_inc(s("ln_out").sem, 1)
                g4 = [P, TPI, E]
                dve.wait_ge(s("gate_logits").sem, s("gate_logits").at(2 * i + 1))
                lps = psM[:, 0:TPI * E].rearrange("p (c e) -> p c e", e=E)
                steps.done(nc.vector.tensor_reduce(top[:], lps, axis=AX.X, op=ALU.max))
                nc.vector.tensor_tensor(lg[:], lps, top[:].unsqueeze(2).broadcast_to(g4), ALU.subtract)\
                    .then_inc(s("gate_logits").sem, 1)
                dve.wait_ge(s("gate_exp").sem, s("gate_exp").at(i + 1))
                steps.done(nc.vector.tensor_reduce(gs[:], ex[:], axis=AX.X, op=ALU.add))
                steps.done(nc.vector.reciprocal(gs[:], gs[:]))
                steps.done(nc.vector.tensor_tensor(ex[:], ex[:], gs[:].unsqueeze(2).broadcast_to(g4), ALU.mult))
                steps.done(nc.vector.tensor_tensor(bi[:], ex[:], gb[:].unsqueeze(1).broadcast_to(g4), ALU.add))
                first_max(nc, steps, bi[:], oh[:], top[:], tmp[:], desc[:])
                steps.done(nc.vector.scalar_tensor_tensor(bi[:], oh[:], -1e30, bi[:], ALU.mult, ALU.add))
                first_max(nc, steps, bi[:], oh2[:], top[:], tmp[:], desc[:])
                steps.done(nc.vector.tensor_tensor(oh[:], oh[:], oh2[:], ALU.add))
                steps.done(nc.vector.tensor_tensor(rw[:, :, 0:E], oh[:], ex[:], ALU.mult))
                three_parts(nc, steps, rw[:], parts[:], hi[:], rest[:], mid[:], NE).then_inc(s("gate_ready").sem, 1)

                def weigh(k):
                    r = slice(0, rows[k])
                    dve.wait_ge(s("hidden_act").sem, s("hidden_act").at(i * CH + k + 1))
                    dve.wait_ge(s("gate_bcast").sem, s("gate_bcast").at(i * CH + k + 1))
                    nc.vector.tensor_tensor(h[r, k % 2, :], sg[r, k % 2, :], psR[k % 2][r, :], ALU.mult)\
                        .then_inc(s("hidden_ready").sem, 1)
                for k in range(CH):
                    r = slice(0, rows[k])
                    dve.wait_ge(s("hidden_b").sem, s("hidden_b").at(i * CH + k + 1))
                    nc.vector.scalar_tensor_tensor(g[r, k % 2, :], psU[k % 2][r, 0, :], cols[r, k:k + 1], t3[r, k % 2, :],
                                                   ALU.add, ALU.mult).then_inc(s("hidden_mul").sem, 1)
                    if k:
                        weigh(k - 1)
                weigh(CH - 1)
                dve.wait_ge(s("ffn_outT_ready").sem, s("ffn_outT_ready").at(i + 1))
                nc.vector.tensor_tensor(x4, x4, psM[:].rearrange("p (c d) -> p c d", d=P), ALU.add)\
                    .then_inc(s("x_added").sem, TPI)
                steps.end()

    n1, n4 = ITERS, ITERS * TPI
    pr.end_block(dict(weights=nload, pool_steps=2, dve_steps=NST * n1, ln_var=n1, ln_rstd=n1, ln_out=n1, ln_T=n1, xT_ready=n1,
                      gate_logits=2 * n1, gate_exp=n1, gate_ready=n1, gate_T=n1, gate_parts=n1, hidden=n1 * CH, hidden_b=n1 * CH,
                      hidden_mul=n1 * CH, hidden_act=n1 * CH, hidden_ready=n1 * CH, gate_bcast=n1 * CH, ffn_out=n1, ffn_outT=n1,
                      ffn_outT_ready=n1, x_added=n4))


def layer2_ffn(pr, x_sb, common, dram):
    nc, s = pr.nc, pr.sig
    E = L2_E
    T4 = TPI * P
    with ExitStack() as ctx:
        def sb(name, shape, dt=F32):
            return ctx.enter_context(nc.sbuf_tensor(f"{name}_f2", shape, dt))
        w = dict(common)
        ident = common["ident"]
        wq, wk, wv, wo = (sb(n, [P, E, P]) for n in ("wq", "wk", "wv", "wo"))
        sim, simsq, ones, sg = sb("sim", [P, E]), sb("simsq", [P, E]), sb("ones", [P, P]), sb("sg", [P, E])
        simn = sb("simn", [P, 2, E])
        tri32, tri = sb("tri32", [P, P]), sb("tri", [P, P], BF16)
        desc = sb("desc", [P, E])
        self32, selb = sb("self32", [3 * E, E * P]), sb("selb", [3 * E, E * P], BF16)
        loads = [(sim[:], dram["F2_sim"]), (sg[:], dram["F2_gates"].partition_broadcast(P)), (desc[:], dram["desc16"].partition_broadcast(P)),
                 (ones[:], dram["ones"]), (tri32[:], dram["tri"]), (self32[:], dram["F2_sel"]),
                 (wq[:], dram["F2_wq"]), (wk[:], dram["F2_wk"]), (wv[:], dram["F2_wv"]), (wo[:], dram["F2_wo"])]
        nload = 16 * len(loads)
        xn, xT = sb("xn", [P, TPI, P]), sb("xT", [P, T4])
        sq, ssq, rn = sb("sq", [P, TPI, P]), sb("ssq", [P, TPI]), sb("rn", [P, TPI])
        lg, ex, gated, oh, oh2, tmp, mask, rest = (sb(n, [P, TPI, E]) for n in ("lg", "ex", "gated", "oh", "oh2", "tmp", "mask", "rest"))
        top, gs, inact = sb("top", [P, TPI]), sb("gs", [P, TPI]), sb("inact", [P, TPI])
        hi, mid = sb("hi", [P, TPI, E], BF16), sb("mid", [P, TPI, E], BF16)
        parts, rwTb = sb("parts", [P, TPI, P]), sb("rwTb", [3 * E, T4], BF16)
        xs = sb("xs", [P, 2, T4])
        qkvT = sb("qkvT", [P, 3, T4])
        v = sb("v", [P, TPI, P])
        nmax, rs = sb("nmax", [P, TPI]), sb("rs", [P, TPI])
        p, pT = sb("p", [P, TPI, S]), sb("pT", [P, TPI, S])
        aoT, oT = sb("aoT", [P, T4]), sb("oT", [P, T4])
        w.update(ln_buffers(sb))
        psR = [ctx.enter_context(nc.psum_tensor(f"psR{k}_f2", [P, T4], F32)) for k in range(2)]
        psQKV = [ctx.enter_context(nc.psum_tensor(f"psQ{k}_f2", [P, T4], F32)) for k in range(3)]
        psM = ctx.enter_context(nc.psum_tensor("psM_f2", [P, T4], F32))
        psX = ctx.enter_context(nc.psum_tensor("psX_f2", [P, T4], F32))
        psA = psQKV + [psX]
        NST = LN_STEPS + 1 + 1 + 2 + 5 + 1 + 5 + 1 + 1 + 1 + 1 + 1 + 1 + 1 + 3 + TPI
        SETUP = 5
        block = ctx.enter_context(nc.Block())

        @block.sync
        def _(sp):
            load_weights(sp, pr, loads, 0)

        @block.gpsimd
        def _(pool):
            pool.wait_ge(s("weights").sem, s("weights").at(nload))
            nc.gpsimd.tensor_copy(selb[:], self32[:]).then_inc(s("pool_steps").sem, 1)
            pool.wait_ge(s("pool_steps").sem, s("pool_steps").at(1))
            nc.gpsimd.tensor_copy(tri[:], tri32[:])
            nc.gpsimd.memset(parts[:], 0.0).then_inc(s("pool_steps").sem, 1)
            pool.wait_ge(s("gate_ready").sem, s("gate_ready").at(1))
            nc.gpsimd.tensor_tensor(simn[:, 1, :], simn[:, 0, :], common["mhalf"][:, 0:E], ALU.pow)\
                .then_inc(s("pool_steps").sem, 1)
            with pool.Fori(0, ITERS) as i:
                layernorm_pool(pr, pool, i + 1, w)
                pool.wait_ge(s("quant").sem, s("quant").at(i + 1))
                nc.gpsimd.tensor_tensor(rn[:], ssq[:], common["mhalf"][:, 0:TPI], ALU.pow).then_inc(s("pool_steps").sem, 1)

        @block.scalar
        def _(act):
            act.wait_ge(s("weights").sem, s("weights").at(nload))
            nc.scalar.activation(simsq[:], sim[:], ACT.Square).then_inc(s("act_steps").sem, 1)
            nc.scalar.activation(sg[:], sg[:], ACT.Exp, scale=-1.0).then_inc(s("act_steps").sem, 1)
            with act.Fori(0, ITERS) as i:
                act.wait_ge(s("ln_out").sem, s("ln_out").at(i + 1))
                for c in range(TPI):
                    ins = nc.scalar.activation(sq[:, c, :], xn[:, c, :], ACT.Square, accum_out=ssq[:, c:c + 1])
                ins.then_inc(s("absmax").sem, 1)
                act.wait_ge(s("ln_T").sem, s("ln_T").at(i + 1))
                nc.scalar.activation(xT[:], psM[:], ACT.Copy).then_inc(s("xT_ready").sem, 1)
                act.wait_ge(s("gate_exp").sem, s("gate_exp").at(2 * i + 1))
                nc.scalar.activation(ex[:], lg[:], ACT.Exp).then_inc(s("gate_exp").sem, 1)
                act.wait_ge(s("gate_T").sem, s("gate_T").at(i + 1))
                nc.scalar.activation(rwTb[:], psM[0:3 * E, :], ACT.Copy).then_inc(s("gate_parts").sem, 1)
                act.wait_ge(s("qkv").sem, s("qkv").at(i + 1))
                nc.scalar.activation(qkvT[:, 2, :], psQKV[2][:], ACT.Copy).then_inc(s("qkv_ready").sem, 1)
                nc.scalar.activation(qkvT[:, 0, :], psQKV[0][:], ACT.Copy, scale=float(P) ** -0.5)
                nc.scalar.activation(qkvT[:, 1, :], psQKV[1][:], ACT.Copy).then_inc(s("qkv_ready").sem, 1)
                act.wait_ge(s("vT").sem, s("vT").at(i + 1))
                nc.scalar.activation(v[:].rearrange("p c d -> p (c d)"), psM[:], ACT.Copy).then_inc(s("v_ready").sem, 1)
                for c in range(TPI):
                    nk = P * (c % 2 + 1)
                    act.wait_ge(s("maxed").sem, s("maxed").at(i * TPI + c + 1))
                    nc.scalar.activation(p[:, c, 0:nk], psA[c][:, 0:nk], ACT.Exp, bias=nmax[:, c:c + 1],
                                         accum_out=rs[:, c:c + 1]).then_inc(s("probs").sem, 1)
                for c in range(TPI):
                    nk = P * (c % 2 + 1)
                    act.wait_ge(s("pT").sem, s("pT").at(i * TPI + c + 1))
                    nc.scalar.activation(pT[:, c, 0:nk], psA[c][:, S:S + nk], ACT.Copy).then_inc(s("pT_ready").sem, 1)
                act.wait_ge(s("ao").sem, s("ao").at(i + 1))
                nc.scalar.activation(aoT[:], psM[:], ACT.Copy).then_inc(s("ao_ready").sem, 1)
                act.wait_ge(s("ffn_out").sem, s("ffn_out").at(i + 1))
                nc.scalar.activation(oT[:], psX[:], ACT.Copy).then_inc(s("ffn_outT").sem, 1)

        @block.tensor
        def _(pe):
            pe.wait_ge(s("weights").sem, s("weights").at(nload))
            pe.wait_ge(s("pool_steps").sem, s("pool_steps").at(2))
            pe.wait_ge(s("act_steps").sem, s("act_steps").at(1))
            nc.tensor.matmul(psM[:, 0:E], ones[:], simsq[:], start=True, stop=True).then_inc(s("gate_logits").sem, 1)
            pe.wait_ge(s("gate_ready").sem, s("gate_ready").at(2))
            with pe.Fori(0, ITERS) as i:
                pe.wait_ge(s("x_added").sem, s("x_added").at(i * TPI))
                pe.wait_ge(s("ln_out").sem, s("ln_out").at(i + 1))
                for c in range(TPI):
                    ins = nc.tensor.transpose(psM[:, c * P:(c + 1) * P], xn[:, c, :], ident[:])
                ins.then_inc(s("ln_T").sem, 1)
                pe.wait_ge(s("xT_ready").sem, s("xT_ready").at(i + 1))
                for c in range(TPI):
                    ins = nc.tensor.matmul(psM[:, c * E:(c + 1) * E], xT[:, c * P:(c + 1) * P], simn[:, 0, :], start=True, stop=True)
                ins.then_inc(s("gate_logits").sem, 1)
                pe.wait_ge(s("gate_ready").sem, s("gate_ready").at(i + 3))
                for c in range(TPI):
                    ins = nc.tensor.transpose(psM[:, c * P:(c + 1) * P], parts[:, c, :], ident[:])
                ins.then_inc(s("gate_T").sem, 1)
                pe.wait_ge(s("gate_parts").sem, s("gate_parts").at(i + 1))

                def spread(m):
                    pe.wait_ge(s("scaled").sem, s("scaled").at(i * 2 * E + m - 1))
                    nc.tensor.matmul(psR[m % 2][:], selb[:, (m % E) * P:(m % E + 1) * P], rwTb[:], start=True, stop=True)\
                        .then_inc(s("gate_bcast").sem, 1)
                spread(0)
                for e in range(E):
                    if e + 1 < E:
                        spread(e + 1)
                    pe.wait_ge(s("scaled").sem, s("scaled").at(i * 2 * E + e + 1))
                    for n, wt in enumerate((wq, wk, wv)):
                        ins = nc.tensor.matmul(psQKV[n][:], wt[:, e, :], xs[:, e % 2, :], start=e == 0, stop=e == E - 1)
                    ins.then_inc(s("qkv").sem if e == E - 1 else s("hidden").sem, 1)
                pe.wait_ge(s("qkv_ready").sem, s("qkv_ready").at(2 * i + 1))
                for c in range(TPI):
                    ins = nc.tensor.transpose(psM[:, c * P:(c + 1) * P], qkvT[:, 2, c * P:(c + 1) * P], ident[:])
                ins.then_inc(s("vT").sem, 1)
                pe.wait_ge(s("qkv_ready").sem, s("qkv_ready").at(2 * i + 2))
                for c in range(TPI):
                    t, b = c % 2, c // 2
                    nk = P * (t + 1)
                    nc.tensor.matmul(psA[c][:, 0:nk], qkvT[:, 0, c * P:(c + 1) * P], qkvT[:, 1, b * S:b * S + nk], start=True, stop=False)
                    nc.tensor.matmul(psA[c][:, t * P:nk], common["identb"][:], tri[:], start=False, stop=True).then_inc(s("scores").sem, 1)
                for c in range(TPI):
                    pe.wait_ge(s("heads_norm").sem, s("heads_norm").at(i * TPI + c + 1))
                    for k in range(c % 2 + 1):
                        ins = nc.tensor.transpose(psA[c][:, S + k * P:S + (k + 1) * P], p[:, c, k * P:(k + 1) * P], ident[:])
                    ins.then_inc(s("pT").sem, 1)
                pe.wait_ge(s("v_ready").sem, s("v_ready").at(i + 1))
                for c in range(TPI):
                    pe.wait_ge(s("pT_ready").sem, s("pT_ready").at(i * TPI + c + 1))
                    for k in range(c % 2 + 1):
                        ins = nc.tensor.matmul(psM[:, c * P:(c + 1) * P], v[:, c - c % 2 + k, :], pT[:, c, k * P:(k + 1) * P],
                                               start=k == 0, stop=k == c % 2)
                ins.then_inc(s("ao").sem, 1)
                spread(E)
                for e in range(E):
                    if e + 1 < E:
                        spread(E + e + 1)
                    pe.wait_ge(s("scaled").sem, s("scaled").at(i * 2 * E + E + e + 1))
                    ins = nc.tensor.matmul(psX[:], wo[:, e, :], xs[:, e % 2, :], start=e == 0, stop=e == E - 1)
                    ins.then_inc(s("ffn_out").sem if e == E - 1 else s("hidden").sem, 1)
                pe.wait_ge(s("ffn_outT").sem, s("ffn_outT").at(i + 1))
                for c in range(TPI):
                    ins = nc.tensor.transpose(psM[:, c * P:(c + 1) * P], oT[:, c * P:(c + 1) * P], ident[:])
                ins.then_inc(s("ffn_outT_ready").sem, 1)

        @block.vector
        def _(dve):
            setup = Steps(dve, s("dve_steps"), 0, SETUP)
            dve.wait_ge(s("weights").sem, s("weights").at(nload))
            dve.wait_ge(s("gate_logits").sem, s("gate_logits").at(1))
            nc.vector.tensor_scalar(simn[:, 0, :], psM[:, 0:E], 1e-12, None, ALU.add).then_inc(s("gate_ready").sem, 1)
            dve.wait_ge(s("pool_steps").sem, s("pool_steps").at(3))
            nc.vector.tensor_tensor(simn[:, 0, :], sim[:], simn[:, 1, :], ALU.mult).then_inc(s("gate_ready").sem, 1)
            dve.wait_ge(s("act_steps").sem, s("act_steps").at(2))
            setup.done(nc.vector.tensor_scalar(sg[:], sg[:], 1.0, None, ALU.add))
            setup.done(nc.vector.reciprocal(sg[:], sg[:]))
            setup.n = 2
            setup.end()
            with dve.Fori(0, ITERS) as i:
                steps = Steps(dve, s("dve_steps"), i, NST)
                steps.k = 2
                x4 = tile4(x_sb, i)
                layernorm_vector(pr, dve, steps, i, w, x4, xn)
                dve.wait_ge(s("ln_rstd").sem, s("ln_rstd").at(i + 1))
                layernorm_apply(pr, dve, w, x4, xn).then_inc(s("ln_out").sem, 1)
                g4 = [P, TPI, E]
                dve.wait_ge(s("absmax").sem, s("absmax").at(i + 1))
                nc.vector.tensor_scalar(ssq[:], ssq[:], 1e-12, None, ALU.add).then_inc(s("quant").sem, 1)
                dve.wait_ge(s("pool_steps").sem, s("pool_steps").at(4 + i))
                dve.wait_ge(s("gate_logits").sem, s("gate_logits").at(i + 2))
                lps = psM[:, 0:TPI * E].rearrange("p (c e) -> p c e", e=E)
                steps.done(nc.vector.tensor_tensor(lg[:], lps, rn[:].unsqueeze(2).broadcast_to(g4), ALU.mult))
                steps.done(nc.vector.tensor_tensor(lg[:], lg[:], sg[:].unsqueeze(1).broadcast_to(g4), ALU.subtract))
                nc.vector.tensor_scalar(gated[:], lg[:], 0.0, None, ALU.max)
                nc.vector.tensor_scalar(mask[:], lg[:], 0.0, None, ALU.is_gt)
                first_max(nc, steps, lg[:], oh[:], gs[:], tmp[:], desc[:])
                steps.done(nc.vector.tensor_reduce(top[:], gated[:], axis=AX.X, op=ALU.max))
                steps.done(nc.vector.tensor_scalar(inact[:], top[:], 0.0, None, ALU.is_le))
                steps.done(nc.vector.scalar_tensor_tensor(lg[:], oh[:], -1e30, lg[:], ALU.mult, ALU.add))
                first_max(nc, steps, lg[:], oh2[:], gs[:], tmp[:], desc[:])
                nc.vector.tensor_tensor(lg[:], gated[:], top[:].unsqueeze(2).broadcast_to(g4), ALU.subtract)\
                    .then_inc(s("gate_exp").sem, 1)
                steps.done(nc.vector.tensor_tensor(oh[:], oh[:], oh2[:], ALU.add))
                steps.done(nc.vector.tensor_tensor(oh[:], oh[:], inact[:].unsqueeze(2).broadcast_to(g4), ALU.mult))
                steps.done(nc.vector.tensor_tensor(mask[:], mask[:], oh[:], ALU.add))
                dve.wait_ge(s("gate_exp").sem, s("gate_exp").at(2 * i + 2))
                steps.done(nc.vector.tensor_tensor(ex[:], ex[:], mask[:], ALU.mult))
                steps.done(nc.vector.tensor_reduce(gs[:], ex[:], axis=AX.X, op=ALU.add))
                steps.done(nc.vector.reciprocal(gs[:], gs[:]))
                steps.done(nc.vector.tensor_tensor(ex[:], ex[:], gs[:].unsqueeze(2).broadcast_to(g4), ALU.mult))
                three_parts(nc, steps, ex[:], parts[:], hi[:], rest[:], mid[:], E).then_inc(s("gate_ready").sem, 1)

                def scale_by(m, src):
                    dve.wait_ge(s("gate_bcast").sem, s("gate_bcast").at(i * 2 * E + m + 1))
                    if m % E >= 2:
                        dve.wait_ge(s("hidden").sem, s("hidden").at(i * 2 * (E - 1) + (m // E) * (E - 1) + m % E - 1))
                    nc.vector.tensor_tensor(xs[:, m % 2, :], src, psR[m % 2][:], ALU.mult).then_inc(s("scaled").sem, 1)
                for e in range(E):
                    scale_by(e, xT[:])
                for c in range(TPI):
                    nk = P * (c % 2 + 1)
                    dve.wait_ge(s("scores").sem, s("scores").at(i * TPI + c + 1))
                    nc.vector.tensor_reduce(nmax[:, c:c + 1], psA[c][:, 0:nk], axis=AX.X, op=ALU.max, negate=True)\
                        .then_inc(s("maxed").sem, 1)
                for c in range(TPI):
                    nk = P * (c % 2 + 1)
                    dve.wait_ge(s("probs").sem, s("probs").at(i * TPI + c + 1))
                    steps.done(nc.vector.reciprocal(rs[:, c:c + 1], rs[:, c:c + 1]))
                    nc.vector.tensor_scalar(p[:, c, 0:nk], p[:, c, 0:nk], rs[:, c:c + 1], None, ALU.mult)\
                        .then_inc(s("heads_norm").sem, 1)
                dve.wait_ge(s("ao_ready").sem, s("ao_ready").at(i + 1))
                for e in range(E):
                    scale_by(E + e, aoT[:])
                dve.wait_ge(s("ffn_outT_ready").sem, s("ffn_outT_ready").at(i + 1))
                nc.vector.tensor_tensor(x4, x4, psM[:].rearrange("p (c d) -> p c d", d=P), ALU.add)\
                    .then_inc(s("x_added").sem, TPI)
                steps.n += 2
                steps.end()

    n1, n4 = ITERS, ITERS * TPI
    pr.end_block(dict(weights=nload, pool_steps=3 + n1, act_steps=2, dve_steps=2 + NST * n1, ln_var=n1, ln_rstd=n1, ln_out=n1,
                      ln_T=n1, xT_ready=n1, gate_logits=n1 + 1, gate_ready=n1 + 2, gate_exp=2 * n1, gate_T=n1, gate_parts=n1,
                      absmax=n1, quant=n1, gate_bcast=2 * E * n1, scaled=2 * E * n1, hidden=2 * (E - 1) * n1, qkv=n1,
                      qkv_ready=2 * n1, vT=n1, v_ready=n1, scores=n4, maxed=n4, probs=n4, heads_norm=n4, pT=n4, pT_ready=n4,
                      ao=n1, ao_ready=n1, ffn_out=n1, ffn_outT=n1, ffn_outT_ready=n1, x_added=n4))


def layer3_ffn(pr, x_sb, common, dram):
    nc, s = pr.nc, pr.sig
    T4 = TPI * P
    NI = L3_I // P
    QMAX = 32767.0
    with ExitStack() as ctx:
        def sb(name, shape, dt=F32):
            return ctx.enter_context(nc.sbuf_tensor(f"{name}_f3", shape, dt))
        w = dict(common)
        ident = common["ident"]
        up, gt = sb("up", [P, NI, ITERS, T4]), sb("gt", [P, NI, ITERS, T4])
        wraw = sb("wraw", [P, 3, L3_I])
        wT = sb("wT", [P, 3, L3_I])
        ws, wi = sb("ws", [P, 3, L3_I // BLK]), sb("wi", [P, 3, L3_I // BLK])
        loads = [(wraw[:], dram["F3_w"])]
        xn, xT = sb("xn", [P, TPI, P]), sb("xT", [P, ITERS, T4])
        xq, oT = sb("xq", [P, 3, T4]), sb("oT", [P, T4])
        am = sb("am", [P, 5, ITERS, NI])
        amr, gm = sb("amr", [P, 5]), sb("gm", [P, 5])
        scale, inv = sb("scale", [P, 5]), sb("inv", [P, 5])
        w.update(ln_buffers(sb))
        PS = [ctx.enter_context(nc.psum_tensor(f"ps{c}_f3", [P, T4], F32)) for c in range(8)]
        X, U, G, GS, O = range(5)

        def close_block(counts):
            pr.end_block(counts)

        def quantise(eng_steps, dst, src, k, clip=None):
            eng_steps.done(nc.vector.tensor_scalar(dst, src, inv[:, k:k + 1], MAGIC, ALU.mult, ALU.add))
            return nc.vector.tensor_scalar(dst, dst, -MAGIC, scale[:, k:k + 1], ALU.add, ALU.mult)

        def scale_vector(dve, steps, k, n, width):
            nc.vector.tensor_reduce(amr[:, k:k + 1], am[:, k, :, 0:width], axis=AX.XY, op=ALU.max).then_inc(s("absmax").sem, 1)
            dve.wait_ge(s("gmax").sem, s("gmax").at(n))
            steps.done(nc.vector.tensor_scalar(scale[:, k:k + 1], gm[:, k:k + 1], 1.0 / QMAX, 1e-12, ALU.mult, ALU.max))
            steps.done(nc.vector.reciprocal(inv[:, k:k + 1], scale[:, k:k + 1]))

        def gmax_pool(pool, k, n):
            pool.wait_ge(s("absmax").sem, s("absmax").at(n))
            nc.gpsimd.partition_all_reduce(gm[:, k:k + 1], amr[:, k:k + 1], P, bass.bass_isa.ReduceOp.max)\
                .then_inc(s("gmax").sem, 1)

        NW = 6
        with nc.Block() as block:
            @block.sync
            def _(sp):
                load_weights(sp, pr, loads, 0)

            @block.gpsimd
            def _(pool):
                with pool.Fori(0, ITERS) as i:
                    layernorm_pool(pr, pool, i + 1, w)
                gmax_pool(pool, X, 1)

            @block.scalar
            def _(act):
                for k in range(3):
                    act.wait_ge(s("vT").sem, s("vT").at(k + 1))
                    nc.scalar.activation(wT[:, k, :], PS[5 + k][:, 0:L3_I], ACT.Copy).then_inc(s("v_ready").sem, 1)
                with act.Fori(0, ITERS) as i:
                    act.wait_ge(s("ln_T").sem, s("ln_T").at(i + 1))
                    nc.scalar.activation(xT[:, bass.ds(i, 1), :].rearrange("p a t -> p (a t)"), PS[0][:], ACT.Copy)\
                        .then_inc(s("xT_ready").sem, 1)

            @block.tensor
            def _(pe):
                pe.wait_ge(s("quant").sem, s("quant").at(1))
                for k in range(3):
                    for j in range(NI):
                        ins = nc.tensor.transpose(PS[5 + k][:, j * P:(j + 1) * P], wraw[:, k, j * P:(j + 1) * P], ident[:])
                    ins.then_inc(s("vT").sem, 1)
                with pe.Fori(0, ITERS) as i:
                    pe.wait_ge(s("ln_out").sem, s("ln_out").at(i + 1))
                    pe.wait_ge(s("xT_ready").sem, s("xT_ready").at(i))
                    for c in range(TPI):
                        ins = nc.tensor.transpose(PS[0][:, c * P:(c + 1) * P], xn[:, c, :], ident[:])
                    ins.then_inc(s("ln_T").sem, 1)

            @block.vector
            def _(dve):
                st = Steps(dve, s("dve_steps"), 0, NW)
                dve.wait_ge(s("weights").sem, s("weights").at(16))
                wb = wraw[:].rearrange("p k (n b) -> p (k n) b", b=BLK)
                wsf, wif = ws[:].rearrange("p k n -> p (k n)"), wi[:].rearrange("p k n -> p (k n)")
                full = list(wb.shape)
                st.done(nc.vector.tensor_reduce(wsf, wb, axis=AX.X, op=ALU.max, apply_absolute_value=True))
                st.done(nc.vector.tensor_scalar(wsf, wsf, 1.0 / 7.0, 1e-12, ALU.mult, ALU.max))
                st.done(nc.vector.reciprocal(wif, wsf))
                st.done(nc.vector.tensor_tensor(wb, wb, wif.unsqueeze(2).broadcast_to(full), ALU.mult))
                st.done(nc.vector.tensor_scalar(wraw[:], wraw[:], MAGIC, -MAGIC, ALU.add, ALU.add))
                st.done(nc.vector.tensor_scalar(wraw[:], wraw[:], 7.0, -8.0, ALU.min, ALU.max))
                nc.vector.tensor_tensor(wb, wb, wsf.unsqueeze(2).broadcast_to(full), ALU.mult).then_inc(s("quant").sem, 1)
                st.end()
                with dve.Fori(0, ITERS) as i:
                    steps = Steps(dve, s("dve_steps"), i, LN_STEPS)
                    steps.k = NW
                    x4 = tile4(x_sb, i)
                    layernorm_vector(pr, dve, steps, i, w, x4, xn)
                    dve.wait_ge(s("ln_rstd").sem, s("ln_rstd").at(i + 1))
                    dve.wait_ge(s("ln_T").sem, s("ln_T").at(i))
                    layernorm_apply(pr, dve, w, x4, xn).then_inc(s("ln_out").sem, 1)
                    dve.wait_ge(s("ln_out").sem, s("ln_out").at(i + 1))
                    nc.vector.tensor_reduce(am[:, X, bass.ds(i, 1), 0:1].rearrange("p a b -> p (a b)"), xn[:], axis=AX.XY,
                                            op=ALU.max, apply_absolute_value=True).then_inc(s("maxed").sem, 1)
                fin = Steps(dve, s("dve_steps"), 0, 2)
                fin.k = NW + LN_STEPS * ITERS
                dve.wait_ge(s("maxed").sem, s("maxed").at(ITERS))
                scale_vector(dve, fin, X, 1, 1)
        pr.end_block(dict(weights=16, ln_var=ITERS, ln_rstd=ITERS, absmax=1, gmax=1, vT=3, v_ready=3, ln_T=ITERS, xT_ready=ITERS,
                          quant=1, ln_out=ITERS, maxed=ITERS, dve_steps=NW + LN_STEPS * ITERS + 2))

        with nc.Block() as block:
            @block.gpsimd
            def _(pool):
                gmax_pool(pool, U, 1)
                gmax_pool(pool, G, 2)

            @block.tensor
            def _(pe):
                with pe.Fori(0, ITERS) as i:
                    pe.wait_ge(s("quant").sem, s("quant").at(i + 1))
                    for n in range(2 * NI):
                        pe.wait_ge(s("hidden_b").sem, s("hidden_b").at(i * 2 * NI))
                        nc.tensor.matmul(PS[n][:], wT[:, n // NI, (n % NI) * P:(n % NI + 1) * P], xq[:, 0, :], start=True, stop=True)\
                            .then_inc(s("hidden").sem, 1)

            def kept(n, i):
                return (gt if n < NI else up)[:, n % NI, bass.ds(i, 1), :].rearrange("p a t -> p (a t)")

            @block.scalar
            def _(act):
                with act.Fori(0, ITERS) as i:
                    for n in range(2 * NI):
                        act.wait_ge(s("hidden").sem, s("hidden").at(i * 2 * NI + n + 1))
                        nc.scalar.activation(kept(n, i), PS[n][:], ACT.Copy).then_inc(s("hidden_b").sem, 1)

            @block.vector
            def _(dve):
                with dve.Fori(0, ITERS) as i:
                    steps = Steps(dve, s("dve_steps"), i, 1)
                    dve.wait_ge(s("hidden").sem, s("hidden").at(i * 2 * NI))
                    quantise(steps, xq[:, 0, :], xT[:, bass.ds(i, 1), :].rearrange("p a t -> p (a t)"), X).then_inc(s("quant").sem, 1)
                    for k, kept_k in ((G, gt), (U, up)):
                        dve.wait_ge(s("hidden_b").sem, s("hidden_b").at(i * 2 * NI + (NI if k == G else 2 * NI)))
                        nc.vector.tensor_reduce(am[:, k, bass.ds(i, 1), 0:1].rearrange("p a b -> p (a b)"),
                                                kept_k[:, :, bass.ds(i, 1), :].rearrange("p n a t -> p (n a) t"), axis=AX.XY,
                                                op=ALU.max, apply_absolute_value=True).then_inc(s("maxed").sem, 1)
                fin = Steps(dve, s("dve_steps"), 0, 4)
                fin.k = ITERS
                dve.wait_ge(s("maxed").sem, s("maxed").at(ITERS * 2))
                scale_vector(dve, fin, U, 1, 1)
                scale_vector(dve, fin, G, 2, 1)
        pr.end_block(dict(absmax=2, gmax=2, quant=ITERS, hidden=ITERS * 2 * NI, hidden_b=ITERS * 2 * NI, maxed=ITERS * 2,
                          dve_steps=ITERS + 4))

        with nc.Block() as block:
            ROWS3 = ITERS * NI
            upf, gtf = up[:].rearrange("p n i t -> p (n i) t"), gt[:].rearrange("p n i t -> p (n i) t")
            amf = am[:, GS, :, :].rearrange("p i n -> p (i n)")

            def part(t, i):
                return t[:, bass.ds(i, 1), :].rearrange("p a t -> p (a t)")

            @block.gpsimd
            def _(pool):
                gmax_pool(pool, GS, 1)

            @block.scalar
            def _(act):
                with act.Fori(0, ROWS3) as i:
                    act.wait_ge(s("quant").sem, s("quant").at(i + 1))
                    nc.scalar.activation(xq[:, 0, :], part(gtf, i), ACT.Sigmoid).then_inc(s("hidden_act").sem, 1)

            @block.vector
            def _(dve):
                with dve.Fori(0, ROWS3) as i:
                    steps = Steps(dve, s("dve_steps"), i, 5)
                    quantise(steps, part(gtf, i), part(gtf, i), G).then_inc(s("quant").sem, 1)
                    quantise(steps, part(upf, i), part(upf, i), U)
                    dve.wait_ge(s("hidden_act").sem, s("hidden_act").at(i + 1))
                    steps.done(nc.vector.tensor_scalar(xq[:, 1, :], xq[:, 0, :], 65536.0, MAGIC, ALU.mult, ALU.add))
                    steps.done(nc.vector.tensor_scalar(xq[:, 1, :], xq[:, 1, :], -MAGIC, 65535.0, ALU.add, ALU.min))
                    steps.done(nc.vector.scalar_tensor_tensor(part(gtf, i), xq[:, 1, :], 1.0 / 65536.0, part(gtf, i), ALU.mult, ALU.mult))
                    nc.vector.tensor_reduce(amf[:, bass.ds(i, 1)], part(gtf, i), axis=AX.X, op=ALU.max,
                                            apply_absolute_value=True).then_inc(s("maxed").sem, 1)
                    steps.end()
                fin = Steps(dve, s("dve_steps"), 0, 2)
                fin.k = 5 * ROWS3
                dve.wait_ge(s("maxed").sem, s("maxed").at(ROWS3))
                scale_vector(dve, fin, GS, 1, NI)
        pr.end_block(dict(absmax=1, gmax=1, quant=ROWS3, hidden_act=ROWS3, maxed=ROWS3, dve_steps=5 * ROWS3 + 2))

        with nc.Block() as block:
            amo = am[:, O, :, :].rearrange("p i n -> p (i n)")

            @block.gpsimd
            def _(pool):
                gmax_pool(pool, O, 1)

            @block.vector
            def _(dve):
                with dve.Fori(0, ROWS3) as i:
                    steps = Steps(dve, s("dve_steps"), i, 3)
                    steps.done(quantise(steps, part(gtf, i), part(gtf, i), GS))
                    steps.done(nc.vector.tensor_tensor(part(gtf, i), part(gtf, i), part(upf, i), ALU.mult))
                    nc.vector.tensor_reduce(amo[:, bass.ds(i, 1)], part(gtf, i), axis=AX.X, op=ALU.max,
                                            apply_absolute_value=True).then_inc(s("maxed").sem, 1)
                    steps.end()
                fin = Steps(dve, s("dve_steps"), 0, 2)
                fin.k = 3 * ROWS3
                dve.wait_ge(s("maxed").sem, s("maxed").at(ROWS3))
                scale_vector(dve, fin, O, 1, NI)
        pr.end_block(dict(absmax=1, gmax=1, maxed=ROWS3, dve_steps=3 * ROWS3 + 2))

        with nc.Block() as block:
            @block.tensor
            def _(pe):
                with pe.Fori(0, ITERS) as i:
                    pe.wait_ge(s("ffn_outT").sem, s("ffn_outT").at(i))
                    for n in range(NI):
                        pe.wait_ge(s("quant").sem, s("quant").at(i * NI + n + 1))
                        ins = nc.tensor.matmul(PS[0][:], wT[:, 2, :].rearrange("p (n d) -> p n d", d=P)[:, n, :], xq[:, n, :],
                                               start=n == 0, stop=n == NI - 1)
                    ins.then_inc(s("ffn_out").sem, 1)
                    pe.wait_ge(s("ffn_outT").sem, s("ffn_outT").at(i + 1))
                    pe.wait_ge(s("x_added").sem, s("x_added").at(i * TPI))
                    for c in range(TPI):
                        ins = nc.tensor.transpose(PS[1][:, c * P:(c + 1) * P], oT[:, c * P:(c + 1) * P], ident[:])
                    ins.then_inc(s("ffn_outT_ready").sem, 1)

            @block.scalar
            def _(act):
                with act.Fori(0, ITERS) as i:
                    act.wait_ge(s("ffn_out").sem, s("ffn_out").at(i + 1))
                    act.wait_ge(s("ffn_outT_ready").sem, s("ffn_outT_ready").at(i))
                    nc.scalar.activation(oT[:], PS[0][:], ACT.Copy).then_inc(s("ffn_outT").sem, 1)

            @block.vector
            def _(dve):
                with dve.Fori(0, ITERS) as i:
                    steps = Steps(dve, s("dve_steps"), i, NI)
                    dve.wait_ge(s("ffn_out").sem, s("ffn_out").at(i))
                    for n in range(NI):
                        quantise(steps, xq[:, n, :], gt[:, n, bass.ds(i, 1), :].rearrange("p a t -> p (a t)"), O).then_inc(s("quant").sem, 1)
                    dve.wait_ge(s("ffn_outT_ready").sem, s("ffn_outT_ready").at(i + 1))
                    x4 = tile4(x_sb, i)
                    nc.vector.tensor_tensor(x4, x4, PS[1][:].rearrange("p (c d) -> p c d", d=P), ALU.add)\
                        .then_inc(s("x_added").sem, TPI)
                    steps.end()
        pr.end_block(dict(quant=ITERS * NI, ffn_out=ITERS, ffn_outT=ITERS, ffn_outT_ready=ITERS, x_added=ITERS * TPI,
                          dve_steps=ITERS * NI))


def build(nc, dram, out):
    with ExitStack() as ctx:
        pr = Program(nc, ctx)
        for name in SIGNALS:
            pr.sig(name)
        x_sb = ctx.enter_context(nc.sbuf_tensor("x_sb", [P, TILES, P], F32))
        common = {}

        def csb(name, shape, dt=F32):
            common[name] = ctx.enter_context(nc.sbuf_tensor(name, shape, dt))
            return common[name]
        csb("ident", [P, P]), csb("identb", [P, P], BF16), csb("ctxT", [P, B * P]), csb("headmask", [P, H])
        csb("mhalf", [P, 16])
        with nc.Block() as block:
            @block.sync
            def _(sp):
                n = load_weights(sp, pr, [(x_sb[:], dram["x"]), (common["ident"][:], dram["ident"]),
                                          (common["headmask"][:], dram["headmask"]), (common["ctxT"][:], dram["ctxT"])],
                                 0)
                sp.wait_ge(pr.sig("weights").sem, n + Signal.PRIME)

            @block.gpsimd
            def _(pool):
                for g in pr.named.values():
                    pool.sem_inc(g.sem, Signal.PRIME)
                nc.gpsimd.memset(common["mhalf"][:], -0.5)

            @block.vector
            def _(dve):
                dve.wait_ge(pr.sig("weights").sem, 64 + Signal.PRIME)
                nc.vector.tensor_copy(common["identb"][:], common["ident"][:])
        pr.end_block(dict(weights=64))
        for n in range(N_SUBLAYERS):
            if n % 2 == 0:
                context_attention(pr, x_sb, common, dram, n // 2)
            elif n == 1:
                layer0_ffn(pr, x_sb, common, dram)
            elif n == 3:
                layer1_ffn(pr, x_sb, common, dram)
            elif n == 5:
                layer2_ffn(pr, x_sb, common, dram)
            else:
                layer3_ffn(pr, x_sb, common, dram)
        with nc.Block() as block:
            @block.sync
            def _(sp):
                sp.dma_start(out, x_sb[:]).then_inc(pr.sig("out_stored").sem, 16)
                sp.wait_ge(pr.sig("out_stored").sem, pr.sig("out_stored").at(16))


def laid_out(inp):
    import numpy as np
    f = {k: np.asarray(v) for k, v in inp.items()}

    def rows(a):
        return a.reshape(-1, P, a.shape[-1]).transpose(1, 0, 2)

    d = {}
    d["x"] = rows(f["x"].reshape(B * S, P))
    ct = f["ctx_1024"].transpose(2, 0, 1)
    d["ctxT"] = np.concatenate([ct, ct], axis=2).reshape(P, B * P)
    d["mask"] = f["mask_Bx1xSxS2_ik1"].reshape(TILES, P, SC).transpose(1, 0, 2)
    d["ident"] = np.eye(P, dtype=np.float32)
    d["headmask"] = np.kron(np.eye(H, dtype=np.float32), np.ones((P // H, 1), np.float32))
    d["L0_wqT"], d["L0_wkT"] = rows(f["L0_xattn_Wq"].T), rows(f["L0_xattn_Wk"].T)
    d["L0_wv"], d["L0_wo"] = f["L0_xattn_Wv"], rows(f["L0_xattn_Wo"])
    d["L0_bo"] = f["L0_xattn_bo"]
    zero = np.zeros(P, np.float32)
    eye = np.eye(P, dtype=np.float32)
    d["L1_w4"] = np.stack([eye, eye, eye, f["L1_xattn_w_proj"].T], axis=1)
    d["L1_cols"] = np.stack([zero, zero, zero], axis=1)
    d["L1_bo"] = f["L1_xattn_b_proj"]
    d["L2_w4"] = np.stack([f["L2_xattn_wq"], f["L2_xattn_wk"], f["L2_xattn_wv"], f["L2_xattn_wo"]], axis=1)
    d["L2_cols"] = np.stack([zero, zero, zero], axis=1)
    d["L2_bo"] = f["L2_xattn_bo"]
    d["L3_w4"] = np.stack([f["L3_xattn_Wq"].T, f["L3_xattn_Wk"].T, f["L3_xattn_Wv"].T, f["L3_xattn_Wo"].T], axis=1)
    d["L3_cols"] = np.stack([f["L3_xattn_bq"], f["L3_xattn_bk"], f["L3_xattn_bv"]], axis=1)
    d["L3_bo"] = f["L3_xattn_bo"]
    d["desc8"] = np.arange(8, 0, -1).astype(np.float32)
    d["F0_wd"] = f["L0_ffn_W_down"].transpose(1, 0, 2).reshape(P, 512)
    d["F0_wu"] = rows(f["L0_ffn_W_up"].reshape(512, P))
    d["F0_wr"], d["F0_br"], d["F0_bup"] = f["L0_ffn_Wr"], f["L0_ffn_br"], f["L0_ffn_b_up"]
    d["F0_cols"] = np.concatenate([np.stack([f["L0_ffn_" + k] for k in ("bn_var", "bn_g", "bn_b", "bn_mean", "ln_g", "ln_b")],
                                            axis=1), f["L0_ffn_b_down"].reshape(4, P).T], axis=1)

    def joined(a, b):
        return np.concatenate([a, b[None]], axis=0)

    def chunked(a):
        out = np.zeros((L1_CH * P, a.shape[1]), a.dtype)
        out[:L1_ALL] = a
        return rows(out)

    for k in ("w1", "w3"):
        d["F1_" + k] = joined(f["L1_ffn_" + k], f["L1_ffn_s" + k]).transpose(1, 0, 2).reshape(P, L1_ALL)
    d["F1_w2"] = chunked(joined(f["L1_ffn_w2"], f["L1_ffn_sw2"]).reshape(L1_ALL, P))
    d["F1_cols"] = np.concatenate([chunked(joined(f["L1_ffn_" + k], f["L1_ffn_s" + k]).reshape(L1_ALL, 1))[:, :, 0]
                                   for k in ("b1", "b3")], axis=1)
    d["F1_b2"] = np.concatenate([joined(f["L1_ffn_b2"], f["L1_ffn_sb2"])] * 3, axis=0)
    d["F1_gw"], d["F1_gb"] = f["L1_ffn_gate_w"].T, f["L1_ffn_gate_b"]
    d["F1_sel"] = np.concatenate([np.kron(np.eye(L1_E + 1, dtype=np.float32), np.ones((1, L1_H), np.float32))] * 3, axis=0)

    d["desc16"] = np.arange(L2_E, 0, -1).astype(np.float32)
    d["F2_sim"], d["F2_gates"] = f["L2_ffn_sim_matrix"], f["L2_ffn_gates"]
    d["ones"] = np.ones((P, P), np.float32)
    d["tri"] = np.triu(np.full((P, P), NEG, np.float32), 1)
    d["F2_sel"] = np.concatenate([np.kron(np.eye(L2_E, dtype=np.float32), np.ones((1, P), np.float32))] * 3, axis=0)
    for k in "qkvo":
        d["F2_w" + k] = f[f"L2_ffn_{k}_proj"].transpose(1, 0, 2)
    d["F3_w"] = np.stack([rows(f["L3_ffn_w_gate"]).reshape(P, L3_I), rows(f["L3_ffn_w_up"]).reshape(P, L3_I),
                          f["L3_ffn_w_down"]], axis=1)
    return d


def kernel(**inputs):
    import numpy as _np
    import concourse.bacc as _bacc
    from concourse import mybir as _mybir
    from concourse.bass_utils import run_bass_kernel_spmd as _run

    nc = _bacc.Bacc("TRN2", target_bir_lowering=False, num_devices=1)
    arrays, dram = {}, {}
    for name, a in laid_out(inputs).items():
        a = _np.ascontiguousarray(a)
        arrays[f"in_{name}"] = a
        dram[name] = nc.dram_tensor(f"in_{name}", a.shape, _mybir.dt.from_np(a.dtype), kind="ExternalInput").ap()
    out = nc.dram_tensor("out_0", (P, TILES, P), F32, kind="ExternalOutput").ap()
    build(nc, dram, out)
    r = _run(nc, [arrays], core_ids=[0])
    got = r.results[0]["out_0"]
    return _np.ascontiguousarray(got.transpose(1, 0, 2)).reshape(B, S, P)
```

```python
from contextlib import ExitStack

import concourse.bass as bass
from concourse import mybir

F32 = mybir.dt.float32
BF16 = mybir.dt.bfloat16
I32 = mybir.dt.int32
ALU = mybir.AluOpType
ACT = mybir.ActivationFunctionType
AX = mybir.AxisListType

N_SUBLAYERS = 8

P = 128
B, S, SC = 16, 256, 64
TILES = B * S // P
TPI = 4
BPI = 2
ITERS = TILES // TPI
H = 16
PAIRS = H // 2
KEYS = H * SC
EPS = 1e-5
L1_E, L1_H = 8, 176
L1_ALL = (L1_E + 1) * L1_H
L1_CH = -(-L1_ALL // P)
L2_E = 16
L3_I = 384
BLK = 32
NEG = -float(2 ** 100)
MAGIC = 1.5 * 2.0 ** 23


class Signal:
    PRIME = 8

    def __init__(self, sem):
        self.sem, self.base = sem, Signal.PRIME

    def at(self, n):
        return n + self.base


class Steps:

    def __init__(self, eng, sig, i, per_iteration):
        self.eng, self.sig, self.i, self.n, self.k = eng, sig, i, per_iteration, 0

    def done(self, instruction):
        self.k += 1
        instruction.then_inc(self.sig.sem, 1)
        self.eng.wait_ge(self.sig.sem, self.sig.at(self.i * self.n + self.k))

    def end(self):
        assert self.k == self.n, (self.k, self.n)


class Program:

    def __init__(self, nc, ctx):
        self.nc, self.ctx, self.named = nc, ctx, {}

    def sig(self, name):
        if name not in self.named:
            self.named[name] = Signal(self.ctx.enter_context(self.nc.semaphore(name)))
        return self.named[name]

    def end_block(self, counts):
        for name, n in counts.items():
            self.named[name].base += n


SIGNALS = [
    "ln_var", "ln_rstd", "ln_out", "ln_T", "xT_ready", "bias_added", "x_added",
    "ctx_ready", "kv_proj", "kv_ready", "khat_ready", "q_proj", "q_ready", "mask_ready",
    "scores", "shifted", "shifted_T", "probs", "heads_out", "heads_norm", "heads_T", "headsT_ready", "attn_proj",
    "dve_steps", "pool_steps", "act_steps", "weights", "out_stored",
    "z_ready", "gate_logits", "gate_exp", "gate_ready", "gate_T", "gate_parts",
    "hidden", "hidden_b", "hidden_ready", "ffn_out", "ffn_outT", "ffn_outT_ready", "gate_bcast", "hidden_mul", "hidden_act",
    "scaled", "qkv", "qkv_ready", "vT", "v_ready", "maxed", "pT", "pT_ready", "ao", "ao_ready",
    "absmax", "gmax", "quant", "wraw", "routes_kept", "sums_inverted",
]


def load_weights(eng, pr, pairs, count):
    for dst, src in pairs:
        eng.dma_start(dst, src).then_inc(pr.sig("weights").sem, 16)
        count += 16
    return count


def ln_buffers(sb):
    return dict(stats=sb("stats", [P, TPI, 6]), mv=sb("mv", [P, 4, TPI]), mean=sb("mean", [P, TPI]),
                vareps=sb("vareps", [P, TPI]), rstd=sb("rstd", [P, TPI]))


LN_STEPS = 3


def layernorm_vector(pr, dve, steps, i, w, x4, xn):
    nc = pr.nc
    for c in range(TPI):
        ins = nc.vector.bn_stats(w["stats"][:, c, :], x4[:, c, :])
    steps.done(ins)
    st, mv = w["stats"], w["mv"]
    nc.vector.tensor_tensor(mv[:, 0, :], st[:, :, 1], st[:, :, 4], ALU.add)
    nc.vector.scalar_tensor_tensor(mv[:, 2, :], st[:, :, 2], P * EPS, st[:, :, 5], ALU.add, ALU.add)
    steps.done(nc.vector.tensor_tensor(mv[:, 1, :], st[:, :, 1], st[:, :, 4], ALU.subtract))
    nc.vector.tensor_scalar(w["mean"][:], mv[:, 0, :], 0.5, None, ALU.mult)
    steps.done(nc.vector.scalar_tensor_tensor(mv[:, 3, :], mv[:, 1, :], 0.25, mv[:, 1, :], ALU.mult, ALU.mult))
    nc.vector.scalar_tensor_tensor(w["vareps"][:], mv[:, 2, :], 1.0 / P, mv[:, 3, :], ALU.mult, ALU.add)\
        .then_inc(pr.sig("ln_var").sem, 1)


def layernorm_apply(pr, dve, w, x4, xn):
    for c in range(TPI):
        ins = pr.nc.vector.tensor_scalar(xn[:, c, :], x4[:, c, :], w["mean"][:, c:c + 1], w["rstd"][:, c:c + 1],
                                         ALU.subtract, ALU.mult)
    return ins


def layernorm_pool(pr, pool, n, w):
    pool.wait_ge(pr.sig("ln_var").sem, pr.sig("ln_var").at(n))
    pr.nc.gpsimd.tensor_tensor(w["rstd"][:], w["vareps"][:], w["mhalf"][:, 0:TPI], ALU.pow).then_inc(pr.sig("ln_rstd").sem, 1)


def tile4(x_sb, i):
    return x_sb[:, bass.ds(i * TPI, TPI), :]


def context_attention(pr, x_sb, common, dram, layer):
    nc = pr.nc
    first = layer == 0
    masked = layer == 2
    dv = SC if first else P // H
    vw = 2 * (dv + 1)
    with ExitStack() as ctx:
        def sb(name, shape, dt=F32):
            return ctx.enter_context(nc.sbuf_tensor(f"{name}_a{layer}", shape, dt))
        w = dict(common)
        ident, ctxT = common["ident"], common["ctxT"]
        if first:
            wqT = sb("wqT", [P, PAIRS, P])
            wkT = sb("wkT", [P, PAIRS, P])
            wv = sb("wv", [P, H * dv])
            wo = sb("wo", [P, PAIRS, P])
            m = sb("m", [P, H, P])
            loads = [(wqT[:], dram["L0_wqT"]), (wkT[:], dram["L0_wkT"]), (wv[:], dram["L0_wv"]), (wo[:], dram["L0_wo"])]
        else:
            ws = sb("ws", [P, 4, P])
            cols = sb("cols", [P, 3])
            loads = [(ws[:], dram[f"L{layer}_w4"]), (cols[:], dram[f"L{layer}_cols"])]
            wq, wk, wv, wo = (ws[:, k, :] for k in range(4))
        bo = sb("bo", [P, P])
        loads.append((bo[:], dram[f"L{layer}_bo"].partition_broadcast(P)))
        if masked:
            maskf = sb("maskf", [P, TPI, SC], I32)
            maskb = sb("maskb", [P, TPI, SC], BF16)
        cb = sb("cb", [P, BPI, P])
        khat = sb("khat", [P, BPI, H, SC])
        kT = sb("kT", [P, BPI, SC])
        vb = sb("vb", [P, BPI, PAIRS, vw])
        xn = sb("xn", [P, TPI, P])
        xT = sb("xT", [P, TPI, P])
        qT = sb("qT", [P, TPI, P])
        shifted = sb("shifted", [P, TPI, KEYS])
        probs = sb("probs", [P, TPI, KEYS])
        smax = sb("smax", [P, TPI, H])
        rsum = sb("rsum", [P, TPI, H])
        w.update(ln_buffers(sb))
        PS = [ctx.enter_context(nc.psum_tensor(f"ps{c}_a{layer}", [P, 1024], F32)) for c in range(TPI)]
        heads = shifted if first else sb("heads", [P, TPI, P])
        headsT = probs if first else sb("headsT", [P, TPI, P])
        PH = 2 if first else 1
        nload = 16 * len(loads)
        block = ctx.enter_context(nc.Block())
        s = pr.sig

        @block.sync
        def _(sp):
            load_weights(sp, pr, loads, 0)
            if masked:
                with sp.Fori(0, ITERS) as i:
                    sp.wait_ge(s("mask_ready").sem, s("mask_ready").at(i))
                    sp.dma_start(maskf[:], dram["mask"][:, bass.ds(i * TPI, TPI), :]).then_inc(s("wraw").sem, 16)

        @block.gpsimd
        def _(pool):
            nc.gpsimd.memset(vb[:], 0.0).then_inc(s("pool_steps").sem, 1)
            pool.wait_ge(s("pool_steps").sem, s("pool_steps").at(1))
            for par in range(2):
                ins = nc.gpsimd.memset(vb[par * SC:(par + 1) * SC, :, :, par * (dv + 1) + dv:par * (dv + 1) + dv + 1], 1.0)
                ins.then_inc(s("pool_steps").sem, 1)
                pool.wait_ge(s("pool_steps").sem, s("pool_steps").at(2 + par))
            pool.wait_ge(s("weights").sem, s("weights").at(nload))
            with pool.Fori(0, ITERS) as i:
                pool.wait_ge(s("kv_proj").sem, s("kv_proj").at(i))
                ins = nc.gpsimd.tensor_copy(cb[:].rearrange("p b k -> p (b k)"), ctxT[:, bass.ds(i * (BPI * P), BPI * P)])
                ins.then_inc(s("ctx_ready").sem, 1)
                layernorm_pool(pr, pool, i + 1, w)
                if not first:
                    pool.wait_ge(s("kv_ready").sem, s("kv_ready").at(i + 1))
                    pool.wait_ge(s("scores").sem, s("scores").at(i * TPI))
                    for b in range(BPI):
                        ins = nc.gpsimd.tensor_tensor(khat[:, b, :, :], kT[:, b, :].unsqueeze(1).broadcast_to([P, H, SC]),
                                                      common["headmask"][:].unsqueeze(2).broadcast_to([P, H, SC]), ALU.mult)
                    ins.then_inc(s("khat_ready").sem, 1)
                pool.wait_ge(s("ln_out").sem, s("ln_out").at(i + 1))
                x4 = tile4(x_sb, i)
                nc.gpsimd.tensor_tensor(x4, x4, bo[:].unsqueeze(1).broadcast_to([P, TPI, P]), ALU.add)\
                    .then_inc(s("bias_added").sem, 1)

        @block.scalar
        def _(act):
            act.wait_ge(s("weights").sem, s("weights").at(nload))
            act.wait_ge(s("pool_steps").sem, s("pool_steps").at(3))
            if first:
                for j in range(2):
                    act.wait_ge(s("q_proj").sem, s("q_proj").at(j + 1))
                    nc.scalar.activation(m[:, j::2, :], PS[j][:].rearrange("p (h d) -> p h d", h=8), ACT.Copy)\
                        .then_inc(s("q_ready").sem, 1)
            with act.Fori(0, ITERS) as i:
                act.wait_ge(s("kv_proj").sem, s("kv_proj").at(i + 1))
                act.wait_ge(s("heads_out").sem, s("heads_out").at(i * TPI * PH))
                if not first:
                    act.wait_ge(s("khat_ready").sem, s("khat_ready").at(i))
                else:
                    act.wait_ge(s("scores").sem, s("scores").at(i * TPI))
                for b in range(BPI):
                    if first:
                        nc.scalar.activation(khat[:, b, :, :], PS[2 * b][:].rearrange("p (h k) -> p h k", h=H), ACT.Copy)
                        v = PS[2 * b + 1][:].rearrange("p (q a d) -> p q a d", a=2, d=dv)
                    else:
                        nc.scalar.activation(kT[:, b, :], PS[2 * b][:, 0:SC], ACT.Identity, bias=cols[:, 1:2])
                        v = PS[2 * b][:, 512:512 + P].rearrange("p (q a d) -> p q a d", a=2, d=dv)
                    for par in range(2):
                        r = slice(par * SC, (par + 1) * SC)
                        ins = nc.scalar.activation(vb[r, b, :, par * (dv + 1):par * (dv + 1) + dv], v[r, :, par, :], ACT.Copy)
                ins.then_inc(s("kv_ready").sem, 1)
                for c in range(TPI):
                    act.wait_ge(s("ln_T").sem, s("ln_T").at(i * TPI + c + 1))
                    nc.scalar.activation(xT[:, c, :], PS[c][:, 0:P], ACT.Copy).then_inc(s("xT_ready").sem, 1)
                if not first:
                    for c in range(TPI):
                        act.wait_ge(s("q_proj").sem, s("q_proj").at(i * TPI + c + 1))
                        nc.scalar.activation(qT[:, c, :], PS[c][:, 512:512 + P], ACT.Identity, bias=cols[:, 0:1])\
                            .then_inc(s("q_ready").sem, 1)
                for c in range(TPI):
                    act.wait_ge(s("shifted_T").sem, s("shifted_T").at(i * TPI + c + 1))
                    nc.scalar.activation(probs[:, c, :], PS[c][:], ACT.Exp, scale=float(dv) ** -0.5).then_inc(s("probs").sem, 1)
                for c in range(TPI):
                    act.wait_ge(s("heads_T").sem, s("heads_T").at(i * TPI + c + 1))
                    if first:
                        nc.scalar.activation(headsT[:, c, :], PS[c][:], ACT.Copy).then_inc(s("headsT_ready").sem, 1)
                    else:
                        nc.scalar.activation(headsT[:, c, :], PS[c][:, 512:512 + P], ACT.Identity, bias=cols[:, 2:3])\
                            .then_inc(s("headsT_ready").sem, 1)

        @block.tensor
        def _(pe):
            pe.wait_ge(s("weights").sem, s("weights").at(nload))
            if first:
                for h in range(H):
                    r = slice((h % 2) * SC, (h % 2 + 1) * SC)
                    ins = nc.tensor.matmul(PS[h % 2][:, (h // 2) * P:(h // 2 + 1) * P], wkT[r, h // 2, :], wqT[r, h // 2, :],
                                           start=True, stop=True)
                    if h >= H - 2:
                        ins.then_inc(s("q_proj").sem, 1)
                pe.wait_ge(s("q_ready").sem, s("q_ready").at(2))
            with pe.Fori(0, ITERS) as i:
                pe.wait_ge(s("ctx_ready").sem, s("ctx_ready").at(i + 1))
                pe.wait_ge(s("x_added").sem, s("x_added").at(i * TPI))
                for b in range(BPI):
                    if first:
                        for h in range(H):
                            nc.tensor.matmul(PS[2 * b][:, h * SC:(h + 1) * SC], m[:, h, :], cb[:, b, 0:SC], start=True, stop=True)
                        for j in range(2):
                            ins = nc.tensor.matmul(PS[2 * b + 1][:, j * 512:(j + 1) * 512], cb[:, b, :],
                                                   wv[:, j * 512:(j + 1) * 512], start=True, stop=True)
                    else:
                        nc.tensor.matmul(PS[2 * b][:, 0:SC], wk, cb[:, b, 0:SC], start=True, stop=True)
                        ins = nc.tensor.matmul(PS[2 * b][:, 512:512 + P], cb[:, b, :], wv, start=True, stop=True)
                ins.then_inc(s("kv_proj").sem, 1)
                pe.wait_ge(s("kv_ready").sem, s("kv_ready").at(i + 1))
                pe.wait_ge(s("ln_out").sem, s("ln_out").at(i + 1))
                for c in range(TPI):
                    nc.tensor.transpose(PS[c][:, 0:P], xn[:, c, :], ident[:]).then_inc(s("ln_T").sem, 1)
                if not first:
                    for c in range(TPI):
                        pe.wait_ge(s("xT_ready").sem, s("xT_ready").at(i * TPI + c + 1))
                        nc.tensor.matmul(PS[c][:, 512:512 + P], wq, xT[:, c, :], start=True, stop=True).then_inc(s("q_proj").sem, 1)
                    pe.wait_ge(s("khat_ready").sem, s("khat_ready").at(i + 1))
                if masked:
                    pe.wait_ge(s("mask_ready").sem, s("mask_ready").at(i + 1))
                for c in range(TPI):
                    src = xT if first else qT
                    if first:
                        pe.wait_ge(s("xT_ready").sem, s("xT_ready").at(i * TPI + c + 1))
                    else:
                        pe.wait_ge(s("q_ready").sem, s("q_ready").at(i * TPI + c + 1))
                    for j in range(2):
                        out = PS[c][:, j * 512:(j + 1) * 512]
                        if masked:
                            nc.tensor.matmul(out, common["identb"][:], maskb[:, c, :].unsqueeze(1).broadcast_to([P, 8, SC]),
                                             start=True, stop=False)
                        ins = nc.tensor.matmul(out, src[:, c, :], khat[:, c // 2, 8 * j:8 * j + 8, :], start=not masked, stop=True)
                    ins.then_inc(s("scores").sem, 1)
                for c in range(TPI):
                    pe.wait_ge(s("shifted").sem, s("shifted").at(i * TPI + c + 1))
                    for q in range(PAIRS):
                        ins = nc.tensor.transpose(PS[c][:, q * P:(q + 1) * P], shifted[:, c, q * P:(q + 1) * P], ident[:])
                    ins.then_inc(s("shifted_T").sem, 1)
                for ph in range(PH):
                    for c in range(TPI):
                        if ph == 0:
                            pe.wait_ge(s("probs").sem, s("probs").at(i * TPI + c + 1))
                        else:
                            pe.wait_ge(s("heads_norm").sem, s("heads_norm").at((i * PH + ph - 1) * TPI + c + 1))
                        for k in range(PAIRS // PH):
                            q = ph * (PAIRS // PH) + k
                            o = (k // 2) * 512 + (k % 2) * vw if first else k * vw
                            ins = nc.tensor.matmul(PS[c][:, o:o + vw], probs[:, c, q * P:(q + 1) * P], vb[:, c // 2, q, :],
                                                   start=True, stop=True)
                        ins.then_inc(s("heads_out").sem, 1)
                for c in range(TPI):
                    pe.wait_ge(s("heads_norm").sem, s("heads_norm").at((i * PH + PH - 1) * TPI + c + 1))
                    if first:
                        for q in range(PAIRS):
                            ins = nc.tensor.transpose(PS[c][:, q * P:(q + 1) * P], heads[:, c, q * P:(q + 1) * P], ident[:])
                    else:
                        ins = nc.tensor.transpose(PS[c][:, 512:512 + P], heads[:, c, :], ident[:])
                    ins.then_inc(s("heads_T").sem, 1)
                for c in range(TPI):
                    pe.wait_ge(s("headsT_ready").sem, s("headsT_ready").at(i * TPI + c + 1))
                    if first:
                        for q in range(PAIRS):
                            ins = nc.tensor.matmul(PS[c][:, 0:P], headsT[:, c, q * P:(q + 1) * P], wo[:, q, :],
                                                   start=q == 0, stop=q == PAIRS - 1)
                    else:
                        ins = nc.tensor.matmul(PS[c][:, 0:P], headsT[:, c, :], wo, start=True, stop=True)
                    ins.then_inc(s("attn_proj").sem, 1)

        @block.vector
        def _(dve):
            with dve.Fori(0, ITERS) as i:
                steps = Steps(dve, s("dve_steps"), i, LN_STEPS + TPI + TPI * PH)
                x4 = tile4(x_sb, i)
                layernorm_vector(pr, dve, steps, i, w, x4, xn)
                if masked:
                    dve.wait_ge(s("wraw").sem, s("wraw").at((i + 1) * 16))
                    dve.wait_ge(s("scores").sem, s("scores").at(i * TPI))
                    nc.vector.tensor_scalar(maskb[:], maskf[:], 0.0, NEG, ALU.is_equal, ALU.mult).then_inc(s("mask_ready").sem, 1)
                dve.wait_ge(s("ln_rstd").sem, s("ln_rstd").at(i + 1))
                layernorm_apply(pr, dve, w, x4, xn).then_inc(s("ln_out").sem, 1)
                for c in range(TPI):
                    dve.wait_ge(s("scores").sem, s("scores").at(i * TPI + c + 1))
                    sc = PS[c][:].rearrange("p (h k) -> p h k", h=H)
                    steps.done(nc.vector.tensor_reduce(smax[:, c, :], sc, axis=AX.X, op=ALU.max))
                    nc.vector.tensor_tensor(shifted[:, c, :].rearrange("p (h k) -> p h k", h=H), sc,
                                            smax[:, c, :].unsqueeze(2).broadcast_to([P, H, SC]), ALU.subtract)\
                        .then_inc(s("shifted").sem, 1)
                for ph in range(PH):
                    for c in range(TPI):
                        dve.wait_ge(s("heads_out").sem, s("heads_out").at((i * PH + ph) * TPI + c + 1))
                        if first:
                            o = PS[c][:].rearrange("p (g n) -> p g n", g=2)[:, :, 0:2 * vw].rearrange("p g (k d) -> p g k d", d=dv + 1)
                            hs = heads[:, c, ph * 512:(ph + 1) * 512].rearrange("p (g k d) -> p g k d", g=2, d=dv)
                            rs = rsum[:, c, ph * 8:ph * 8 + 8].rearrange("p (g k) -> p g k", g=2)
                            steps.done(nc.vector.reciprocal(rs, o[:, :, :, dv]))
                            ins = nc.vector.tensor_tensor(hs, o[:, :, :, 0:dv], rs.unsqueeze(3).broadcast_to([P, 2, 4, dv]), ALU.mult)
                        else:
                            o = PS[c][:, 0:H * (dv + 1)].rearrange("p (h d) -> p h d", h=H)
                            steps.done(nc.vector.reciprocal(rsum[:, c, :], o[:, :, dv]))
                            ins = nc.vector.tensor_tensor(heads[:, c, :].rearrange("p (h d) -> p h d", h=H), o[:, :, 0:dv],
                                                          rsum[:, c, :].unsqueeze(2).broadcast_to([P, H, dv]), ALU.mult)
                        ins.then_inc(s("heads_norm").sem, 1)
                dve.wait_ge(s("bias_added").sem, s("bias_added").at(i + 1))
                for c in range(TPI):
                    dve.wait_ge(s("attn_proj").sem, s("attn_proj").at(i * TPI + c + 1))
                    xc = x_sb[:, bass.ds(i * TPI + c, 1), :].rearrange("p a d -> p (a d)")
                    nc.vector.tensor_tensor(xc, xc, PS[c][:, 0:P], ALU.add).then_inc(s("x_added").sem, 1)
                steps.end()

    n4, n1 = ITERS * TPI, ITERS
    counts = dict(weights=nload, kv_proj=n1, ctx_ready=n1, ln_var=n1, ln_rstd=n1, kv_ready=n1, ln_out=n1, bias_added=n1,
                  ln_T=n4, xT_ready=n4, scores=n4, shifted=n4, shifted_T=n4, probs=n4, heads_out=n4 * PH, heads_norm=n4 * PH,
                  heads_T=n4, headsT_ready=n4, attn_proj=n4, x_added=n4, pool_steps=3, dve_steps=n1 * (LN_STEPS + TPI + TPI * PH))
    if first:
        counts.update(q_proj=2, q_ready=2)
    else:
        counts.update(khat_ready=n1, q_proj=n4, q_ready=n4)
    if masked:
        counts.update(mask_ready=n1, wraw=16 * n1)
    pr.end_block(counts)


def narrow_attention(pr, x_sb, common, dram, layer):
    nc, s = pr.nc, pr.sig
    masked = layer == 2
    dv = P // H
    vw = 2 * (dv + 1)
    T4 = TPI * P
    with ExitStack() as ctx:
        def sb(name, shape, dt=F32):
            return ctx.enter_context(nc.sbuf_tensor(f"{name}_a{layer}", shape, dt))
        w = dict(common)
        ident, ctxT = common["ident"], common["ctxT"]
        ws, cols, bo = sb("ws", [P, 4, P]), sb("cols", [P, 3]), sb("bo", [P, P])
        loads = [(ws[:], dram[f"L{layer}_w4"]), (cols[:], dram[f"L{layer}_cols"]), (bo[:], dram[f"L{layer}_bo"].partition_broadcast(P))]
        nload = 16 * len(loads)
        wq, wk, wv, wo = (ws[:, k, :] for k in range(4))
        if masked:
            maskf = sb("maskf", [P, TPI, SC], I32)
            maskb = sb("maskb", [P, 2, TPI, SC], BF16)
        cb = sb("cb", [P, BPI, P])
        kT = sb("kT", [P, BPI, SC])
        khat = sb("khat", [P, 2, BPI, H, SC])
        vb = sb("vb", [P, 2, BPI, PAIRS, vw])
        xn, xT, qT = sb("xn", [P, TPI, P]), sb("xT", [P, T4]), sb("qT", [P, 2, T4])
        shifted, probs = sb("shifted", [P, 2, KEYS]), sb("probs", [P, 2, KEYS])
        smax, rsum = sb("smax", [P, 2, H]), sb("rsum", [P, 2, H])
        heads, headsT = sb("heads", [P, 2, P]), sb("headsT", [P, 2, P])
        w.update(ln_buffers(sb))
        psS = [ctx.enter_context(nc.psum_tensor(f"psS{c}_a{layer}", [P, KEYS], F32)) for c in range(2)]
        psF = [ctx.enter_context(nc.psum_tensor(f"psF{c}_a{layer}", [P, T4], F32)) for c in range(2)]
        psC = [ctx.enter_context(nc.psum_tensor(f"psC{c}_a{layer}", [P, T4], F32)) for c in range(2)]
        block = ctx.enter_context(nc.Block())
        BODY = 2 * TPI

        def run_bodies(eng, body):
            body(0, True, False)
            with eng.Fori(1, ITERS // 2 - 1) as i:
                body(i, False, False)
            body(ITERS // 2 - 1, False, True)

        def by_head(ap):
            return ap.rearrange("p (h k) -> p h k", h=H)

        @block.sync
        def _(sp):
            load_weights(sp, pr, loads, 0)
            if masked:
                with sp.Fori(0, ITERS) as i:
                    sp.wait_ge(s("mask_ready").sem, s("mask_ready").at(i))
                    sp.dma_start(maskf[:], dram["mask"][:, bass.ds(i * TPI, TPI), :]).then_inc(s("wraw").sem, 16)

        @block.gpsimd
        def _(pool):
            nc.gpsimd.memset(vb[:], 0.0).then_inc(s("pool_steps").sem, 1)
            pool.wait_ge(s("pool_steps").sem, s("pool_steps").at(1))
            for par in range(2):
                ins = nc.gpsimd.memset(vb[par * SC:(par + 1) * SC, :, :, :, par * (dv + 1) + dv:par * (dv + 1) + dv + 1], 1.0)
                ins.then_inc(s("pool_steps").sem, 1)
                pool.wait_ge(s("pool_steps").sem, s("pool_steps").at(2 + par))
            pool.wait_ge(s("weights").sem, s("weights").at(nload))

            def front(j, q):
                pool.wait_ge(s("kv_proj").sem, s("kv_proj").at(j))
                nc.gpsimd.tensor_copy(cb[:].rearrange("p b k -> p (b k)"), ctxT[:, bass.ds(j * (BPI * P), BPI * P)])\
                    .then_inc(s("ctx_ready").sem, 1)
                layernorm_pool(pr, pool, j + 1, w)
                pool.wait_ge(s("ln_out").sem, s("ln_out").at(j + 1))
                x4 = tile4(x_sb, j)
                nc.gpsimd.tensor_tensor(x4, x4, bo[:].unsqueeze(1).broadcast_to([P, TPI, P]), ALU.add)\
                    .then_inc(s("bias_added").sem, 1)
                pool.wait_ge(s("kv_ready").sem, s("kv_ready").at(j + 1))
                pool.wait_ge(s("scores").sem, s("scores").at((j - 1) * TPI))
                for b in range(BPI):
                    ins = nc.gpsimd.tensor_tensor(khat[:, q, b, :, :], kT[:, b, :].unsqueeze(1).broadcast_to([P, H, SC]),
                                                  common["headmask"][:].unsqueeze(2).broadcast_to([P, H, SC]), ALU.mult)
                ins.then_inc(s("khat_ready").sem, 1)
            with pool.Fori(0, ITERS // 2) as i:
                front(2 * i, 0)
                front(2 * i + 1, 1)

        @block.scalar
        def _(act):
            act.wait_ge(s("weights").sem, s("weights").at(nload))
            act.wait_ge(s("pool_steps").sem, s("pool_steps").at(3))

            def front_kv(j, q):
                act.wait_ge(s("kv_proj").sem, s("kv_proj").at(j + 1))
                act.wait_ge(s("khat_ready").sem, s("khat_ready").at(j))
                act.wait_ge(s("heads_out").sem, s("heads_out").at((j - 1) * TPI))
                for b in range(BPI):
                    nc.scalar.activation(kT[:, b, :], psF[1][:, 2 * b * P:2 * b * P + SC], ACT.Identity, bias=cols[:, 1:2])
                    v = psF[1][:, (2 * b + 1) * P:(2 * b + 2) * P].rearrange("p (q a d) -> p q a d", a=2, d=dv)
                    for par in range(2):
                        r = slice(par * SC, (par + 1) * SC)
                        ins = nc.scalar.activation(vb[r, q, b, :, par * (dv + 1):par * (dv + 1) + dv], v[r, :, par, :], ACT.Copy)
                ins.then_inc(s("kv_ready").sem, 1)

            def front_x(j):
                act.wait_ge(s("ln_T").sem, s("ln_T").at(j + 1))
                nc.scalar.activation(xT[:], psF[0][:], ACT.Copy).then_inc(s("xT_ready").sem, 1)

            def front_q(j, q):
                act.wait_ge(s("q_proj").sem, s("q_proj").at(j + 1))
                act.wait_ge(s("scores").sem, s("scores").at((j - 1) * TPI))
                nc.scalar.activation(qT[:, q, :], psF[1][:], ACT.Identity, bias=cols[:, 0:1]).then_inc(s("q_ready").sem, 1)

            def exp(n, g):
                act.wait_ge(s("shifted_T").sem, s("shifted_T").at(n + 1))
                act.wait_ge(s("heads_out").sem, s("heads_out").at(n - 1))
                nc.scalar.activation(probs[:, g % 2, :], psS[g % 2][:], ACT.Exp, scale=float(dv) ** -0.5)\
                    .then_inc(s("probs").sem, 1)

            def store_heads(n, g):
                act.wait_ge(s("heads_T").sem, s("heads_T").at(n + 1))
                nc.scalar.activation(headsT[:, g % 2, :], psC[g % 2][:, 256:256 + P], ACT.Identity, bias=cols[:, 2:3])\
                    .then_inc(s("headsT_ready").sem, 1)

            def body(i, first, last):
                for g in range(BODY):
                    n, c, p = i * BODY + g, g % TPI, g // TPI
                    j = 2 * i + p
                    exp(n, g)
                    if not (last and p):
                        if c == 0:
                            front_kv(j + 1, 1 - p)
                            front_x(j + 1)
                        elif c == 1:
                            front_q(j + 1, 1 - p)
                    if g or not first:
                        store_heads(n - 1, g - 1)
            front_kv(0, 0)
            front_x(0)
            front_q(0, 0)
            run_bodies(act, body)
            store_heads(TILES - 1, TILES - 1)

        @block.tensor
        def _(pe):
            pe.wait_ge(s("weights").sem, s("weights").at(nload))

            def front_kv(j):
                pe.wait_ge(s("ctx_ready").sem, s("ctx_ready").at(j + 1))
                pe.wait_ge(s("q_ready").sem, s("q_ready").at(j))
                for b in range(BPI):
                    nc.tensor.matmul(psF[1][:, 2 * b * P:2 * b * P + SC], wk, cb[:, b, 0:SC], start=True, stop=True)
                    ins = nc.tensor.matmul(psF[1][:, (2 * b + 1) * P:(2 * b + 2) * P], cb[:, b, :], wv, start=True, stop=True)
                ins.then_inc(s("kv_proj").sem, 1)

            def front_x(j):
                pe.wait_ge(s("xT_ready").sem, s("xT_ready").at(j))
                pe.wait_ge(s("ln_out").sem, s("ln_out").at(j + 1))
                for c in range(TPI):
                    ins = nc.tensor.transpose(psF[0][:, c * P:(c + 1) * P], xn[:, c, :], ident[:])
                ins.then_inc(s("ln_T").sem, 1)

            def front_q(j):
                pe.wait_ge(s("kv_ready").sem, s("kv_ready").at(j + 1))
                pe.wait_ge(s("xT_ready").sem, s("xT_ready").at(j + 1))
                nc.tensor.matmul(psF[1][:], wq, xT[:], start=True, stop=True).then_inc(s("q_proj").sem, 1)

            def scores(n, g):
                c, p = g % TPI, g // TPI % 2
                pe.wait_ge(s("probs").sem, s("probs").at(n - 1))
                for h in range(2):
                    out = psS[g % 2][:, h * 512:(h + 1) * 512]
                    if masked:
                        nc.tensor.matmul(out, common["identb"][:], maskb[:, p, c, :].unsqueeze(1).broadcast_to([P, 8, SC]),
                                         start=True, stop=False)
                    ins = nc.tensor.matmul(out, qT[:, p, c * P:(c + 1) * P], khat[:, p, c // 2, 8 * h:8 * h + 8, :],
                                           start=not masked, stop=True)
                ins.then_inc(s("scores").sem, 1)

            def front_done(j):
                pe.wait_ge(s("q_ready").sem, s("q_ready").at(j + 1))
                pe.wait_ge(s("khat_ready").sem, s("khat_ready").at(j + 1))
                if masked:
                    pe.wait_ge(s("mask_ready").sem, s("mask_ready").at(j + 1))

            def shifted_T(n, g):
                pe.wait_ge(s("shifted").sem, s("shifted").at(n + 1))
                for k in range(PAIRS):
                    ins = nc.tensor.transpose(psS[g % 2][:, k * P:(k + 1) * P], shifted[:, g % 2, k * P:(k + 1) * P], ident[:])
                ins.then_inc(s("shifted_T").sem, 1)

            def heads_out(n, g):
                pe.wait_ge(s("probs").sem, s("probs").at(n + 1))
                pe.wait_ge(s("x_added").sem, s("x_added").at(n - 1))
                for k in range(PAIRS):
                    ins = nc.tensor.matmul(psC[g % 2][:, k * vw:(k + 1) * vw], probs[:, g % 2, k * P:(k + 1) * P],
                                           vb[:, g // TPI, g % TPI // 2, k, :], start=True, stop=True)
                ins.then_inc(s("heads_out").sem, 1)

            def heads_T(n, g):
                pe.wait_ge(s("heads_norm").sem, s("heads_norm").at(n + 1))
                nc.tensor.transpose(psC[g % 2][:, 256:256 + P], heads[:, g % 2, :], ident[:]).then_inc(s("heads_T").sem, 1)

            def project(n, g):
                pe.wait_ge(s("headsT_ready").sem, s("headsT_ready").at(n + 1))
                nc.tensor.matmul(psC[g % 2][:, 384:384 + P], headsT[:, g % 2, :], wo, start=True, stop=True)\
                    .then_inc(s("attn_proj").sem, 1)

            def body(i, first, last):
                for g in range(BODY):
                    n, c, p = i * BODY + g, g % TPI, g // TPI
                    j = 2 * i + p
                    front = not (last and p)
                    shifted_T(n, g)
                    if g > 1 or not first:
                        project(n - 2, g - 2)
                    if g or not first:
                        heads_out(n - 1, (g - 1) % BODY)
                    if front and c == 0:
                        front_kv(j + 1)
                        front_x(j + 1)
                    if front and c == 1:
                        front_q(j + 1)
                    if front and c == 2:
                        front_done(j + 1)
                    if front or c < 2:
                        scores(n + 2, (g + 2) % BODY)
                    if g or not first:
                        heads_T(n - 1, g - 1)
            front_kv(0)
            front_x(0)
            front_q(0)
            front_done(0)
            scores(0, 0)
            scores(1, 1)
            run_bodies(pe, body)
            n = TILES - 1
            project(n - 1, n - 1)
            heads_out(n, n % BODY)
            heads_T(n, n)
            project(n, n)

        @block.vector
        def _(dve):
            def front_ln(j):
                steps = Steps(dve, s("dve_steps"), j, LN_STEPS)
                layernorm_vector(pr, dve, steps, j, w, tile4(x_sb, j), xn)
                steps.end()

            def front_mask(j, q):
                dve.wait_ge(s("wraw").sem, s("wraw").at((j + 1) * 16))
                dve.wait_ge(s("scores").sem, s("scores").at((j - 1) * TPI))
                nc.vector.tensor_scalar(maskb[:, q, :, :], maskf[:], 0.0, NEG, ALU.is_equal, ALU.mult)\
                    .then_inc(s("mask_ready").sem, 1)

            def front_xn(j):
                dve.wait_ge(s("ln_rstd").sem, s("ln_rstd").at(j + 1))
                dve.wait_ge(s("ln_T").sem, s("ln_T").at(j))
                layernorm_apply(pr, dve, w, tile4(x_sb, j), xn).then_inc(s("ln_out").sem, 1)

            def largest(n, g):
                dve.wait_ge(s("scores").sem, s("scores").at(n + 1))
                nc.vector.tensor_reduce(smax[:, g % 2, :], by_head(psS[g % 2][:]), axis=AX.X, op=ALU.max)\
                    .then_inc(s("maxed").sem, 1)

            def shift(n, g):
                dve.wait_ge(s("maxed").sem, s("maxed").at(n + 1))
                dve.wait_ge(s("shifted_T").sem, s("shifted_T").at(n - 1))
                nc.vector.tensor_tensor(by_head(shifted[:, g % 2, :]), by_head(psS[g % 2][:]),
                                        smax[:, g % 2, :].unsqueeze(2).broadcast_to([P, H, SC]), ALU.subtract)\
                    .then_inc(s("shifted").sem, 1)

            def normalise(n, g):
                dve.wait_ge(s("heads_out").sem, s("heads_out").at(n + 1))
                o = psC[g % 2][:, 0:H * (dv + 1)].rearrange("p (h d) -> p h d", h=H)
                nc.vector.reciprocal(rsum[:, g % 2, :], o[:, :, dv]).then_inc(s("sums_inverted").sem, 1)
                dve.wait_ge(s("sums_inverted").sem, s("sums_inverted").at(n + 1))
                nc.vector.tensor_tensor(heads[:, g % 2, :].rearrange("p (h d) -> p h d", h=H), o[:, :, 0:dv],
                                        rsum[:, g % 2, :].unsqueeze(2).broadcast_to([P, H, dv]), ALU.mult)\
                    .then_inc(s("heads_norm").sem, 1)

            def add(n, g):
                dve.wait_ge(s("attn_proj").sem, s("attn_proj").at(n + 1))
                xc = x_sb[:, bass.ds(n, 1), :].rearrange("p a d -> p (a d)")
                nc.vector.tensor_tensor(xc, xc, psC[g % 2][:, 384:384 + P], ALU.add).then_inc(s("x_added").sem, 1)

            def body(i, first, last):
                for g in range(BODY):
                    n, c, p = i * BODY + g, g % TPI, g // TPI
                    j = 2 * i + p
                    if not (last and g == BODY - 1):
                        largest(n + 1, g + 1)
                    if g > 1 or not first:
                        if c == 2:
                            dve.wait_ge(s("bias_added").sem, s("bias_added").at(j + 1))
                        add(n - 2, g - 2)
                    if not (last and g == BODY - 1):
                        shift(n + 1, g + 1)
                    if g or not first:
                        normalise(n - 1, g - 1)
                    if masked and c == 0 and not (last and p):
                        front_mask(j + 1, 1 - p)
                    if not last and c == 2:
                        front_ln(j + 2)
                    if not last and c == 3:
                        front_xn(j + 2)
            for j in range(2):
                front_ln(j)
                if masked and not j:
                    front_mask(0, 0)
                front_xn(j)
            largest(0, 0)
            shift(0, 0)
            run_bodies(dve, body)
            n = TILES - 1
            add(n - 1, n - 1)
            normalise(n, n)
            add(n, n)

    n4, n1 = ITERS * TPI, ITERS
    counts = dict(weights=nload, kv_proj=n1, ctx_ready=n1, ln_var=n1, ln_rstd=n1, kv_ready=n1, ln_out=n1, bias_added=n1,
                  ln_T=n1, xT_ready=n1, q_proj=n1, q_ready=n1, khat_ready=n1, scores=n4, maxed=n4, shifted=n4, shifted_T=n4,
                  probs=n4, heads_out=n4, sums_inverted=n4, heads_norm=n4, heads_T=n4, headsT_ready=n4, attn_proj=n4,
                  x_added=n4, pool_steps=3, dve_steps=n1 * LN_STEPS)
    if masked:
        counts.update(mask_ready=n1, wraw=16 * n1)
    pr.end_block(counts)


def first_max(nc, steps, src, onehot, top, scratch, desc):
    shape = list(src.shape)
    steps.done(nc.vector.tensor_reduce(top, src, axis=AX.X, op=ALU.max))
    steps.done(nc.vector.tensor_tensor(scratch, src, top.unsqueeze(2).broadcast_to(shape), ALU.is_equal))
    steps.done(nc.vector.tensor_tensor(scratch, scratch, desc.unsqueeze(1).broadcast_to(shape), ALU.mult))
    steps.done(nc.vector.tensor_reduce(top, scratch, axis=AX.X, op=ALU.max))
    steps.done(nc.vector.tensor_tensor(onehot, desc.unsqueeze(1).broadcast_to(shape), top.unsqueeze(2).broadcast_to(shape),
                                       ALU.is_equal))


def three_parts(nc, steps, src, parts, hi, rest, mid, n):
    steps.done(nc.vector.tensor_copy(hi, src))
    nc.vector.tensor_copy(parts[:, :, 0:n], hi)
    steps.done(nc.vector.tensor_tensor(rest, src, hi, ALU.subtract))
    steps.done(nc.vector.tensor_copy(mid, rest))
    nc.vector.tensor_copy(parts[:, :, n:2 * n], mid)
    return nc.vector.tensor_tensor(parts[:, :, 2 * n:3 * n], rest, mid, ALU.subtract)


def xc_of(x_sb, i, c):
    return x_sb[:, bass.ds(i * TPI + c, 1), :].rearrange("p a d -> p (a d)")


def layer0_ffn(pr, x_sb, common, dram):
    nc, s = pr.nc, pr.sig
    E, CH = 8, 4
    with ExitStack() as ctx:
        def sb(name, shape, dt=F32):
            return ctx.enter_context(nc.sbuf_tensor(f"{name}_f0", shape, dt))
        w = dict(common)
        ident = common["ident"]
        wd, wu = sb("wd", [P, CH * P]), sb("wu", [P, CH, P])
        wr, br = sb("wr", [P, E]), sb("br", [P, E])
        bup, cols, desc = sb("bup", [E, P]), sb("cols", [P, 6 + CH]), sb("desc", [P, E])
        loads = [(wd[:], dram["F0_wd"]), (wu[:], dram["F0_wu"]), (wr[:], dram["F0_wr"]), (cols[:], dram["F0_cols"]),
                 (bup[:], dram["F0_bup"]), (br[:], dram["F0_br"].partition_broadcast(P)),
                 (desc[:], dram["desc8"].partition_broadcast(P))]
        nload = 16 * len(loads)
        bn = sb("bn", [P, 4])
        xn, zh, zT = sb("xn", [P, TPI, P]), sb("zh", [P, TPI, P]), sb("zT", [P, TPI, P])
        zsum, zs, zbn = sb("zsum", [P, TPI]), sb("zs", [P, BPI]), sb("zbn", [P, BPI, P])
        lg, ex, oh, tmp = (sb(n, [P, BPI, E]) for n in ("lg", "ex", "oh", "tmp"))
        top, gsum, gate = (sb(n, [P, BPI]) for n in ("top", "gsum", "gate"))
        sel, bsel = sb("sel", [P, BPI, CH]), sb("bsel", [P, BPI, CH])
        gd, gdb = sb("gd", [E, BPI]), sb("gdb", [E, BPI, P])
        hT = sb("hT", [P, BPI, CH, BPI * P])
        w.update(ln_buffers(sb))
        PS = [ctx.enter_context(nc.psum_tensor(f"ps{c}_f0", [P, 1024], F32)) for c in range(TPI)]
        NST = 2 * LN_STEPS + 1 + 1 + 2 + 2 + 5 + 1 + 1 + 1 + 1
        SETUP = 4
        block = ctx.enter_context(nc.Block())

        @block.sync
        def _(sp):
            load_weights(sp, pr, loads, 0)

        @block.gpsimd
        def _(pool):
            pool.wait_ge(s("act_steps").sem, s("act_steps").at(1))
            nc.gpsimd.tensor_tensor(bn[:, 1:2], bn[:, 0:1], common["mhalf"][:, 0:1], ALU.pow).then_inc(s("pool_steps").sem, 1)
            with pool.Fori(0, ITERS) as i:
                layernorm_pool(pr, pool, 2 * i + 1, w)
                layernorm_pool(pr, pool, 2 * i + 2, w)

        @block.scalar
        def _(act):
            act.wait_ge(s("weights").sem, s("weights").at(nload))
            nc.scalar.activation(bn[:, 0:1], cols[:, 0:1], ACT.Copy, bias=EPS).then_inc(s("act_steps").sem, 1)
            with act.Fori(0, ITERS) as i:
                act.wait_ge(s("hidden").sem, s("hidden").at(i * BPI))
                for c in range(TPI):
                    act.wait_ge(s("ln_T").sem, s("ln_T").at(i * TPI + c + 1))
                    nc.scalar.activation(zT[:, c, :], PS[c][:, 0:P], ACT.Identity, scale=cols[:, 4:5], bias=cols[:, 5:6],
                                         accum_out=zsum[:, c:c + 1]).then_inc(s("z_ready").sem, 1)
                act.wait_ge(s("gate_logits").sem, s("gate_logits").at(2 * i + 2))
                nc.scalar.activation(ex[:], lg[:], ACT.Exp).then_inc(s("gate_exp").sem, 1)
                act.wait_ge(s("gate_ready").sem, s("gate_ready").at(i + 1))
                for b in range(BPI):
                    act.wait_ge(s("hidden").sem, s("hidden").at(i * BPI + b + 1))
                    for j in range(CH):
                        ins = nc.scalar.activation(hT[:, b, j, :], PS[2 * b][:, j * BPI * P:(j + 1) * BPI * P], ACT.Relu,
                                                   scale=sel[:, b, j:j + 1], bias=bsel[:, b, j:j + 1])
                    ins.then_inc(s("hidden_ready").sem, 1)

        @block.tensor
        def _(pe):
            pe.wait_ge(s("weights").sem, s("weights").at(nload))
            with pe.Fori(0, ITERS) as i:
                pe.wait_ge(s("x_added").sem, s("x_added").at(i * TPI))
                pe.wait_ge(s("ln_out").sem, s("ln_out").at(i + 1))
                for c in range(TPI):
                    nc.tensor.transpose(PS[c][:, 0:P], zh[:, c, :], ident[:]).then_inc(s("ln_T").sem, 1)
                pe.wait_ge(s("scaled").sem, s("scaled").at(i + 1))
                for b in range(BPI):
                    ins = nc.tensor.matmul(PS[0][:, 512 + b * E:512 + (b + 1) * E], zbn[:, b, :], wr[:], start=True, stop=True)
                ins.then_inc(s("gate_logits").sem, 1)
                pe.wait_ge(s("gate_ready").sem, s("gate_ready").at(i + 1))
                for b in range(BPI):
                    for j in range(CH):
                        ins = nc.tensor.matmul(PS[2 * b][:, j * BPI * P:(j + 1) * BPI * P], wd[:, j * P:(j + 1) * P],
                                               zT[:, 2 * b:2 * b + 2, :], start=True, stop=True)
                    ins.then_inc(s("hidden").sem, 1)
                for b in range(BPI):
                    pe.wait_ge(s("hidden_ready").sem, s("hidden_ready").at(i * BPI + b + 1))
                    for t in range(2):
                        out = PS[2 * b + 1][:, t * 512:t * 512 + P]
                        for j in range(CH):
                            nc.tensor.matmul(out, hT[:, b, j, t * P:(t + 1) * P], wu[:, j, :], start=j == 0, stop=False)
                        nc.tensor.matmul(out, gdb[:, b, :], bup[:], start=False, stop=True).then_inc(s("ffn_out").sem, 1)

        @block.vector
        def _(dve):
            setup = Steps(dve, s("dve_steps"), 0, SETUP)
            dve.wait_ge(s("weights").sem, s("weights").at(nload))
            dve.wait_ge(s("pool_steps").sem, s("pool_steps").at(1))
            setup.done(nc.vector.tensor_tensor(bn[:, 1:2], bn[:, 1:2], cols[:, 1:2], ALU.mult))
            setup.done(nc.vector.tensor_scalar(bn[:, 2:3], bn[:, 1:2], 1.0 / S, None, ALU.mult))
            setup.done(nc.vector.tensor_tensor(bn[:, 3:4], bn[:, 1:2], cols[:, 3:4], ALU.mult))
            setup.done(nc.vector.tensor_tensor(bn[:, 3:4], cols[:, 2:3], bn[:, 3:4], ALU.subtract))
            setup.end()
            with dve.Fori(0, ITERS) as i:
                steps = Steps(dve, s("dve_steps"), i, NST)
                steps.k = SETUP
                x4 = tile4(x_sb, i)
                layernorm_vector(pr, dve, steps, i, w, x4, xn)
                dve.wait_ge(s("ln_rstd").sem, s("ln_rstd").at(2 * i + 1))
                steps.done(layernorm_apply(pr, dve, w, x4, xn))
                layernorm_vector(pr, dve, steps, i, w, xn, zh)
                dve.wait_ge(s("ln_rstd").sem, s("ln_rstd").at(2 * i + 2))
                layernorm_apply(pr, dve, w, xn, zh).then_inc(s("ln_out").sem, 1)
                dve.wait_ge(s("z_ready").sem, s("z_ready").at(i * TPI + TPI))
                z2 = zsum[:].rearrange("p (b t) -> p b t", t=2)
                steps.done(nc.vector.tensor_tensor(zs[:], z2[:, :, 0], z2[:, :, 1], ALU.add))
                nc.vector.tensor_scalar(zbn[:], zs[:].unsqueeze(2).broadcast_to([P, BPI, P]), bn[:, 2:3], bn[:, 3:4],
                                        ALU.mult, ALU.add).then_inc(s("scaled").sem, 1)
                dve.wait_ge(s("gate_logits").sem, s("gate_logits").at(2 * i + 1))
                lps = PS[0][:, 512:512 + BPI * E].rearrange("p (b e) -> p b e", e=E)
                steps.done(nc.vector.tensor_tensor(lg[:], lps, br[:].unsqueeze(1).broadcast_to([P, BPI, E]), ALU.add))
                steps.done(nc.vector.tensor_reduce(top[:], lg[:], axis=AX.X, op=ALU.max))
                nc.vector.tensor_tensor(lg[:], lg[:], top[:].unsqueeze(2).broadcast_to([P, BPI, E]), ALU.subtract)\
                    .then_inc(s("gate_logits").sem, 1)
                dve.wait_ge(s("gate_logits").sem, s("gate_logits").at(2 * i + 2))
                dve.wait_ge(s("gate_exp").sem, s("gate_exp").at(i + 1))
                steps.done(nc.vector.tensor_reduce(gsum[:], ex[:], axis=AX.X, op=ALU.add))
                steps.done(nc.vector.reciprocal(gate[:], gsum[:]))
                first_max(nc, steps, lg[:], oh[:], top[:], tmp[:], desc[:])
                steps.done(nc.vector.tensor_tensor(oh[:], oh[:], gate[:].unsqueeze(2).broadcast_to([P, BPI, E]), ALU.mult))
                ohp = oh[:].rearrange("p b (j a) -> p b j a", a=2)
                dve.wait_ge(s("hidden_ready").sem, s("hidden_ready").at(i * BPI))
                dve.wait_ge(s("ffn_out").sem, s("ffn_out").at(i * TPI))
                nc.vector.tensor_copy(sel[0:64, :, :], ohp[0:64, :, :, 0])
                nc.vector.tensor_tensor(tmp[0:E, :, :], oh[0:E, :, :], ident[0:E, 0:E].unsqueeze(1).broadcast_to([E, BPI, E]), ALU.mult)
                steps.done(nc.vector.tensor_copy(sel[64:128, :, :], ohp[64:128, :, :, 1]))
                steps.done(nc.vector.tensor_reduce(gd[:], tmp[0:E, :, :], axis=AX.X, op=ALU.add))
                steps.done(nc.vector.tensor_copy(gdb[:], gd[:].unsqueeze(2).broadcast_to([E, BPI, P])))
                nc.vector.tensor_tensor(bsel[:], sel[:], cols[:, 6:6 + CH].unsqueeze(1).broadcast_to([P, BPI, CH]), ALU.mult)\
                    .then_inc(s("gate_ready").sem, 1)
                for c in range(TPI):
                    dve.wait_ge(s("ffn_out").sem, s("ffn_out").at(i * TPI + c + 1))
                    xc = xc_of(x_sb, i, c)
                    nc.vector.tensor_tensor(xc, xc, PS[c - c % 2 + 1][:, (c % 2) * 512:(c % 2) * 512 + P], ALU.add)\
                        .then_inc(s("x_added").sem, 1)
                steps.n += SETUP
                steps.end()

    n1, n4 = ITERS, ITERS * TPI
    pr.end_block(dict(weights=nload, act_steps=1, pool_steps=1, dve_steps=SETUP + NST * n1, ln_var=2 * n1, ln_rstd=2 * n1,
                      ln_out=n1, ln_T=n4, z_ready=n4, scaled=n1, gate_logits=2 * n1, gate_exp=n1, gate_ready=n1,
                      hidden=n1 * BPI, hidden_ready=n1 * BPI, ffn_out=n4, x_added=n4))


def layer1_ffn(pr, x_sb, common, dram):
    nc, s = pr.nc, pr.sig
    E, NE, CH = L1_E, L1_E + 1, L1_CH
    T4 = TPI * P
    with ExitStack() as ctx:
        def sb(name, shape, dt=F32):
            return ctx.enter_context(nc.sbuf_tensor(f"{name}_f1", shape, dt))
        w = dict(common)
        ident = common["ident"]
        w1, w3, w2 = sb("w1", [P, L1_ALL]), sb("w3", [P, L1_ALL]), sb("w2", [P, CH, P])
        cols, gw, gb, desc = sb("cols", [P, 2 * CH]), sb("gw", [P, E]), sb("gb", [P, E]), sb("desc", [P, E])
        b2, self32, selb = sb("b2", [3 * NE, P]), sb("self32", [3 * NE, L1_ALL]), sb("selb", [3 * NE, L1_ALL], BF16)
        loads = [(gw[:], dram["F1_gw"]), (gb[:], dram["F1_gb"].partition_broadcast(P)), (desc[:], dram["desc8"].partition_broadcast(P)),
                 (cols[:], dram["F1_cols"]), (b2[:], dram["F1_b2"]), (self32[:], dram["F1_sel"]),
                 (w1[:], dram["F1_w1"]), (w3[:], dram["F1_w3"]), (w2[:], dram["F1_w2"])]
        nload = 16 * len(loads)
        xn, xT = sb("xn", [P, TPI, P]), sb("xT", [P, 2, T4])
        lg, ex, bi, oh, oh2, tmp = (sb(n, [P, TPI, E]) for n in ("lg", "ex", "bi", "oh", "oh2", "tmp"))
        top, gs = sb("top", [P, TPI]), sb("gs", [P, TPI])
        rw, rest = sb("rw", [P, TPI, NE]), sb("rest", [P, TPI, NE])
        hi, mid = sb("hi", [P, TPI, NE], BF16), sb("mid", [P, TPI, NE], BF16)
        parts = sb("parts", [P, TPI, 3 * NE])
        rwT, rwTb = sb("rwT", [3 * NE, 2, T4]), sb("rwTb", [3 * NE, 2, T4], BF16)
        t3, g_, act_h, h = (sb(n, [P, 2, T4]) for n in ("t3", "g", "act_h", "h"))
        oT = sb("oT", [P, T4])
        w.update(ln_buffers(sb))
        psU = [ctx.enter_context(nc.psum_tensor(f"psU{k}_f1", [P, 2, T4], F32)) for k in range(2)]
        psR = [ctx.enter_context(nc.psum_tensor(f"psR{k}_f1", [P, T4], F32)) for k in range(2)]
        psO = ctx.enter_context(nc.psum_tensor("psO_f1", [P, T4], F32))
        psM = ctx.enter_context(nc.psum_tensor("psM_f1", [P, T4], F32))
        NST = LN_STEPS + 1 + 1 + 1 + 1 + 1 + 5 + 1 + 5 + 1 + 1 + 3
        rows = [min(P, L1_ALL - k * P) for k in range(CH)]
        block = ctx.enter_context(nc.Block())

        BODY = 2 * CH

        def run_bodies(eng, body):
            with eng.Fori(0, ITERS // 2 - 1) as i:
                body(i, False)
            body(ITERS // 2 - 1, True)

        @block.sync
        def _(sp):
            load_weights(sp, pr, loads, 0)

        @block.gpsimd
        def _(pool):
            pool.wait_ge(s("weights").sem, s("weights").at(nload))
            nc.gpsimd.tensor_copy(selb[:], self32[:]).then_inc(s("pool_steps").sem, 1)
            pool.wait_ge(s("pool_steps").sem, s("pool_steps").at(1))
            nc.gpsimd.memset(rw[:], 1.0).then_inc(s("pool_steps").sem, 1)
            with pool.Fori(0, ITERS) as i:
                layernorm_pool(pr, pool, i + 1, w)

        @block.scalar
        def _(act):
            act.wait_ge(s("weights").sem, s("weights").at(nload))

            def front_x(j, q):
                act.wait_ge(s("ln_T").sem, s("ln_T").at(j + 1))
                nc.scalar.activation(xT[:, q, :], psM[:], ACT.Copy).then_inc(s("xT_ready").sem, 1)

            def front_exp(j):
                act.wait_ge(s("gate_logits").sem, s("gate_logits").at(2 * j + 2))
                nc.scalar.activation(ex[:], lg[:], ACT.Exp).then_inc(s("gate_exp").sem, 1)

            def front_parts(j, q):
                act.wait_ge(s("gate_T").sem, s("gate_T").at(j + 1))
                nc.scalar.activation(rwT[:, q, :], psM[0:3 * NE, :], ACT.Copy)
                nc.scalar.activation(rwTb[:, q, :], psM[0:3 * NE, :], ACT.Copy).then_inc(s("gate_parts").sem, 1)

            def bias(n, g):
                r = slice(0, rows[g % CH])
                act.wait_ge(s("hidden").sem, s("hidden").at(n + 1))
                nc.scalar.activation(t3[r, g % 2, :], psU[g % 2][r, 1, :], ACT.Identity, bias=cols[r, CH + g % CH:CH + g % CH + 1])\
                    .then_inc(s("hidden_b").sem, 1)

            def silu(n, g):
                r = slice(0, rows[g % CH])
                act.wait_ge(s("hidden_mul").sem, s("hidden_mul").at(n + 1))
                nc.scalar.activation(act_h[r, g % 2, :], g_[r, g % 2, :], ACT.Silu).then_inc(s("hidden_act").sem, 1)

            def body(i, last):
                for p in range(2):
                    j = 2 * i + p
                    for k in range(CH):
                        g = p * CH + k
                        bias(i * BODY + g, g)
                        if k:
                            silu(i * BODY + g - 1, g - 1)
                        if not (last and p):
                            if k == 2:
                                front_x(j + 1, 1 - p)
                            if k == 4:
                                front_exp(j + 1)
                            if k == 11:
                                front_parts(j + 1, 1 - p)
                    silu(i * BODY + g, g)
                    act.wait_ge(s("ffn_out").sem, s("ffn_out").at(j + 1))
                    act.wait_ge(s("ffn_outT_ready").sem, s("ffn_outT_ready").at(j))
                    nc.scalar.activation(oT[:], psO[:], ACT.Copy).then_inc(s("ffn_outT").sem, 1)
            front_x(0, 0)
            front_exp(0)
            front_parts(0, 0)
            run_bodies(act, body)

        @block.tensor
        def _(pe):
            pe.wait_ge(s("weights").sem, s("weights").at(nload))
            pe.wait_ge(s("pool_steps").sem, s("pool_steps").at(2))

            def front_x(j, added):
                if added is not None:
                    pe.wait_ge(s("x_added").sem, s("x_added").at(added * TPI))
                pe.wait_ge(s("ln_out").sem, s("ln_out").at(j + 1))
                for c in range(TPI):
                    ins = nc.tensor.transpose(psM[:, c * P:(c + 1) * P], xn[:, c, :], ident[:])
                ins.then_inc(s("ln_T").sem, 1)

            def front_logits(j, q):
                pe.wait_ge(s("xT_ready").sem, s("xT_ready").at(j + 1))
                for c in range(TPI):
                    ins = nc.tensor.matmul(psM[:, c * E:(c + 1) * E], xT[:, q, c * P:(c + 1) * P], gw[:], start=True, stop=True)
                ins.then_inc(s("gate_logits").sem, 1)

            def front_parts(j):
                pe.wait_ge(s("gate_ready").sem, s("gate_ready").at(j + 1))
                for c in range(TPI):
                    ins = nc.tensor.transpose(psM[0:3 * NE, c * P:(c + 1) * P], parts[:, c, :], ident[:])
                ins.then_inc(s("gate_T").sem, 1)

            def up(n, g):
                k, q = g % CH, g // CH % 2
                cs, r = slice(k * P, k * P + rows[k]), slice(0, rows[k])
                pe.wait_ge(s("hidden_mul").sem, s("hidden_mul").at(n - 1))
                nc.tensor.matmul(psU[g % 2][r, 1, :], w3[:, cs], xT[:, q, :], start=True, stop=True)
                nc.tensor.matmul(psU[g % 2][r, 0, :], w1[:, cs], xT[:, q, :], start=True, stop=True).then_inc(s("hidden").sem, 1)

            def spread(n, g):
                k, q = g % CH, g // CH
                pe.wait_ge(s("hidden_ready").sem, s("hidden_ready").at(n - 1))
                nc.tensor.matmul(psR[g % 2][0:rows[k], :], selb[:, k * P:k * P + rows[k]], rwTb[:, q, :], start=True, stop=True)\
                    .then_inc(s("gate_bcast").sem, 1)

            def down(n, g, j):
                k, q = g % CH, g // CH
                if k == 0:
                    pe.wait_ge(s("ffn_outT").sem, s("ffn_outT").at(j))
                    nc.tensor.matmul(psO[:], b2[:], rwT[:, q, :], start=True, stop=False)
                pe.wait_ge(s("hidden_ready").sem, s("hidden_ready").at(n + 1))
                ins = nc.tensor.matmul(psO[:], w2[0:rows[k], k, :], h[0:rows[k], g % 2, :], start=False, stop=k == CH - 1)
                if k == CH - 1:
                    ins.then_inc(s("ffn_out").sem, 1)

            def out_T(j):
                pe.wait_ge(s("ffn_outT").sem, s("ffn_outT").at(j + 1))
                pe.wait_ge(s("gate_parts").sem, s("gate_parts").at(min(j + 2, ITERS) if isinstance(j, int) else j + 2))
                for c in range(TPI):
                    ins = nc.tensor.transpose(psM[:, c * P:(c + 1) * P], oT[:, c * P:(c + 1) * P], ident[:])
                ins.then_inc(s("ffn_outT_ready").sem, 1)

            def body(i, last):
                for p in range(2):
                    j = 2 * i + p
                    for k in range(CH):
                        g = p * CH + k
                        n = i * BODY + g
                        if not (last and g == BODY - 1):
                            if g == BODY - 1:
                                pe.wait_ge(s("xT_ready").sem, s("xT_ready").at(j + 2))
                            up(n + 1, (g + 1) % BODY)
                        if not (last and p):
                            if k == 2:
                                front_x(j + 1, j)
                            if k == 4:
                                front_logits(j + 1, 1 - p)
                            if k == 11:
                                front_parts(j + 1)
                        spread(n, g)
                        if k:
                            down(n - 1, g - 1, j)
                    down(n, g, j)
                    out_T(j)
            front_x(0, None)
            front_logits(0, 0)
            up(0, 0)
            front_parts(0)
            pe.wait_ge(s("gate_parts").sem, s("gate_parts").at(1))
            run_bodies(pe, body)

        @block.vector
        def _(dve):
            dve.wait_ge(s("weights").sem, s("weights").at(nload))
            dve.wait_ge(s("pool_steps").sem, s("pool_steps").at(2))
            g4 = [P, TPI, E]

            def front_steps(j, k0):
                st = Steps(dve, s("dve_steps"), j, NST)
                st.k = k0
                return st

            def front_ln(j):
                steps = front_steps(j, 0)
                layernorm_vector(pr, dve, steps, j, w, tile4(x_sb, j), xn)
                return steps

            def front_xn(j):
                dve.wait_ge(s("ln_rstd").sem, s("ln_rstd").at(j + 1))
                layernorm_apply(pr, dve, w, tile4(x_sb, j), xn).then_inc(s("ln_out").sem, 1)

            def front_shift(j, steps):
                dve.wait_ge(s("gate_logits").sem, s("gate_logits").at(2 * j + 1))
                lps = psM[:, 0:TPI * E].rearrange("p (c e) -> p c e", e=E)
                steps.done(nc.vector.tensor_reduce(top[:], lps, axis=AX.X, op=ALU.max))
                nc.vector.tensor_tensor(lg[:], lps, top[:].unsqueeze(2).broadcast_to(g4), ALU.subtract)\
                    .then_inc(s("gate_logits").sem, 1)

            def front_scores(j, steps):
                dve.wait_ge(s("gate_exp").sem, s("gate_exp").at(j + 1))
                steps.done(nc.vector.tensor_reduce(gs[:], ex[:], axis=AX.X, op=ALU.add))
                steps.done(nc.vector.reciprocal(gs[:], gs[:]))
                steps.done(nc.vector.tensor_tensor(ex[:], ex[:], gs[:].unsqueeze(2).broadcast_to(g4), ALU.mult))
                steps.done(nc.vector.tensor_tensor(bi[:], ex[:], gb[:].unsqueeze(1).broadcast_to(g4), ALU.add))

            def front_best(steps):
                first_max(nc, steps, bi[:], oh[:], top[:], tmp[:], desc[:])

            def front_second(steps):
                steps.done(nc.vector.scalar_tensor_tensor(bi[:], oh[:], -1e30, bi[:], ALU.mult, ALU.add))
                first_max(nc, steps, bi[:], oh2[:], top[:], tmp[:], desc[:])

            def front_parts(steps):
                steps.done(nc.vector.tensor_tensor(oh[:], oh[:], oh2[:], ALU.add))
                steps.done(nc.vector.tensor_tensor(rw[:, :, 0:E], oh[:], ex[:], ALU.mult))
                three_parts(nc, steps, rw[:], parts[:], hi[:], rest[:], mid[:], NE).then_inc(s("gate_ready").sem, 1)
                steps.end()

            def multiply(n, g):
                k = g % CH
                r = slice(0, rows[k])
                dve.wait_ge(s("hidden_b").sem, s("hidden_b").at(n + 1))
                nc.vector.scalar_tensor_tensor(g_[r, g % 2, :], psU[g % 2][r, 0, :], cols[r, k:k + 1], t3[r, g % 2, :],
                                               ALU.add, ALU.mult).then_inc(s("hidden_mul").sem, 1)

            def weigh(n, g):
                r = slice(0, rows[g % CH])
                dve.wait_ge(s("hidden_act").sem, s("hidden_act").at(n + 1))
                dve.wait_ge(s("gate_bcast").sem, s("gate_bcast").at(n + 1))
                nc.vector.tensor_tensor(h[r, g % 2, :], act_h[r, g % 2, :], psR[g % 2][r, :], ALU.mult)\
                    .then_inc(s("hidden_ready").sem, 1)

            def body(i, last):
                for p in range(2):
                    j = 2 * i + p
                    front = not (last and p)
                    for k in range(CH):
                        g = p * CH + k
                        n = i * BODY + g
                        multiply(n, g)
                        if k:
                            weigh(n - 1, g - 1)
                        if front:
                            if k == 0:
                                steps = front_ln(j + 1)
                            elif k == 1:
                                front_xn(j + 1)
                            elif k == 4:
                                front_shift(j + 1, steps)
                            elif k == 6:
                                front_scores(j + 1, steps)
                            elif k == 7:
                                front_best(steps)
                            elif k == 8:
                                front_second(steps)
                            elif k == 9:
                                front_parts(steps)
                    weigh(n, g)
                    dve.wait_ge(s("ffn_outT_ready").sem, s("ffn_outT_ready").at(j + 1))
                    x4 = tile4(x_sb, j)
                    nc.vector.tensor_tensor(x4, x4, psM[:].rearrange("p (c d) -> p c d", d=P), ALU.add)\
                        .then_inc(s("x_added").sem, TPI)
            steps = front_ln(0)
            front_xn(0)
            front_shift(0, steps)
            front_scores(0, steps)
            front_best(steps)
            front_second(steps)
            front_parts(steps)
            run_bodies(dve, body)

    n1, n4 = ITERS, ITERS * TPI
    pr.end_block(dict(weights=nload, pool_steps=2, dve_steps=NST * n1, ln_var=n1, ln_rstd=n1, ln_out=n1, ln_T=n1, xT_ready=n1,
                      gate_logits=2 * n1, gate_exp=n1, gate_ready=n1, gate_T=n1, gate_parts=n1, hidden=n1 * CH, hidden_b=n1 * CH,
                      hidden_mul=n1 * CH, hidden_act=n1 * CH, hidden_ready=n1 * CH, gate_bcast=n1 * CH, ffn_out=n1, ffn_outT=n1,
                      ffn_outT_ready=n1, x_added=n4))


def layer2_ffn(pr, x_sb, common, dram):
    nc, s = pr.nc, pr.sig
    E = L2_E
    T4 = TPI * P
    with ExitStack() as ctx:
        def sb(name, shape, dt=F32):
            return ctx.enter_context(nc.sbuf_tensor(f"{name}_f2", shape, dt))
        w = dict(common)
        ident = common["ident"]
        wq, wk, wv, wo = (sb(n, [P, E, P]) for n in ("wq", "wk", "wv", "wo"))
        sim, simsq, ones, sg = sb("sim", [P, E]), sb("simsq", [P, E]), sb("ones", [P, P]), sb("sg", [P, E])
        simn = sb("simn", [P, 2, E])
        tri32, tri = sb("tri32", [P, P]), sb("tri", [P, P], BF16)
        desc = sb("desc", [P, E])
        self32, selb = sb("self32", [3 * E, E * P]), sb("selb", [3 * E, E * P], BF16)
        loads = [(sim[:], dram["F2_sim"]), (sg[:], dram["F2_gates"].partition_broadcast(P)), (desc[:], dram["desc16"].partition_broadcast(P)),
                 (ones[:], dram["ones"]), (tri32[:], dram["tri"]), (self32[:], dram["F2_sel"]),
                 (wq[:], dram["F2_wq"]), (wk[:], dram["F2_wk"]), (wv[:], dram["F2_wv"]), (wo[:], dram["F2_wo"])]
        nload = 16 * len(loads)
        xn, xT = sb("xn", [P, TPI, P]), sb("xT", [P, 2, T4])
        sq, ssq, rn = sb("sq", [P, TPI, P]), sb("ssq", [P, TPI]), sb("rn", [P, TPI])
        lg, ex, gated, oh, oh2, tmp, mask, rest = (sb(n, [P, TPI, E]) for n in ("lg", "ex", "gated", "oh", "oh2", "tmp", "mask", "rest"))
        top, gs, inact = sb("top", [P, TPI]), sb("gs", [P, TPI]), sb("inact", [P, TPI])
        hi, mid = sb("hi", [P, TPI, E], BF16), sb("mid", [P, TPI, E], BF16)
        parts, rwTb = sb("parts", [P, TPI, P]), sb("rwTb", [3 * E, 2, T4], BF16)
        rwTo = sb("rwTo", [3 * E, T4], BF16)
        xs = sb("xs", [P, 2, T4])
        qkvT = sb("qkvT", [P, 3, T4])
        v = sb("v", [P, TPI, P])
        nmax, rs = sb("nmax", [P, TPI]), sb("rs", [P, TPI])
        p, pT = sb("p", [P, TPI, S]), sb("pT", [P, TPI, S])
        aoT, oT = sb("aoT", [P, 2, T4]), sb("oT", [P, T4])
        w.update(ln_buffers(sb))
        psR = [ctx.enter_context(nc.psum_tensor(f"psR{k}_f2", [P, T4], F32)) for k in range(2)]
        psQKV = [ctx.enter_context(nc.psum_tensor(f"psQ{k}_f2", [P, T4], F32)) for k in range(3)]
        psM = ctx.enter_context(nc.psum_tensor("psM_f2", [P, T4], F32))
        psX = ctx.enter_context(nc.psum_tensor("psX_f2", [P, T4], F32))
        psY = ctx.enter_context(nc.psum_tensor("psY_f2", [P, T4], F32))
        psA = psQKV + [psY]
        NST = LN_STEPS + 1 + 1 + 2 + 5 + 1 + 5 + 1 + 1 + 1 + 1 + 1 + 1 + 1 + 3
        block = ctx.enter_context(nc.Block())

        def qn(j, e):
            return e if isinstance(j, int) and j == 0 else 2 * E * j - E + e

        def on(j, e):
            return 2 * E * j + e - (E if isinstance(j, int) and j == ITERS else 0)

        def run_mains(eng, main):
            main(0, 0)
            main(1, 1)
            with eng.Fori(1, ITERS // 2 - 1) as i:
                main(2 * i, 0)
                main(2 * i + 1, 1)
            main(ITERS - 2, 0)
            main(ITERS - 1, 1)

        def is_first(j, n):
            return isinstance(j, int) and j < n

        def is_last(j):
            return isinstance(j, int) and j == ITERS - 1

        @block.sync
        def _(sp):
            load_weights(sp, pr, loads, 0)

        @block.gpsimd
        def _(pool):
            pool.wait_ge(s("weights").sem, s("weights").at(nload))
            nc.gpsimd.tensor_copy(selb[:], self32[:]).then_inc(s("pool_steps").sem, 1)
            pool.wait_ge(s("pool_steps").sem, s("pool_steps").at(1))
            nc.gpsimd.tensor_copy(tri[:], tri32[:])
            nc.gpsimd.memset(parts[:], 0.0).then_inc(s("pool_steps").sem, 1)
            pool.wait_ge(s("gate_ready").sem, s("gate_ready").at(1))
            nc.gpsimd.tensor_tensor(simn[:, 1, :], simn[:, 0, :], common["mhalf"][:, 0:E], ALU.pow)\
                .then_inc(s("pool_steps").sem, 1)

            def front(j):
                layernorm_pool(pr, pool, j + 1, w)
                pool.wait_ge(s("quant").sem, s("quant").at(j + 1))
                nc.gpsimd.tensor_tensor(rn[:], ssq[:], common["mhalf"][:, 0:TPI], ALU.pow).then_inc(s("pool_steps").sem, 1)

            def keep_routes(j, q):
                pool.wait_ge(s("gate_bcast").sem, s("gate_bcast").at(2 * E * j + E))
                pool.wait_ge(s("gate_parts").sem, s("gate_parts").at(j + 1))
                nc.gpsimd.tensor_tensor(rwTo[:].rearrange("e (c t) -> e c t", t=P), rwTb[:, q, :].rearrange("e (c t) -> e c t", t=P),
                                        ones[0:3 * E, :].unsqueeze(1).broadcast_to([3 * E, TPI, P]), ALU.mult)\
                    .then_inc(s("routes_kept").sem, 1)

            def main(j, q):
                if not is_last(j):
                    front(j + 1)
                keep_routes(j, q)
            front(0)
            run_mains(pool, main)

        @block.scalar
        def _(act):
            act.wait_ge(s("weights").sem, s("weights").at(nload))
            nc.scalar.activation(simsq[:], sim[:], ACT.Square).then_inc(s("act_steps").sem, 1)
            nc.scalar.activation(sg[:], sg[:], ACT.Exp, scale=-1.0).then_inc(s("act_steps").sem, 1)

            def front(j, q):
                act.wait_ge(s("ln_out").sem, s("ln_out").at(j + 1))
                for c in range(TPI):
                    ins = nc.scalar.activation(sq[:, c, :], xn[:, c, :], ACT.Square, accum_out=ssq[:, c:c + 1])
                ins.then_inc(s("absmax").sem, 1)
                act.wait_ge(s("ln_T").sem, s("ln_T").at(j + 1))
                nc.scalar.activation(xT[:, q, :], psM[:], ACT.Copy).then_inc(s("xT_ready").sem, 1)
                act.wait_ge(s("gate_exp").sem, s("gate_exp").at(2 * j + 1))
                nc.scalar.activation(ex[:], lg[:], ACT.Exp).then_inc(s("gate_exp").sem, 1)
                act.wait_ge(s("gate_T").sem, s("gate_T").at(j + 1))
                if not is_first(j, 2):
                    act.wait_ge(s("routes_kept").sem, s("routes_kept").at(j - 1))
                nc.scalar.activation(rwTb[:, q, :], psM[0:3 * E, :], ACT.Copy).then_inc(s("gate_parts").sem, 1)

            def store_o(j):
                act.wait_ge(s("hidden").sem, s("hidden").at(on(j, E)))
                act.wait_ge(s("ffn_outT_ready").sem, s("ffn_outT_ready").at(j - 1))
                nc.scalar.activation(oT[:], psX[:], ACT.Copy).then_inc(s("ffn_outT").sem, 1)

            def main(j, q):
                if not is_last(j):
                    front(j + 1, 1 - q)
                act.wait_ge(s("hidden").sem, s("hidden").at(qn(j, E)))
                nc.scalar.activation(qkvT[:, 0, :], psQKV[0][:], ACT.Copy, scale=float(P) ** -0.5)
                nc.scalar.activation(qkvT[:, 1, :], psQKV[1][:], ACT.Copy).then_inc(s("qkv_ready").sem, 1)
                nc.scalar.activation(qkvT[:, 2, :], psQKV[2][:], ACT.Copy).then_inc(s("qkv_ready").sem, 1)
                for c in range(TPI):
                    nk = P * (c % 2 + 1)
                    act.wait_ge(s("maxed").sem, s("maxed").at(j * TPI + c + 1))
                    nc.scalar.activation(p[:, c, 0:nk], psA[c][:, 0:nk], ACT.Exp, bias=nmax[:, c:c + 1],
                                         accum_out=rs[:, c:c + 1]).then_inc(s("probs").sem, 1)
                act.wait_ge(s("vT").sem, s("vT").at(j + 1))
                nc.scalar.activation(v[:].rearrange("p c d -> p (c d)"), psM[:], ACT.Copy).then_inc(s("v_ready").sem, 1)
                for c in range(TPI):
                    nk = P * (c % 2 + 1)
                    act.wait_ge(s("pT").sem, s("pT").at(j * TPI + c + 1))
                    nc.scalar.activation(pT[:, c, 0:nk], psA[c][:, S:S + nk], ACT.Copy).then_inc(s("pT_ready").sem, 1)
                act.wait_ge(s("ao").sem, s("ao").at(j + 1))
                nc.scalar.activation(aoT[:, q, :], psM[:], ACT.Copy).then_inc(s("ao_ready").sem, 1)
                if not is_first(j, 1):
                    store_o(j)
            front(0, 0)
            run_mains(act, main)
            store_o(ITERS)

        @block.tensor
        def _(pe):
            pe.wait_ge(s("weights").sem, s("weights").at(nload))
            pe.wait_ge(s("pool_steps").sem, s("pool_steps").at(2))
            pe.wait_ge(s("act_steps").sem, s("act_steps").at(1))
            nc.tensor.matmul(psM[:, 0:E], ones[:], simsq[:], start=True, stop=True).then_inc(s("gate_logits").sem, 1)
            pe.wait_ge(s("gate_ready").sem, s("gate_ready").at(2))

            def front_x(j):
                pe.wait_ge(s("ln_out").sem, s("ln_out").at(j + 1))
                for c in range(TPI):
                    ins = nc.tensor.transpose(psM[:, c * P:(c + 1) * P], xn[:, c, :], ident[:])
                ins.then_inc(s("ln_T").sem, 1)

            def front_logits(j, q):
                pe.wait_ge(s("xT_ready").sem, s("xT_ready").at(j + 1))
                for c in range(TPI):
                    ins = nc.tensor.matmul(psM[:, c * E:(c + 1) * E], xT[:, q, c * P:(c + 1) * P], simn[:, 0, :], start=True, stop=True)
                ins.then_inc(s("gate_logits").sem, 1)

            def front_parts(j):
                pe.wait_ge(s("gate_ready").sem, s("gate_ready").at(j + 3))
                for c in range(TPI):
                    ins = nc.tensor.transpose(psM[:, c * P:(c + 1) * P], parts[:, c, :], ident[:])
                ins.then_inc(s("gate_T").sem, 1)

            def out_T(j):
                pe.wait_ge(s("ffn_outT").sem, s("ffn_outT").at(j + 1))
                for c in range(TPI):
                    ins = nc.tensor.transpose(psM[:, c * P:(c + 1) * P], oT[:, c * P:(c + 1) * P], ident[:])
                ins.then_inc(s("ffn_outT_ready").sem, 1)

            def spread(n, e, weights):
                pe.wait_ge(s("scaled").sem, s("scaled").at(n - 1))
                nc.tensor.matmul(psR[e % 2][:], selb[:, e * P:(e + 1) * P], weights, start=True, stop=True)\
                    .then_inc(s("gate_bcast").sem, 1)

            def v_to_tokens(j):
                pe.wait_ge(s("qkv_ready").sem, s("qkv_ready").at(2 * j + 2))
                for c in range(TPI):
                    ins = nc.tensor.transpose(psM[:, c * P:(c + 1) * P], qkvT[:, 2, c * P:(c + 1) * P], ident[:])
                ins.then_inc(s("vT").sem, 1)

            def scores(j):
                pe.wait_ge(s("qkv_ready").sem, s("qkv_ready").at(2 * j + 2))
                for c in range(TPI):
                    t, b = c % 2, c // 2
                    nk = P * (t + 1)
                    nc.tensor.matmul(psA[c][:, 0:nk], qkvT[:, 0, c * P:(c + 1) * P], qkvT[:, 1, b * S:b * S + nk], start=True, stop=False)
                    nc.tensor.matmul(psA[c][:, t * P:nk], common["identb"][:], tri[:], start=False, stop=True).then_inc(s("scores").sem, 1)

            def probs_T(j, c):
                pe.wait_ge(s("heads_norm").sem, s("heads_norm").at(j * TPI + c + 1))
                for k in range(c % 2 + 1):
                    ins = nc.tensor.transpose(psA[c][:, S + k * P:S + (k + 1) * P], p[:, c, k * P:(k + 1) * P], ident[:])
                ins.then_inc(s("pT").sem, 1)

            def attend(j):
                pe.wait_ge(s("v_ready").sem, s("v_ready").at(j + 1))
                for c in range(TPI):
                    pe.wait_ge(s("pT_ready").sem, s("pT_ready").at(j * TPI + c + 1))
                    for k in range(c % 2 + 1):
                        ins = nc.tensor.matmul(psM[:, c * P:(c + 1) * P], v[:, c - c % 2 + k, :], pT[:, c, k * P:(k + 1) * P],
                                               start=k == 0, stop=k == c % 2)
                ins.then_inc(s("ao").sem, 1)

            def mix_o(j, attention):
                pe.wait_ge(s("routes_kept").sem, s("routes_kept").at(j))
                spread(on(j, 0), 0, rwTo[:])
                pe.wait_ge(s("ffn_outT").sem, s("ffn_outT").at(j - 1))
                for e in range(E):
                    if e + 1 < E:
                        spread(on(j, e + 1), e + 1, rwTo[:])
                    if e in attention:
                        attention[e]()
                    pe.wait_ge(s("scaled").sem, s("scaled").at(on(j, e + 1)))
                    nc.tensor.matmul(psX[:], wo[:, e, :], xs[:, e % 2, :], start=e == 0, stop=e == E - 1)\
                        .then_inc(s("hidden").sem, 1)

            def main(j, q):
                pe.wait_ge(s("gate_parts").sem, s("gate_parts").at(j + 1))
                spread(qn(j, 0), 0, rwTb[:, q, :])
                for e in range(E):
                    if e + 1 < E:
                        spread(qn(j, e + 1), e + 1, rwTb[:, q, :])
                    if e == 0:
                        pe.wait_ge(s("pT_ready").sem, s("pT_ready").at(j * TPI))
                    pe.wait_ge(s("scaled").sem, s("scaled").at(qn(j, e + 1)))
                    for n, wt in enumerate((wq, wk, wv)):
                        ins = nc.tensor.matmul(psQKV[n][:], wt[:, e, :], xs[:, e % 2, :], start=e == 0, stop=e == E - 1)
                    ins.then_inc(s("hidden").sem, 1)
                    if e == 0:
                        pe.wait_ge(s("ao_ready").sem, s("ao_ready").at(j))
                        if not is_first(j, 2):
                            out_T(j - 2)
                    if not is_last(j):
                        if e == 2:
                            if not is_first(j, 2):
                                pe.wait_ge(s("x_added").sem, s("x_added").at((j - 1) * TPI))
                            front_x(j + 1)
                        elif e == 4:
                            front_logits(j + 1, 1 - q)
                        elif e == 12:
                            front_parts(j + 1)
                if is_last(j):
                    pe.wait_ge(s("x_added").sem, s("x_added").at((j - 1) * TPI))
                else:
                    pe.wait_ge(s("gate_parts").sem, s("gate_parts").at(j + 2))
                stages = {0: lambda: scores(j), 1: lambda: v_to_tokens(j), 4: lambda: (probs_T(j, 0), probs_T(j, 1)),
                          6: lambda: (probs_T(j, 2), probs_T(j, 3)), 8: lambda: attend(j)}
                if is_first(j, 1):
                    for stage in stages.values():
                        stage()
                else:
                    mix_o(j, stages)
            front_x(0)
            front_logits(0, 0)
            front_parts(0)
            run_mains(pe, main)
            pe.wait_ge(s("ao_ready").sem, s("ao_ready").at(ITERS))
            out_T(ITERS - 2)
            mix_o(ITERS, {})
            pe.wait_ge(s("x_added").sem, s("x_added").at((ITERS - 1) * TPI))
            out_T(ITERS - 1)

        @block.vector
        def _(dve):
            setup = Steps(dve, s("dve_steps"), 0, 2)
            dve.wait_ge(s("weights").sem, s("weights").at(nload))
            dve.wait_ge(s("gate_logits").sem, s("gate_logits").at(1))
            nc.vector.tensor_scalar(simn[:, 0, :], psM[:, 0:E], 1e-12, None, ALU.add).then_inc(s("gate_ready").sem, 1)
            dve.wait_ge(s("pool_steps").sem, s("pool_steps").at(3))
            nc.vector.tensor_tensor(simn[:, 0, :], sim[:], simn[:, 1, :], ALU.mult).then_inc(s("gate_ready").sem, 1)
            dve.wait_ge(s("act_steps").sem, s("act_steps").at(2))
            setup.done(nc.vector.tensor_scalar(sg[:], sg[:], 1.0, None, ALU.add))
            setup.done(nc.vector.reciprocal(sg[:], sg[:]))
            setup.end()
            g4 = [P, TPI, E]

            def front_ln(j):
                steps = Steps(dve, s("dve_steps"), j, NST)
                steps.k = 2
                layernorm_vector(pr, dve, steps, j, w, tile4(x_sb, j), xn)
                return steps

            def front_xn(j):
                dve.wait_ge(s("ln_rstd").sem, s("ln_rstd").at(j + 1))
                layernorm_apply(pr, dve, w, tile4(x_sb, j), xn).then_inc(s("ln_out").sem, 1)

            def front_norm(j):
                dve.wait_ge(s("absmax").sem, s("absmax").at(j + 1))
                nc.vector.tensor_scalar(ssq[:], ssq[:], 1e-12, None, ALU.add).then_inc(s("quant").sem, 1)

            def front_gate(j, steps):
                dve.wait_ge(s("pool_steps").sem, s("pool_steps").at(4 + j))
                dve.wait_ge(s("gate_logits").sem, s("gate_logits").at(j + 2))
                lps = psM[:, 0:TPI * E].rearrange("p (c e) -> p c e", e=E)
                steps.done(nc.vector.tensor_tensor(lg[:], lps, rn[:].unsqueeze(2).broadcast_to(g4), ALU.mult))
                steps.done(nc.vector.tensor_tensor(lg[:], lg[:], sg[:].unsqueeze(1).broadcast_to(g4), ALU.subtract))
                nc.vector.tensor_scalar(gated[:], lg[:], 0.0, None, ALU.max)
                nc.vector.tensor_scalar(mask[:], lg[:], 0.0, None, ALU.is_gt)

            def front_best(steps):
                first_max(nc, steps, lg[:], oh[:], gs[:], tmp[:], desc[:])

            def front_second(steps):
                steps.done(nc.vector.tensor_reduce(top[:], gated[:], axis=AX.X, op=ALU.max))
                steps.done(nc.vector.tensor_scalar(inact[:], top[:], 0.0, None, ALU.is_le))
                steps.done(nc.vector.scalar_tensor_tensor(lg[:], oh[:], -1e30, lg[:], ALU.mult, ALU.add))
                first_max(nc, steps, lg[:], oh2[:], gs[:], tmp[:], desc[:])

            def front_mask(steps):
                nc.vector.tensor_tensor(lg[:], gated[:], top[:].unsqueeze(2).broadcast_to(g4), ALU.subtract)\
                    .then_inc(s("gate_exp").sem, 1)
                steps.done(nc.vector.tensor_tensor(oh[:], oh[:], oh2[:], ALU.add))
                steps.done(nc.vector.tensor_tensor(oh[:], oh[:], inact[:].unsqueeze(2).broadcast_to(g4), ALU.mult))
                steps.done(nc.vector.tensor_tensor(mask[:], mask[:], oh[:], ALU.add))

            def front_weights(j, steps):
                dve.wait_ge(s("gate_exp").sem, s("gate_exp").at(2 * j + 2))
                steps.done(nc.vector.tensor_tensor(ex[:], ex[:], mask[:], ALU.mult))
                steps.done(nc.vector.tensor_reduce(gs[:], ex[:], axis=AX.X, op=ALU.add))
                steps.done(nc.vector.reciprocal(gs[:], gs[:]))
                steps.done(nc.vector.tensor_tensor(ex[:], ex[:], gs[:].unsqueeze(2).broadcast_to(g4), ALU.mult))

            def front_parts(steps):
                three_parts(nc, steps, ex[:], parts[:], hi[:], rest[:], mid[:], E).then_inc(s("gate_ready").sem, 1)
                steps.n += 2
                steps.end()

            def scale_by(n, e, src):
                dve.wait_ge(s("gate_bcast").sem, s("gate_bcast").at(n + 1))
                dve.wait_ge(s("hidden").sem, s("hidden").at(n - 1))
                nc.vector.tensor_tensor(xs[:, e % 2, :], src, psR[e % 2][:], ALU.mult).then_inc(s("scaled").sem, 1)

            def maxima(j):
                for c in range(TPI):
                    nk = P * (c % 2 + 1)
                    dve.wait_ge(s("scores").sem, s("scores").at(j * TPI + c + 1))
                    nc.vector.tensor_reduce(nmax[:, c:c + 1], psA[c][:, 0:nk], axis=AX.X, op=ALU.max, negate=True)\
                        .then_inc(s("maxed").sem, 1)

            def normalise(j, c):
                nk = P * (c % 2 + 1)
                dve.wait_ge(s("probs").sem, s("probs").at(j * TPI + c + 1))
                nc.vector.reciprocal(rs[:, c:c + 1], rs[:, c:c + 1]).then_inc(s("sums_inverted").sem, 1)
                dve.wait_ge(s("sums_inverted").sem, s("sums_inverted").at(j * TPI + c + 1))
                nc.vector.tensor_scalar(p[:, c, 0:nk], p[:, c, 0:nk], rs[:, c:c + 1], None, ALU.mult)\
                    .then_inc(s("heads_norm").sem, 1)

            def add(j):
                dve.wait_ge(s("ffn_outT_ready").sem, s("ffn_outT_ready").at(j + 1))
                x4 = tile4(x_sb, j)
                nc.vector.tensor_tensor(x4, x4, psM[:].rearrange("p (c d) -> p c d", d=P), ALU.add)\
                    .then_inc(s("x_added").sem, TPI)

            def mix_o(j, q, attention):
                dve.wait_ge(s("ao_ready").sem, s("ao_ready").at(j))
                for e in range(E):
                    scale_by(on(j, e), e, aoT[:, q, :])
                    if e in attention:
                        attention[e]()

            def main(j, q):
                for e in range(E):
                    scale_by(qn(j, e), e, xT[:, q, :])
                    if e == 1 and not is_first(j, 2):
                        add(j - 2)
                    if not is_last(j):
                        if e == 0:
                            steps = front_ln(j + 1)
                        elif e == 1:
                            front_xn(j + 1)
                        elif e == 3:
                            front_norm(j + 1)
                        elif e == 5:
                            front_gate(j + 1, steps)
                        elif e == 6:
                            front_best(steps)
                        elif e == 7:
                            front_second(steps)
                        elif e == 8:
                            front_mask(steps)
                        elif e == 9:
                            front_weights(j + 1, steps)
                        elif e == 10:
                            front_parts(steps)
                stages = {0: lambda: maxima(j), 2: lambda: (normalise(j, 0), normalise(j, 1)),
                          4: lambda: (normalise(j, 2), normalise(j, 3))}
                if is_first(j, 1):
                    for stage in stages.values():
                        stage()
                else:
                    mix_o(j, 1 - q, stages)
            steps = front_ln(0)
            front_xn(0)
            front_norm(0)
            front_gate(0, steps)
            front_best(steps)
            front_second(steps)
            front_mask(steps)
            front_weights(0, steps)
            front_parts(steps)
            run_mains(dve, main)
            add(ITERS - 2)
            mix_o(ITERS, 1, {})
            add(ITERS - 1)

    n1, n4 = ITERS, ITERS * TPI
    pr.end_block(dict(weights=nload, pool_steps=3 + n1, act_steps=2, dve_steps=2 + NST * n1, ln_var=n1, ln_rstd=n1, ln_out=n1,
                      ln_T=n1, xT_ready=n1, gate_logits=n1 + 1, gate_ready=n1 + 2, gate_exp=2 * n1, gate_T=n1, gate_parts=n1,
                      absmax=n1, quant=n1, gate_bcast=2 * E * n1, scaled=2 * E * n1, hidden=2 * E * n1,
                      routes_kept=n1, sums_inverted=n4,
                      qkv_ready=2 * n1, vT=n1, v_ready=n1, scores=n4, maxed=n4, probs=n4, heads_norm=n4, pT=n4, pT_ready=n4,
                      ao=n1, ao_ready=n1, ffn_outT=n1, ffn_outT_ready=n1, x_added=n4))


def rows_in_steps(eng, rows, depth, step):
    for r in range(depth):
        step(r, r)
    with eng.Fori(1, rows // depth) as i:
        for k in range(depth):
            step(i * depth + k, k)
    for r in range(rows, rows + depth):
        step(r, r - rows)


def has(r, rows):
    return not isinstance(r, int) or 0 <= r < rows


def layer3_ffn(pr, x_sb, common, dram):
    nc, s = pr.nc, pr.sig
    T4 = TPI * P
    NI = L3_I // P
    ROWS = ITERS * NI
    QMAX = 32767.0
    with ExitStack() as ctx:
        def sb(name, shape, dt=F32):
            return ctx.enter_context(nc.sbuf_tensor(f"{name}_f3", shape, dt))
        ident = common["ident"]
        up, gt = sb("up", [P, NI, ITERS, T4]), sb("gt", [P, NI, ITERS, T4])
        wraw = sb("wraw", [P, 3, L3_I])
        wT = sb("wT", [P, 3, L3_I])
        ws, wi = sb("ws", [P, 3, L3_I // BLK]), sb("wi", [P, 3, L3_I // BLK])
        loads = [(wraw[:], dram["F3_w"])]
        xT = sb("xT", [P, ITERS, T4])
        xq = sb("xq", [P, 2, NI, T4])
        gq, sig, uq = xT[:, 0:4, :], xT[:, 4:8, :], xq[:].rearrange("p a n t -> p (a n) t")[:, 0:4, :]
        am = sb("am", [P, 5, ROWS])
        amr, gm = sb("amr", [P, 5]), sb("gm", [P, 5])
        scale, inv, fac = sb("scale", [P, 5]), sb("inv", [P, 5]), sb("fac", [P, 5])
        magic = sb("magic", [P, 2])
        stats, mv = sb("stats", [P, TILES, 6]), sb("mv", [P, 4, TILES])
        mean, vareps, rstd, mhalf = (sb(k, [P, TILES]) for k in ("mean", "vareps", "rstd", "mhalf32"))
        PS = [ctx.enter_context(nc.psum_tensor(f"ps{c}_f3", [P, T4], F32)) for c in range(8)]
        X, U, G, GS, O = range(5)
        SC_STEPS = 4
        upf, gtf = up[:].rearrange("p n i t -> p (n i) t"), gt[:].rearrange("p n i t -> p (n i) t")

        def part(t, r):
            return t[:, bass.ds(r, 1), :].rearrange("p a t -> p (a t)")

        def scale_vector(dve, done, k, n, width, factor=None):
            col = slice(k, k + 1)
            nc.vector.tensor_reduce(amr[:, col], am[:, k, 0:width], axis=AX.X, op=ALU.max).then_inc(s("absmax").sem, 1)
            dve.wait_ge(s("gmax").sem, s("gmax").at(n))
            f = 1.0 if factor is None else factor
            done(nc.vector.tensor_scalar(scale[:, col], gm[:, col], f, 1.0 / QMAX, ALU.mult, ALU.mult))
            done(nc.vector.tensor_scalar(scale[:, col], scale[:, col], 1e-12, None, ALU.max))
            done(nc.vector.reciprocal(inv[:, col], scale[:, col]))
            done(nc.vector.tensor_scalar(inv[:, col], inv[:, col], f, None, ALU.mult))

        def gmax_pool(pool, k, n):
            pool.wait_ge(s("absmax").sem, s("absmax").at(n))
            nc.gpsimd.partition_all_reduce(gm[:, k:k + 1], amr[:, k:k + 1], P, bass.bass_isa.ReduceOp.max)\
                .then_inc(s("gmax").sem, 1)

        NW = 2 + 6 + SC_STEPS
        with nc.Block() as block:
            @block.sync
            def _(sp):
                load_weights(sp, pr, loads, 0)

            @block.gpsimd
            def _(pool):
                nc.gpsimd.memset(magic[:, 0:1], MAGIC)
                nc.gpsimd.memset(magic[:, 1:2], -MAGIC)
                nc.gpsimd.memset(mhalf[:], -0.5).then_inc(s("pool_steps").sem, 1)
                pool.wait_ge(s("pool_steps").sem, s("pool_steps").at(1))
                pool.wait_ge(s("ln_var").sem, s("ln_var").at(1))
                nc.gpsimd.tensor_tensor(rstd[:], vareps[:], mhalf[:], ALU.pow).then_inc(s("ln_rstd").sem, 1)
                gmax_pool(pool, X, 1)

            @block.scalar
            def _(act):
                for k in range(3):
                    act.wait_ge(s("vT").sem, s("vT").at(k + 1))
                    nc.scalar.activation(wT[:, k, :], PS[5 + k][:, 0:L3_I], ACT.Copy).then_inc(s("v_ready").sem, 1)
                for i in range(ITERS):
                    act.wait_ge(s("ln_T").sem, s("ln_T").at(i + 1))
                    nc.scalar.activation(xT[:, i, :], PS[i % 2][:], ACT.Copy).then_inc(s("xT_ready").sem, 1)

            @block.tensor
            def _(pe):
                pe.wait_ge(s("quant").sem, s("quant").at(1))
                for k in range(3):
                    for j in range(NI):
                        ins = nc.tensor.transpose(PS[5 + k][:, j * P:(j + 1) * P], wraw[:, k, j * P:(j + 1) * P], ident[:])
                    ins.then_inc(s("vT").sem, 1)
                for i in range(ITERS):
                    pe.wait_ge(s("ln_out").sem, s("ln_out").at(i + 1))
                    pe.wait_ge(s("xT_ready").sem, s("xT_ready").at(i - 1))
                    for c in range(TPI):
                        ins = nc.tensor.transpose(PS[i % 2][:, c * P:(c + 1) * P], xq[:, i % 2, 0, c * P:(c + 1) * P], ident[:])
                    ins.then_inc(s("ln_T").sem, 1)

            @block.vector
            def _(dve):
                st = Steps(dve, s("dve_steps"), 0, NW)
                with dve.Fori(0, TILES) as i:
                    nc.vector.bn_stats(stats[:, bass.ds(i, 1), :].rearrange("p a s -> p (a s)"),
                                       x_sb[:, bass.ds(i, 1), :].rearrange("p a d -> p (a d)")).then_inc(s("z_ready").sem, 1)
                dve.wait_ge(s("z_ready").sem, s("z_ready").at(TILES))
                nc.vector.tensor_tensor(mv[:, 0, :], stats[:, :, 1], stats[:, :, 4], ALU.add)
                nc.vector.scalar_tensor_tensor(mv[:, 2, :], stats[:, :, 2], P * EPS, stats[:, :, 5], ALU.add, ALU.add)
                st.done(nc.vector.tensor_tensor(mv[:, 1, :], stats[:, :, 1], stats[:, :, 4], ALU.subtract))
                nc.vector.tensor_scalar(mean[:], mv[:, 0, :], 0.5, None, ALU.mult)
                st.done(nc.vector.scalar_tensor_tensor(mv[:, 3, :], mv[:, 1, :], 0.25, mv[:, 1, :], ALU.mult, ALU.mult))
                nc.vector.scalar_tensor_tensor(vareps[:], mv[:, 2, :], 1.0 / P, mv[:, 3, :], ALU.mult, ALU.add)\
                    .then_inc(s("ln_var").sem, 1)
                dve.wait_ge(s("weights").sem, s("weights").at(16))
                wb = wraw[:].rearrange("p k (n b) -> p (k n) b", b=BLK)
                wsf, wif = ws[:].rearrange("p k n -> p (k n)"), wi[:].rearrange("p k n -> p (k n)")
                full = list(wb.shape)
                st.done(nc.vector.tensor_reduce(wsf, wb, axis=AX.X, op=ALU.max, apply_absolute_value=True))
                st.done(nc.vector.tensor_scalar(wsf, wsf, 1.0 / 7.0, 1e-12, ALU.mult, ALU.max))
                st.done(nc.vector.reciprocal(wif, wsf))
                st.done(nc.vector.tensor_tensor(wb, wb, wif.unsqueeze(2).broadcast_to(full), ALU.mult))
                st.done(nc.vector.tensor_scalar(wraw[:], wraw[:], MAGIC, -MAGIC, ALU.add, ALU.add))
                st.done(nc.vector.tensor_scalar(wraw[:], wraw[:], 7.0, -8.0, ALU.min, ALU.max))
                nc.vector.tensor_tensor(wb, wb, wsf.unsqueeze(2).broadcast_to(full), ALU.mult).then_inc(s("quant").sem, 1)
                dve.wait_ge(s("ln_rstd").sem, s("ln_rstd").at(1))

                def largest(i):
                    dve.wait_ge(s("ln_out").sem, s("ln_out").at(i + 1))
                    nc.vector.tensor_reduce(am[:, X, i:i + 1], xq[:, i % 2, 0, :], axis=AX.X, op=ALU.max,
                                            apply_absolute_value=True).then_inc(s("maxed").sem, 1)
                for i in range(ITERS):
                    dve.wait_ge(s("ln_T").sem, s("ln_T").at(i - 1))
                    dve.wait_ge(s("maxed").sem, s("maxed").at(i - 1))
                    for c in range(TPI):
                        n = i * TPI + c
                        ins = nc.vector.tensor_scalar(xq[:, i % 2, 0, c * P:(c + 1) * P], x_sb[:, n, :], mean[:, n:n + 1],
                                                      rstd[:, n:n + 1], ALU.subtract, ALU.mult)
                    ins.then_inc(s("ln_out").sem, 1)
                    if i:
                        largest(i - 1)
                largest(ITERS - 1)
                dve.wait_ge(s("maxed").sem, s("maxed").at(ITERS))
                scale_vector(dve, st.done, X, 1, ITERS)
                st.end()
        pr.end_block(dict(weights=16, ln_var=1, ln_rstd=1, absmax=1, gmax=1, vT=3, v_ready=3, ln_T=ITERS, xT_ready=ITERS,
                          quant=1, ln_out=ITERS, maxed=ITERS, dve_steps=NW, z_ready=TILES, pool_steps=1))

        with nc.Block() as block:
            NP = 2 * NI

            @block.gpsimd
            def _(pool):
                gmax_pool(pool, U, 1)
                gmax_pool(pool, G, 2)

            @block.tensor
            def _(pe):
                def project(i, k):
                    pe.wait_ge(s("quant").sem, s("quant").at(i + 1))
                    for n in range(NP):
                        pe.wait_ge(s("hidden_b").sem, s("hidden_b").at((i - 1) * NP + n + 1))
                        nc.tensor.matmul(PS[n][:], wT[:, n // NI, (n % NI) * P:(n % NI + 1) * P], xq[:, k, 0, :],
                                         start=True, stop=True).then_inc(s("hidden").sem, 1)
                with pe.Fori(0, ITERS // 2) as i:
                    project(2 * i, 0)
                    project(2 * i + 1, 1)

            @block.scalar
            def _(act):
                with act.Fori(0, ITERS) as i:
                    for n in range(NP):
                        act.wait_ge(s("hidden").sem, s("hidden").at(i * NP + n + 1))
                        kept = (gt if n < NI else up)[:, n % NI, bass.ds(i, 1), :].rearrange("p a t -> p (a t)")
                        nc.scalar.activation(kept, PS[n][:], ACT.Copy, scale=scale[:, X:X + 1]).then_inc(s("hidden_b").sem, 1)

            @block.vector
            def _(dve):
                def quantise(i, k):
                    dve.wait_ge(s("hidden").sem, s("hidden").at((i - 1) * NP))
                    nc.vector.tensor_scalar(xq[:, k, 0, :], part(xT, i), inv[:, X:X + 1], MAGIC, ALU.mult, ALU.add)\
                        .then_inc(s("scaled").sem, 1)
                    dve.wait_ge(s("scaled").sem, s("scaled").at(i + 1))
                    nc.vector.tensor_scalar(xq[:, k, 0, :], xq[:, k, 0, :], -MAGIC, None, ALU.add).then_inc(s("quant").sem, 1)

                def largest(i):
                    for k, kept in ((G, gt), (U, up)):
                        dve.wait_ge(s("hidden_b").sem, s("hidden_b").at(i * NP + (NI if k == G else NP)))
                        nc.vector.tensor_reduce(am[:, k, bass.ds(i, 1)], kept[:, :, bass.ds(i, 1), :].rearrange("p n a t -> p (n a) t"),
                                                axis=AX.XY, op=ALU.max, apply_absolute_value=True).then_inc(s("maxed").sem, 1)
                quantise(0, 0)
                quantise(1, 1)
                with dve.Fori(0, ITERS // 2 - 1) as i:
                    for k in range(2):
                        largest(2 * i + k)
                        quantise(2 * i + k + 2, k)
                largest(ITERS - 2)
                largest(ITERS - 1)
                st = Steps(dve, s("dve_steps"), 0, 2 * SC_STEPS)
                dve.wait_ge(s("maxed").sem, s("maxed").at(ITERS * 2))
                scale_vector(dve, st.done, U, 1, ITERS)
                scale_vector(dve, st.done, G, 2, ITERS)
        pr.end_block(dict(absmax=2, gmax=2, quant=ITERS, scaled=ITERS, hidden=ITERS * NP, hidden_b=ITERS * NP, maxed=ITERS * 2,
                          dve_steps=2 * SC_STEPS))

        DEPTH = 4
        with nc.Block() as block:
            @block.gpsimd
            def _(pool):
                def step(r, k):
                    if has(r - 1, ROWS):
                        pool.wait_ge(s("hidden_ready").sem, s("hidden_ready").at(r))
                        nc.gpsimd.tensor_tensor(part(gtf, r - 1), gq[:, (k - 1) % DEPTH, :], sig[:, (k - 1) % DEPTH, :], ALU.mult)\
                            .then_inc(s("hidden_mul").sem, 1)
                rows_in_steps(pool, ROWS, DEPTH, step)
                gmax_pool(pool, GS, 1)

            @block.scalar
            def _(act):
                def step(r, k):
                    if has(r, ROWS):
                        act.wait_ge(s("hidden_mul").sem, s("hidden_mul").at(r + 1 - DEPTH))
                        act.wait_ge(s("qkv_ready").sem, s("qkv_ready").at(r + 1 - DEPTH))
                        nc.scalar.activation(gq[:, k, :], part(gtf, r), ACT.Identity, bias=magic[:, 0:1], scale=inv[:, G:G + 1])\
                            .then_inc(s("scaled").sem, 1)
                        nc.scalar.activation(uq[:, k, :], part(upf, r), ACT.Identity, bias=magic[:, 0:1], scale=inv[:, U:U + 1])\
                            .then_inc(s("act_steps").sem, 1)
                    if has(r - 1, ROWS):
                        q = (k - 1) % DEPTH
                        act.wait_ge(s("act_steps").sem, s("act_steps").at(r))
                        act.wait_ge(s("quant").sem, s("quant").at(r))
                        nc.scalar.activation(sig[:, q, :], gq[:, q, :], ACT.Sigmoid, scale=scale[:, G:G + 1])\
                            .then_inc(s("hidden_act").sem, 1)
                        nc.scalar.activation(part(upf, r - 1), uq[:, q, :], ACT.Identity, bias=magic[:, 1:2])\
                            .then_inc(s("qkv_ready").sem, 1)
                rows_in_steps(act, ROWS, DEPTH, step)

            @block.vector
            def _(dve):
                def step(r, k):
                    if has(r, ROWS):
                        dve.wait_ge(s("scaled").sem, s("scaled").at(r + 1))
                        nc.vector.tensor_scalar(gq[:, k, :], gq[:, k, :], -MAGIC, None, ALU.add).then_inc(s("quant").sem, 1)
                    if has(r - 1, ROWS):
                        dve.wait_ge(s("hidden_act").sem, s("hidden_act").at(r))
                        sg = sig[:, (k - 1) % DEPTH, :]
                        nc.vector.tensor_scalar(sg, sg, 65536.0, 65535.0, ALU.mult, ALU.min).then_inc(s("hidden").sem, 1)
                    if has(r - 3, ROWS):
                        dve.wait_ge(s("hidden_mul").sem, s("hidden_mul").at(r - 2))
                        nc.vector.tensor_reduce(am[:, GS, bass.ds(r - 3, 1)], part(gtf, r - 3), axis=AX.X, op=ALU.max,
                                                apply_absolute_value=True).then_inc(s("maxed").sem, 1)
                    if has(r - 1, ROWS):
                        dve.wait_ge(s("hidden").sem, s("hidden").at(r))
                        nc.vector.tensor_scalar(sg, sg, MAGIC, -MAGIC, ALU.add, ALU.add).then_inc(s("hidden_ready").sem, 1)
                rows_in_steps(dve, ROWS, DEPTH, step)
                st = Steps(dve, s("dve_steps"), 0, SC_STEPS + 1)
                dve.wait_ge(s("maxed").sem, s("maxed").at(ROWS))
                st.done(nc.vector.tensor_scalar(fac[:, GS:GS + 1], scale[:, G:G + 1], 1.0 / 65536.0, None, ALU.mult))
                scale_vector(dve, st.done, GS, 1, ROWS, fac[:, GS:GS + 1])
        pr.end_block(dict(absmax=1, gmax=1, quant=ROWS, scaled=ROWS, act_steps=ROWS, qkv_ready=ROWS, hidden_act=ROWS, hidden=ROWS,
                          hidden_ready=ROWS, hidden_mul=ROWS, maxed=ROWS, dve_steps=SC_STEPS + 1))

        with nc.Block() as block:
            @block.gpsimd
            def _(pool):
                gmax_pool(pool, O, 1)

            @block.scalar
            def _(act):
                with act.Fori(0, ROWS) as r:
                    nc.scalar.activation(part(gtf, r), part(gtf, r), ACT.Identity, bias=magic[:, 0:1], scale=inv[:, GS:GS + 1])\
                        .then_inc(s("scaled").sem, 1)

            @block.vector
            def _(dve):
                def step(r, k):
                    if has(r, ROWS):
                        dve.wait_ge(s("scaled").sem, s("scaled").at(r + 1))
                        nc.vector.scalar_tensor_tensor(part(gtf, r), part(gtf, r), -MAGIC, part(upf, r), ALU.add, ALU.mult)\
                            .then_inc(s("quant").sem, 1)
                    if has(r - 1, ROWS):
                        dve.wait_ge(s("quant").sem, s("quant").at(r))
                        nc.vector.tensor_reduce(am[:, O, bass.ds(r - 1, 1)], part(gtf, r - 1), axis=AX.X, op=ALU.max,
                                                apply_absolute_value=True).then_inc(s("maxed").sem, 1)
                rows_in_steps(dve, ROWS, DEPTH, step)
                st = Steps(dve, s("dve_steps"), 0, SC_STEPS + 1)
                dve.wait_ge(s("maxed").sem, s("maxed").at(ROWS))
                st.done(nc.vector.tensor_tensor(fac[:, O:O + 1], scale[:, GS:GS + 1], scale[:, U:U + 1], ALU.mult))
                scale_vector(dve, st.done, O, 1, ROWS, fac[:, O:O + 1])
        pr.end_block(dict(absmax=1, gmax=1, scaled=ROWS, quant=ROWS, maxed=ROWS, dve_steps=SC_STEPS + 1))

        with nc.Block() as block:
            @block.tensor
            def _(pe):
                def down(i, k):
                    pe.wait_ge(s("quant").sem, s("quant").at(i + 1))
                    pe.wait_ge(s("x_added").sem, s("x_added").at(i - 1))
                    for c in range(TPI):
                        for n in range(NI):
                            ins = nc.tensor.matmul(PS[k][:, c * P:(c + 1) * P], xq[:, k, n, c * P:(c + 1) * P],
                                                   wT[:, 2, n * P:(n + 1) * P], start=n == 0, stop=n == NI - 1)
                    ins.then_inc(s("ffn_out").sem, 1)
                with pe.Fori(0, ITERS // 2) as i:
                    down(2 * i, 0)
                    down(2 * i + 1, 1)

            @block.scalar
            def _(act):
                def quantise(i, k):
                    act.wait_ge(s("ffn_out").sem, s("ffn_out").at(i - 1))
                    nc.scalar.activation(xq[:, k, :, :], gt[:, :, bass.ds(i, 1), :].rearrange("p n a t -> p (n a) t"),
                                         ACT.Identity, bias=magic[:, 0:1], scale=inv[:, O:O + 1]).then_inc(s("scaled").sem, 1)
                with act.Fori(0, ITERS // 2) as i:
                    quantise(2 * i, 0)
                    quantise(2 * i + 1, 1)

            @block.vector
            def _(dve):
                def integers(i, k):
                    dve.wait_ge(s("scaled").sem, s("scaled").at(i + 1))
                    nc.vector.tensor_scalar(xq[:, k, :, :], xq[:, k, :, :], -MAGIC, None, ALU.add).then_inc(s("quant").sem, 1)

                def add(i, k):
                    dve.wait_ge(s("ffn_out").sem, s("ffn_out").at(i + 1))
                    x4 = tile4(x_sb, i)
                    nc.vector.scalar_tensor_tensor(x4, PS[k][:].rearrange("p (c d) -> p c d", d=P), scale[:, O:O + 1], x4,
                                                   ALU.mult, ALU.add).then_inc(s("x_added").sem, 1)
                integers(0, 0)
                with dve.Fori(0, ITERS // 2 - 1) as i:
                    for k in range(2):
                        integers(2 * i + k + 1, 1 - k)
                        add(2 * i + k, k)
                integers(ITERS - 1, 1)
                add(ITERS - 2, 0)
                add(ITERS - 1, 1)
        pr.end_block(dict(scaled=ITERS, quant=ITERS, ffn_out=ITERS, x_added=ITERS))


def build(nc, dram, out):
    with ExitStack() as ctx:
        pr = Program(nc, ctx)
        for name in SIGNALS:
            pr.sig(name)
        x_sb = ctx.enter_context(nc.sbuf_tensor("x_sb", [P, TILES, P], F32))
        common = {}

        def csb(name, shape, dt=F32):
            common[name] = ctx.enter_context(nc.sbuf_tensor(name, shape, dt))
            return common[name]
        csb("ident", [P, P]), csb("identb", [P, P], BF16), csb("ctxT", [P, B * P]), csb("headmask", [P, H])
        csb("mhalf", [P, 16])
        with nc.Block() as block:
            @block.sync
            def _(sp):
                n = load_weights(sp, pr, [(x_sb[:], dram["x"]), (common["ident"][:], dram["ident"]),
                                          (common["headmask"][:], dram["headmask"]), (common["ctxT"][:], dram["ctxT"])],
                                 0)
                sp.wait_ge(pr.sig("weights").sem, n + Signal.PRIME)

            @block.gpsimd
            def _(pool):
                for g in pr.named.values():
                    pool.sem_inc(g.sem, Signal.PRIME)
                nc.gpsimd.memset(common["mhalf"][:], -0.5)

            @block.vector
            def _(dve):
                dve.wait_ge(pr.sig("weights").sem, 64 + Signal.PRIME)
                nc.vector.tensor_copy(common["identb"][:], common["ident"][:])
        pr.end_block(dict(weights=64))
        for n in range(N_SUBLAYERS):
            if n == 0:
                context_attention(pr, x_sb, common, dram, 0)
            elif n % 2 == 0:
                narrow_attention(pr, x_sb, common, dram, n // 2)
            elif n == 1:
                layer0_ffn(pr, x_sb, common, dram)
            elif n == 3:
                layer1_ffn(pr, x_sb, common, dram)
            elif n == 5:
                layer2_ffn(pr, x_sb, common, dram)
            else:
                layer3_ffn(pr, x_sb, common, dram)
        with nc.Block() as block:
            @block.sync
            def _(sp):
                sp.dma_start(out, x_sb[:]).then_inc(pr.sig("out_stored").sem, 16)
                sp.wait_ge(pr.sig("out_stored").sem, pr.sig("out_stored").at(16))


def laid_out(inp):
    import numpy as np
    f = {k: np.asarray(v) for k, v in inp.items()}

    def rows(a):
        return a.reshape(-1, P, a.shape[-1]).transpose(1, 0, 2)

    d = {}
    d["x"] = rows(f["x"].reshape(B * S, P))
    ct = f["ctx_1024"].transpose(2, 0, 1)
    d["ctxT"] = np.concatenate([ct, ct], axis=2).reshape(P, B * P)
    d["mask"] = f["mask_Bx1xSxS2_ik1"].reshape(TILES, P, SC).transpose(1, 0, 2)
    d["ident"] = np.eye(P, dtype=np.float32)
    d["headmask"] = np.kron(np.eye(H, dtype=np.float32), np.ones((P // H, 1), np.float32))
    d["L0_wqT"], d["L0_wkT"] = rows(f["L0_xattn_Wq"].T), rows(f["L0_xattn_Wk"].T)
    d["L0_wv"], d["L0_wo"] = f["L0_xattn_Wv"], rows(f["L0_xattn_Wo"])
    d["L0_bo"] = f["L0_xattn_bo"]
    zero = np.zeros(P, np.float32)
    eye = np.eye(P, dtype=np.float32)
    d["L1_w4"] = np.stack([eye, eye, eye, f["L1_xattn_w_proj"].T], axis=1)
    d["L1_cols"] = np.stack([zero, zero, zero], axis=1)
    d["L1_bo"] = f["L1_xattn_b_proj"]
    d["L2_w4"] = np.stack([f["L2_xattn_wq"], f["L2_xattn_wk"], f["L2_xattn_wv"], f["L2_xattn_wo"]], axis=1)
    d["L2_cols"] = np.stack([zero, zero, zero], axis=1)
    d["L2_bo"] = f["L2_xattn_bo"]
    d["L3_w4"] = np.stack([f["L3_xattn_Wq"].T, f["L3_xattn_Wk"].T, f["L3_xattn_Wv"].T, f["L3_xattn_Wo"].T], axis=1)
    d["L3_cols"] = np.stack([f["L3_xattn_bq"], f["L3_xattn_bk"], f["L3_xattn_bv"]], axis=1)
    d["L3_bo"] = f["L3_xattn_bo"]
    d["desc8"] = np.arange(8, 0, -1).astype(np.float32)
    d["F0_wd"] = f["L0_ffn_W_down"].transpose(1, 0, 2).reshape(P, 512)
    d["F0_wu"] = rows(f["L0_ffn_W_up"].reshape(512, P))
    d["F0_wr"], d["F0_br"], d["F0_bup"] = f["L0_ffn_Wr"], f["L0_ffn_br"], f["L0_ffn_b_up"]
    d["F0_cols"] = np.concatenate([np.stack([f["L0_ffn_" + k] for k in ("bn_var", "bn_g", "bn_b", "bn_mean", "ln_g", "ln_b")],
                                            axis=1), f["L0_ffn_b_down"].reshape(4, P).T], axis=1)

    def joined(a, b):
        return np.concatenate([a, b[None]], axis=0)

    def chunked(a):
        out = np.zeros((L1_CH * P, a.shape[1]), a.dtype)
        out[:L1_ALL] = a
        return rows(out)

    for k in ("w1", "w3"):
        d["F1_" + k] = joined(f["L1_ffn_" + k], f["L1_ffn_s" + k]).transpose(1, 0, 2).reshape(P, L1_ALL)
    d["F1_w2"] = chunked(joined(f["L1_ffn_w2"], f["L1_ffn_sw2"]).reshape(L1_ALL, P))
    d["F1_cols"] = np.concatenate([chunked(joined(f["L1_ffn_" + k], f["L1_ffn_s" + k]).reshape(L1_ALL, 1))[:, :, 0]
                                   for k in ("b1", "b3")], axis=1)
    d["F1_b2"] = np.concatenate([joined(f["L1_ffn_b2"], f["L1_ffn_sb2"])] * 3, axis=0)
    d["F1_gw"], d["F1_gb"] = f["L1_ffn_gate_w"].T, f["L1_ffn_gate_b"]
    d["F1_sel"] = np.concatenate([np.kron(np.eye(L1_E + 1, dtype=np.float32), np.ones((1, L1_H), np.float32))] * 3, axis=0)

    d["desc16"] = np.arange(L2_E, 0, -1).astype(np.float32)
    d["F2_sim"], d["F2_gates"] = f["L2_ffn_sim_matrix"], f["L2_ffn_gates"]
    d["ones"] = np.ones((P, P), np.float32)
    d["tri"] = np.triu(np.full((P, P), NEG, np.float32), 1)
    d["F2_sel"] = np.concatenate([np.kron(np.eye(L2_E, dtype=np.float32), np.ones((1, P), np.float32))] * 3, axis=0)
    for k in "qkvo":
        d["F2_w" + k] = f[f"L2_ffn_{k}_proj"].transpose(1, 0, 2)
    d["F3_w"] = np.stack([rows(f["L3_ffn_w_gate"]).reshape(P, L3_I), rows(f["L3_ffn_w_up"]).reshape(P, L3_I),
                          f["L3_ffn_w_down"]], axis=1)
    return d


def kernel(**inputs):
    import numpy as _np
    import concourse.bacc as _bacc
    from concourse import mybir as _mybir
    from concourse.bass_utils import run_bass_kernel_spmd as _run

    nc = _bacc.Bacc("TRN2", target_bir_lowering=False, num_devices=1)
    arrays, dram = {}, {}
    for name, a in laid_out(inputs).items():
        a = _np.ascontiguousarray(a)
        arrays[f"in_{name}"] = a
        dram[name] = nc.dram_tensor(f"in_{name}", a.shape, _mybir.dt.from_np(a.dtype), kind="ExternalInput").ap()
    out = nc.dram_tensor("out_0", (P, TILES, P), F32, kind="ExternalOutput").ap()
    build(nc, dram, out)
    r = _run(nc, [arrays], core_ids=[0])
    got = r.results[0]["out_0"]
    return _np.ascontiguousarray(got.transpose(1, 0, 2)).reshape(B, S, P)
```

```python
from contextlib import ExitStack

import concourse.bass as bass
from concourse import mybir

F32 = mybir.dt.float32
BF16 = mybir.dt.bfloat16
F32R = mybir.dt.float32r
I32 = mybir.dt.int32
ALU = mybir.AluOpType
ACT = mybir.ActivationFunctionType
AX = mybir.AxisListType

N_SUBLAYERS = 8

P = 128
B, S, SC = 16, 256, 64
TILES = B * S // P
TPI = 4
BPI = 2
ITERS = TILES // TPI
H = 16
PAIRS = H // 2
KEYS = H * SC
EPS = 1e-5
L1_E, L1_H = 8, 176
L1_ALL = (L1_E + 1) * L1_H
L1_CH = -(-L1_ALL // P)
L2_E = 16
L3_I = 384
BLK = 32
NEG = -float(2 ** 100)
MAGIC = 1.5 * 2.0 ** 23


class Signal:
    PRIME = 8

    def __init__(self, sem):
        self.sem, self.base = sem, Signal.PRIME

    def at(self, n):
        return n + self.base


class Steps:

    def __init__(self, eng, sig, i, per_iteration):
        self.eng, self.sig, self.i, self.n, self.k = eng, sig, i, per_iteration, 0

    def done(self, instruction):
        self.k += 1
        instruction.then_inc(self.sig.sem, 1)
        self.eng.wait_ge(self.sig.sem, self.sig.at(self.i * self.n + self.k))

    def end(self):
        assert self.k == self.n, (self.k, self.n)


class Program:

    def __init__(self, nc, ctx):
        self.nc, self.ctx, self.named = nc, ctx, {}

    def sig(self, name):
        if name not in self.named:
            self.named[name] = Signal(self.ctx.enter_context(self.nc.semaphore(name)))
        return self.named[name]

    def end_block(self, counts):
        for name, n in counts.items():
            self.named[name].base += n


SIGNALS = [
    "ln_var", "ln_rstd", "ln_out", "ln_T", "xT_ready", "bias_added", "x_added",
    "ctx_ready", "kv_proj", "kv_ready", "khat_ready", "q_proj", "q_ready", "mask_ready",
    "scores", "shifted", "shifted_T", "probs", "heads_out", "heads_norm", "heads_T", "headsT_ready", "attn_proj",
    "dve_steps", "pool_steps", "act_steps", "ahead", "split", "up_scaled", "up_ready", "ctx_high", "ctx_split", "n_split", "q_split", "k_split", "khat_first", "x_split", "x_high", "x_loaded", "weights_qk", "inputs", "out_stored",
    "z_ready", "gate_logits", "gate_exp", "gate_ready", "gate_T", "gate_parts",
    "hidden", "hidden_b", "hidden_ready", "ffn_out", "ffn_outT", "ffn_outT_ready", "gate_bcast", "hidden_mul", "hidden_act",
    "scaled", "qkv", "qkv_ready", "vT", "v_ready", "maxed", "pT", "pT_ready", "ao", "ao_ready",
    "absmax", "gmax", "quant", "wraw", "routes_kept", "sums_inverted",
    "front_out", "front_ready", "stats_ready", "probs_T", "normed", "summed",
]


def load(eng, signal, pairs):
    for dst, src in pairs:
        eng.dma_start(dst, src).then_inc(signal.sem, 16)


def buffers(nc, ctx, tag):
    def sb(name, shape, dt=F32):
        return ctx.enter_context(nc.sbuf_tensor(f"{name}_{tag}", shape, dt))
    return sb


class Ahead:

    def __init__(self, tensors, loads, copies=(), splits=()):
        self.tensors, self.loads, self.copies, self.splits = tensors, loads, tuple(copies), tuple(splits)

    def __add__(self, other):
        return Ahead({**self.tensors, **other.tensors}, self.loads + other.loads, self.copies + other.copies,
                     self.splits + other.splits)

    def start(self, pr, sp):
        load(sp, pr.sig("ahead"), self.loads)

    def convert(self, pr, act):
        act.wait_ge(pr.sig("ahead").sem, pr.sig("ahead").at(16 * len(self.loads)))
        for dst, src in self.copies:
            pr.nc.scalar.activation(dst, src, ACT.Copy)

    def split(self, pr, pool):
        if self.splits:
            pool.wait_ge(pr.sig("ahead").sem, pr.sig("ahead").at(16 * len(self.loads)))
        for k, (raw, hi, lo) in enumerate(self.splits):
            pr.nc.gpsimd.tensor_copy(hi, raw).then_inc(pr.sig("split").sem, 1)
            pool.wait_ge(pr.sig("split").sem, pr.sig("split").at(k + 1))
            pr.nc.gpsimd.tensor_tensor(lo, raw, hi, ALU.subtract)

    @property
    def counts(self):
        return dict(ahead=16 * len(self.loads), split=len(self.splits))


def ln_buffers(sb):
    return dict(stats=sb("stats", [P, TPI, 6]), mv=sb("mv", [P, 4, TPI]), mean=sb("mean", [P, TPI]),
                vareps=sb("vareps", [P, TPI]), rstd=sb("rstd", [P, TPI]))


LN_STEPS = 3


def layernorm_vector(pr, dve, steps, i, w, x4, xn):
    nc = pr.nc
    for c in range(TPI):
        ins = nc.vector.bn_stats(w["stats"][:, c, :], x4[:, c, :])
    steps.done(ins)
    st, mv = w["stats"], w["mv"]
    nc.vector.tensor_tensor(mv[:, 0, :], st[:, :, 1], st[:, :, 4], ALU.add)
    nc.vector.scalar_tensor_tensor(mv[:, 2, :], st[:, :, 2], P * EPS, st[:, :, 5], ALU.add, ALU.add)
    steps.done(nc.vector.tensor_tensor(mv[:, 1, :], st[:, :, 1], st[:, :, 4], ALU.subtract))
    nc.vector.tensor_scalar(w["mean"][:], mv[:, 0, :], 0.5, None, ALU.mult)
    steps.done(nc.vector.scalar_tensor_tensor(mv[:, 3, :], mv[:, 1, :], 0.25, mv[:, 1, :], ALU.mult, ALU.mult))
    nc.vector.scalar_tensor_tensor(w["vareps"][:], mv[:, 2, :], 1.0 / P, mv[:, 3, :], ALU.mult, ALU.add)\
        .then_inc(pr.sig("ln_var").sem, 1)


def layernorm_apply(pr, dve, w, x4, xn):
    for c in range(TPI):
        ins = pr.nc.vector.tensor_scalar(xn[:, c, :], x4[:, c, :], w["mean"][:, c:c + 1], w["rstd"][:, c:c + 1],
                                         ALU.subtract, ALU.mult)
    return ins


def layernorm_pool(pr, pool, n, w):
    pool.wait_ge(pr.sig("ln_var").sem, pr.sig("ln_var").at(n))
    pr.nc.gpsimd.tensor_tensor(w["rstd"][:], w["vareps"][:], w["mhalf"][:, 0:TPI], ALU.pow).then_inc(pr.sig("ln_rstd").sem, 1)


def tile4(x_sb, i):
    return x_sb[:, bass.ds(i * TPI, TPI), :]


def has(r, rows):
    return not isinstance(r, int) or 0 <= r < rows


def all_ln_buffers(sb):
    return dict(stats=sb("stats", [P, TILES, 6]), mv=sb("mv", [P, 4, TILES]), mean=sb("mean", [P, TILES]),
                vareps=sb("vareps", [P, TILES]), rstd=sb("rstd", [P, TILES]), mhalf=sb("mhalf32", [P, TILES]))


def all_ln_vector(pr, dve, done, w, x_sb, k=1):
    nc, st, mv, z = pr.nc, w["stats"], w["mv"], pr.sig("stats_ready")
    for i in range(TILES):
        ins = nc.vector.bn_stats(st[:, i, :], x_sb[:, i, :])
    ins.then_inc(z.sem, 1)
    dve.wait_ge(z.sem, z.at(k))
    nc.vector.tensor_tensor(mv[:, 0, :], st[:, :, 1], st[:, :, 4], ALU.add)
    nc.vector.scalar_tensor_tensor(mv[:, 2, :], st[:, :, 2], P * EPS, st[:, :, 5], ALU.add, ALU.add)
    done(nc.vector.tensor_tensor(mv[:, 1, :], st[:, :, 1], st[:, :, 4], ALU.subtract))
    nc.vector.tensor_scalar(w["mean"][:], mv[:, 0, :], 0.5, None, ALU.mult)
    done(nc.vector.scalar_tensor_tensor(mv[:, 3, :], mv[:, 1, :], 0.25, mv[:, 1, :], ALU.mult, ALU.mult))
    nc.vector.scalar_tensor_tensor(w["vareps"][:], mv[:, 2, :], 1.0 / P, mv[:, 3, :], ALU.mult, ALU.add)\
        .then_inc(pr.sig("ln_var").sem, 1)


def all_ln_pool(pr, pool, w):
    nc, steps = pr.nc, pr.sig("pool_steps")
    nc.gpsimd.memset(w["mhalf"][:], -0.5).then_inc(steps.sem, 1)
    pool.wait_ge(steps.sem, steps.at(1))
    all_rstd(pr, pool, w, 1)


RSTD_PARTS = 4
RSTD_TILES = TILES // RSTD_PARTS


def all_rstd(pr, pool, w, k):
    pool.wait_ge(pr.sig("ln_var").sem, pr.sig("ln_var").at(k))
    for part in range(RSTD_PARTS):
        c = slice(part * RSTD_TILES, (part + 1) * RSTD_TILES)
        pr.nc.gpsimd.tensor_tensor(w["rstd"][:, c], w["vareps"][:, c], w["mhalf"][:, c], ALU.pow)\
            .then_inc(pr.sig("ln_rstd").sem, 1)


def wait_rstd(pr, dve, n, k=1):
    if n % RSTD_TILES == 0:
        dve.wait_ge(pr.sig("ln_rstd").sem, pr.sig("ln_rstd").at((k - 1) * RSTD_PARTS + n // RSTD_TILES + 1))


N_INPUTS = 16 * 6


def wide_attention(pr, x_sb, common, wt, ahead):
    nc, s = pr.nc, pr.sig
    T4 = TPI * P
    with ExitStack() as ctx:
        def sb(name, shape, dt=F32):
            return ctx.enter_context(nc.sbuf_tensor(f"{name}_a0", shape, dt))
        ident, ctxT = common["ident"], common["ctxT"]
        wqT, wkT, wvT, wo, bo = (wt[k] for k in ("wqT", "wkT", "wvT", "wo", "bo"))
        mk = sb("mk", [P, H, P])
        nh, nl = sb("nh", [P, H, P], F32R), sb("nl", [P, H, P], F32R)
        cb = sb("cb", [P, 2, BPI, P])
        cbh, cbl = sb("cbh", [P, 2, BPI, P], F32R), sb("cbl", [P, 2, BPI, P], F32R)
        khat = sb("khat", [P, 2, BPI, H, SC])
        vhat = sb("vhat", [P, 2, BPI, PAIRS, P])
        xn, xT = sb("xn", [P, TPI, P]), sb("xT", [P, 2, T4])
        e = sb("e", [P, 4, KEYS])
        pT = sb("pT", [P, 2, KEYS])
        smax, rsum = sb("smax", [P, 2, H]), sb("rsum", [P, 2, 2, H])
        w = all_ln_buffers(sb)
        psS = [ctx.enter_context(nc.psum_tensor(f"psS{c}_a0", [P, KEYS], F32)) for c in range(2)]
        psT = ctx.enter_context(nc.psum_tensor("psT_a0", [P, KEYS], F32))
        psC = ctx.enter_context(nc.psum_tensor("psC_a0", [P, T4], F32))
        psF = ctx.enter_context(nc.psum_tensor("psF_a0", [P, T4], F32))
        block = ctx.enter_context(nc.Block())
        BODY = 2 * TPI

        def run_bodies(eng, step):
            for g in range(BODY):
                step(g // TPI, g, g)
            with eng.Fori(1, ITERS // 2 - 1) as i:
                for g in range(BODY):
                    step(2 * i + g // TPI, i * BODY + g, g)
            for g in range(BODY):
                step(ITERS - 2 + g // TPI, TILES - BODY + g, g)

        FIRST_UNITS = [("x", 0, 0, 0)] + [("k", 0, 0, u) for u in range(4)] + [("v", 0, 0, u) for u in range(5)] + \
                      [("x", 1, 1, 0)] + [("k", 1, 1, u) for u in range(3)]
        PER_ITER = 1 + 4 + 8

        def unit_bank(index):
            if isinstance(index, int) and index < len(FIRST_UNITS):
                return (psT[:, 0:T4], index - 1) if index % 2 else (psF[:], index - 1)
            return psF[:], index

        def units(j, g):
            c, p = g % TPI, g // TPI % 2
            here, nxt, two = (j, p), (j + 1, 1 - p), (j + 2, p)
            all_units = [[("k", nxt, 3)] + [("v", here, u) for u in (5, 6, 7)],
                         [("v", nxt, u) for u in (0, 1, 2)],
                         [("x", two, 0), ("k", two, 0), ("v", nxt, 3)],
                         [("k", two, 1), ("k", two, 2), ("v", nxt, 4)]][c]
            return [(kind, jj, q, u) for kind, (jj, q), u in all_units if has(jj, ITERS)]

        def units_before(j, c):
            if isinstance(j, int):
                return len(FIRST_UNITS) + sum(len(units(a, b)) for a in range(j + 1) for b in range(TPI) if (a, b) < (j, c))
            return len(FIRST_UNITS) + PER_ITER * j + (0, 4, 7, 10)[c]

        def by_head(ap):
            return ap.rearrange("p (h k) -> p h k", h=H)

        @block.sync
        def _(sp):
            ahead.start(pr, sp)

        @block.gpsimd
        def _(pool):
            all_ln_pool(pr, pool, w)

            def copies(j, q):
                flat, flat_h, flat_l = (t[:, q, :, :].rearrange("p b k -> p (b k)") for t in (cb, cbh, cbl))
                nc.gpsimd.tensor_copy(flat, ctxT[:, bass.ds(j * (BPI * P), BPI * P)]).then_inc(s("ctx_ready").sem, 1)
                nc.gpsimd.tensor_copy(flat_h, ctxT[:, bass.ds(j * (BPI * P), BPI * P)]).then_inc(s("ctx_high").sem, 1)
                pool.wait_ge(s("ctx_ready").sem, s("ctx_ready").at(j + 1))
                pool.wait_ge(s("ctx_high").sem, s("ctx_high").at(j + 1))
                nc.gpsimd.tensor_tensor(flat_l, flat, flat_h, ALU.subtract).then_inc(s("ctx_split").sem, 1)

            def bias(j):
                pool.wait_ge(s("ln_out").sem, s("ln_out").at(j + 1))
                x4 = tile4(x_sb, j)
                nc.gpsimd.tensor_tensor(x4, x4, bo[:].unsqueeze(1).broadcast_to([P, TPI, P]), ALU.add)\
                    .then_inc(s("bias_added").sem, 1)
            pool.wait_ge(s("inputs").sem, s("inputs").at(N_INPUTS))
            copies(0, 0)
            copies(1, 1)
            bias(0)
            bias(1)
            with pool.Fori(1, ITERS // 2) as i:
                for q in range(2):
                    j = 2 * i + q
                    pool.wait_ge(s("front_out").sem, s("front_out").at(len(FIRST_UNITS) + PER_ITER * (j - 2) + 4))
                    copies(j, q)
                    bias(j)

        @block.scalar
        def _(act):
            for k, m in enumerate((mk, nh)):
                for par in range(2):
                    act.wait_ge(s("q_proj").sem, s("q_proj").at(2 * k + par + 1))
                    nc.scalar.activation(m[:, par::2, :], psS[par][:].rearrange("p (h d) -> p h d", h=PAIRS), ACT.Copy)\
                        .then_inc(s("q_ready").sem, 1)

            def unit(index, kind, j, q, u):
                act.wait_ge(s("front_out").sem, s("front_out").at(index + 1))
                bank, _ = unit_bank(index)
                if kind == "x":
                    act.wait_ge(s("scores").sem, s("scores").at((j - 1) * TPI))
                    ins = nc.scalar.activation(xT[:, q, :], bank, ACT.Copy)
                elif kind == "k":
                    act.wait_ge(s("scores").sem, s("scores").at((j - 1) * TPI))
                    ins = nc.scalar.activation(khat[:, q, :, 4 * u:4 * u + 4, :].rearrange("p b h k -> p h b k"),
                                               bank.rearrange("p (h b k) -> p h b k", h=4, b=BPI), ACT.Copy)
                else:
                    act.wait_ge(s("attn_proj").sem, s("attn_proj").at((j - 1) * TPI))
                    b, v = u // 4, u % 4
                    src = bank.rearrange("p (q a d) -> p q a d", a=2, d=P)
                    for par in range(2):
                        r = slice(par * SC, (par + 1) * SC)
                        ins = nc.scalar.activation(vhat[r, q, b, 2 * v:2 * v + 2, :], src[r, :, par, :], ACT.Copy)
                ins.then_inc(s("front_ready").sem, 1)

            def exp(n, g):
                act.wait_ge(s("shifted").sem, s("shifted").at(n + 1))
                nc.scalar.activation(e[:, g % 4, :], e[:, g % 4, :], ACT.Exp, scale=float(SC) ** -0.5).then_inc(s("probs").sem, 1)

            def store_pT(n, g):
                act.wait_ge(s("probs_T").sem, s("probs_T").at(n + 1))
                act.wait_ge(s("attn_proj").sem, s("attn_proj").at(n - 1))
                nc.scalar.activation(pT[:, g % 2, :], psT[:], ACT.Copy).then_inc(s("pT_ready").sem, 1)

            def step(j, n, g):
                todo = [(units_before(j, g % TPI) + k, u) for k, u in enumerate(units(j, g))]
                store_pT(n, g)
                for index, u in todo[:1]:
                    unit(index, *u)
                if has(n + 2, TILES):
                    exp(n + 2, g + 2)
                for index, u in todo[1:]:
                    unit(index, *u)
            for index, u in enumerate(FIRST_UNITS):
                if index == 10:
                    exp(0, 0)
                unit(index, *u)
            exp(1, 1)
            run_bodies(act, step)
            ahead.convert(pr, act)

        @block.tensor
        def _(pe):
            for k, (left, right) in enumerate(((wkT, wqT), (wvT, wo))):
                ready = s(("weights_qk", "inputs")[k])
                pe.wait_ge(ready.sem, ready.at((32, N_INPUTS)[k]))
                for par in range(2):
                    if k:
                        pe.wait_ge(s("q_ready").sem, s("q_ready").at(par + 1))
                    r = slice(par * SC, (par + 1) * SC)
                    for q in range(PAIRS):
                        ins = nc.tensor.matmul(psS[par][:, q * P:(q + 1) * P], left[r, q, :], right[r, q, :], start=True, stop=True)
                    ins.then_inc(s("q_proj").sem, 1)

            def unit(index, kind, j, q, u):
                bank, before = unit_bank(index)
                pe.wait_ge(s("front_ready").sem, s("front_ready").at(before))
                if kind == "x":
                    pe.wait_ge(s("ln_out").sem, s("ln_out").at(j + 1))
                    for c in range(TPI):
                        ins = nc.tensor.transpose(bank[:, c * P:(c + 1) * P], xn[:, c, :], ident[:])
                elif kind == "k":
                    pe.wait_ge(s("ctx_ready").sem, s("ctx_ready").at(j + 1))
                    for h in range(4):
                        ins = nc.tensor.matmul(bank[:, h * P:(h + 1) * P], mk[:, 4 * u + h, :], cb[:, q, :, 0:SC], start=True, stop=True)
                else:
                    v = u % 4
                    pe.wait_ge(s("ctx_split").sem, s("ctx_split").at(j + 1))
                    for m, (c_part, n_part) in enumerate(((cbl, nh), (cbh, nl), (cbh, nh))):
                        ins = nc.tensor.matmul(bank, c_part[:, q, u // 4, :], n_part[:, 4 * v:4 * v + 4, :], start=m == 0, stop=m == 2)
                ins.then_inc(s("front_out").sem, 1)

            def scores(n, g):
                c, p = g % TPI, g // TPI % 2
                pe.wait_ge(s("shifted").sem, s("shifted").at(n - 1))
                for h in range(2):
                    ins = nc.tensor.matmul(psS[g % 2][:, h * 512:(h + 1) * 512], xT[:, p, c * P:(c + 1) * P],
                                           khat[:, p, c // 2, 8 * h:8 * h + 8, :], start=True, stop=True)
                ins.then_inc(s("scores").sem, 1)

            def probs_T(n, g):
                pe.wait_ge(s("normed").sem, s("normed").at(n + 1))
                pe.wait_ge(s("pT_ready").sem, s("pT_ready").at(n))
                for k in range(PAIRS):
                    ins = nc.tensor.transpose(psT[:, k * P:(k + 1) * P], e[:, g % 4, k * P:(k + 1) * P], ident[:])
                ins.then_inc(s("probs_T").sem, 1)

            def output(n, g):
                pe.wait_ge(s("pT_ready").sem, s("pT_ready").at(n + 1))
                pe.wait_ge(s("x_added").sem, s("x_added").at(n))
                for k in range(PAIRS):
                    ins = nc.tensor.matmul(psC[:, 0:P], pT[:, g % 2, k * P:(k + 1) * P], vhat[:, g // TPI % 2, g % TPI // 2, k, :],
                                           start=k == 0, stop=k == PAIRS - 1)
                ins.then_inc(s("attn_proj").sem, 1)

            def step(j, n, g):
                todo = [(units_before(j, g % TPI) + k, u) for k, u in enumerate(units(j, g))]
                probs_T(n, g)
                for index, u in todo[:1]:
                    unit(index, *u)
                if g % TPI == 1:
                    pe.wait_ge(s("front_ready").sem, s("front_ready").at(units_before(j, 1)))
                if has(n - 1, TILES):
                    output(n - 1, (g - 1) % BODY)
                for index, u in todo[1:2]:
                    unit(index, *u)
                if has(n + 3, TILES):
                    scores(n + 3, (g + 3) % BODY)
                for index, u in todo[2:]:
                    unit(index, *u)
            pe.wait_ge(s("q_ready").sem, s("q_ready").at(4))
            for index, u in enumerate(FIRST_UNITS):
                if index == 5:
                    pe.wait_ge(s("front_ready").sem, s("front_ready").at(5))
                    pe.wait_ge(s("n_split").sem, s("n_split").at(2))
                    scores(0, 0)
                    scores(1, 1)
                if index == 10:
                    scores(2, 2)
                unit(index, *u)
            pe.wait_ge(s("front_ready").sem, s("front_ready").at(len(FIRST_UNITS)))
            run_bodies(pe, step)
            output(TILES - 1, BODY - 1)

        @block.vector
        def _(dve):
            steps = Steps(dve, s("dve_steps"), 0, 2)
            dve.wait_ge(s("x_loaded").sem, s("x_loaded").at(16))
            all_ln_vector(pr, dve, steps.done, w, x_sb)
            steps.end()

            def normalised_x(j, before):
                dve.wait_ge(s("front_out").sem, s("front_out").at(before))
                for c in range(TPI):
                    n = j * TPI + c
                    ins = nc.vector.tensor_scalar(xn[:, c, :], x_sb[:, bass.ds(n, 1), :].rearrange("p a d -> p (a d)"),
                                                  w["mean"][:, bass.ds(n, 1)], w["rstd"][:, bass.ds(n, 1)], ALU.subtract, ALU.mult)
                ins.then_inc(s("ln_out").sem, 1)

            def largest(n, g):
                dve.wait_ge(s("scores").sem, s("scores").at(n + 1))
                nc.vector.tensor_reduce(smax[:, g % 2, :], by_head(psS[g % 2][:]), axis=AX.X, op=ALU.max)\
                    .then_inc(s("maxed").sem, 1)

            def shift(n, g):
                dve.wait_ge(s("maxed").sem, s("maxed").at(n + 1))
                dve.wait_ge(s("probs_T").sem, s("probs_T").at(n - 3))
                nc.vector.tensor_tensor(by_head(e[:, g % 4, :]), by_head(psS[g % 2][:]),
                                        smax[:, g % 2, :].unsqueeze(2).broadcast_to([P, H, SC]), ALU.subtract)\
                    .then_inc(s("shifted").sem, 1)

            def sums(n, g):
                dve.wait_ge(s("probs").sem, s("probs").at(n + 1))
                nc.vector.tensor_reduce(rsum[:, g % 2, 0, :], by_head(e[:, g % 4, :]), axis=AX.X, op=ALU.add)\
                    .then_inc(s("summed").sem, 1)

            def normalise(n, g):
                dve.wait_ge(s("summed").sem, s("summed").at(n + 1))
                nc.vector.reciprocal(rsum[:, g % 2, 1, :], rsum[:, g % 2, 0, :]).then_inc(s("sums_inverted").sem, 1)
                dve.wait_ge(s("sums_inverted").sem, s("sums_inverted").at(n + 1))
                eh = by_head(e[:, g % 4, :])
                nc.vector.tensor_tensor(eh, eh, rsum[:, g % 2, 1, :].unsqueeze(2).broadcast_to([P, H, SC]), ALU.mult)\
                    .then_inc(s("normed").sem, 1)

            def add(n):
                dve.wait_ge(s("attn_proj").sem, s("attn_proj").at(n + 1))
                xc = x_sb[:, bass.ds(n, 1), :].rearrange("p a d -> p (a d)")
                nc.vector.tensor_tensor(xc, xc, psC[:, 0:P], ALU.add).then_inc(s("x_added").sem, 1)

            def step(j, n, g):
                if has(n + 2, TILES):
                    largest(n + 2, g + 2)
                if has(n + 1, TILES):
                    sums(n + 1, g + 1)
                if has(n + 2, TILES):
                    shift(n + 2, g + 2)
                if has(n + 1, TILES):
                    normalise(n + 1, g + 1)
                if g % TPI == 1:
                    dve.wait_ge(s("bias_added").sem, s("bias_added").at(j + 1))
                if has(n - 1, TILES):
                    add(n - 1)
                if g % TPI == 1 and has(j + 2, ITERS):
                    normalised_x(j + 2, units_before(j, 0))
            dve.wait_ge(s("ln_rstd").sem, s("ln_rstd").at(1))
            normalised_x(0, 0)
            for par in range(2):
                dve.wait_ge(s("q_ready").sem, s("q_ready").at(3 + par))
                nc.vector.tensor_tensor(nl[:, par::2, :], psS[par][:].rearrange("p (h d) -> p h d", h=PAIRS), nh[:, par::2, :],
                                        ALU.subtract).then_inc(s("n_split").sem, 1)
            normalised_x(1, 1)
            for n in range(2):
                largest(n, n)
                shift(n, n)
            sums(0, 0)
            normalise(0, 0)
            dve.wait_ge(s("ln_rstd").sem, s("ln_rstd").at(RSTD_PARTS))
            run_bodies(dve, step)
            add(TILES - 1)

    n4, n1 = ITERS * TPI, ITERS
    pr.end_block(dict(**ahead.counts, x_loaded=16, weights_qk=32, inputs=N_INPUTS, ln_var=1, ln_rstd=RSTD_PARTS, stats_ready=1, pool_steps=1, dve_steps=2, ctx_ready=n1, ctx_high=n1, ctx_split=n1, n_split=2, ln_out=n1,
                      bias_added=n1, front_out=PER_ITER * n1, front_ready=PER_ITER * n1, q_proj=4, q_ready=4, scores=n4, maxed=n4,
                      shifted=n4, probs=n4, summed=n4, sums_inverted=n4, normed=n4, probs_T=n4, pT_ready=n4, attn_proj=n4,
                      x_added=n4))


def narrow_attention_weights(nc, ctx, dram, layer):
    sb = buffers(nc, ctx, f"a{layer}w")
    ws, cols, bo = sb("ws", [P, 4, P]), sb("cols", [P, 3]), sb("bo", [P, P])
    return Ahead({f"ws{layer}": ws, f"cols{layer}": cols, f"bo{layer}": bo},
                 [(ws[:], dram[f"L{layer}_w4"]), (cols[:], dram[f"L{layer}_cols"]),
                  (bo[:], dram[f"L{layer}_bo"].partition_broadcast(P))])


def narrow_attention(pr, x_sb, common, dram, layer, wt, ahead):
    nc, s = pr.nc, pr.sig
    masked = layer == 2
    dv = P // H
    vw = 2 * (dv + 1)
    T4 = TPI * P
    with ExitStack() as ctx:
        def sb(name, shape, dt=F32):
            return ctx.enter_context(nc.sbuf_tensor(f"{name}_a{layer}", shape, dt))
        w = dict(common)
        ident, ctxT = common["ident"], common["ctxT"]
        ws, cols, bo = (wt[f"{k}{layer}"] for k in ("ws", "cols", "bo"))
        wq, wk, wv, wo = (ws[:, k, :] for k in range(4))
        if masked:
            maskf = sb("maskf", [P, TPI, SC], I32)
            maskb = sb("maskb", [P, 2, TPI, SC], BF16)
        cb = sb("cb", [P, BPI, P])
        kT = sb("kT", [P, BPI, SC])
        kTh, kTl = sb("kTh", [P, BPI, SC], F32R), sb("kTl", [P, BPI, SC], F32R)
        khath, khatl = sb("khath", [P, 2, BPI, H, SC], F32R), sb("khatl", [P, 2, BPI, H, SC], F32R)
        vb = sb("vb", [P, 2, BPI, PAIRS, vw])
        xn, xT = sb("xn", [P, TPI, P]), sb("xT", [P, T4])
        qh, ql = sb("qh", [P, 2, T4], F32R), sb("ql", [P, 2, T4], F32R)
        shifted, probs = sb("shifted", [P, 2, KEYS]), sb("probs", [P, 2, KEYS])
        smax, rsum = sb("smax", [P, 2, H]), sb("rsum", [P, 2, H])
        heads, headsT = sb("heads", [P, 2, P]), sb("headsT", [P, 2, P])
        w.update(ln_buffers(sb))
        psS = [ctx.enter_context(nc.psum_tensor(f"psS{c}_a{layer}", [P, KEYS], F32)) for c in range(2)]
        psF = [ctx.enter_context(nc.psum_tensor(f"psF{c}_a{layer}", [P, T4], F32)) for c in range(2)]
        psC = [ctx.enter_context(nc.psum_tensor(f"psC{c}_a{layer}", [P, T4], F32)) for c in range(2)]
        block = ctx.enter_context(nc.Block())
        BODY = 2 * TPI

        def run_bodies(eng, body):
            body(0, True, False)
            with eng.Fori(1, ITERS // 2 - 1) as i:
                body(i, False, False)
            body(ITERS // 2 - 1, False, True)

        def spread_keys(eng, part, khat, q, b):
            return eng.tensor_tensor(khat[:, q, b, :, :], part[:, b, :].unsqueeze(1).broadcast_to([P, H, SC]),
                                     common["headmask"][:].unsqueeze(2).broadcast_to([P, H, SC]), ALU.mult)

        def by_head(ap):
            return ap.rearrange("p (h k) -> p h k", h=H)

        @block.sync
        def _(sp):
            def load_mask(j):
                sp.wait_ge(s("mask_ready").sem, s("mask_ready").at(j))
                sp.dma_start(maskf[:], dram["mask"][:, bass.ds(j * TPI, TPI), :]).then_inc(s("wraw").sem, 16)
            if masked:
                load_mask(0)
            ahead.start(pr, sp)
            if masked:
                with sp.Fori(1, ITERS) as i:
                    load_mask(i)

        @block.gpsimd
        def _(pool):
            nc.gpsimd.memset(vb[:], 0.0).then_inc(s("pool_steps").sem, 1)
            pool.wait_ge(s("pool_steps").sem, s("pool_steps").at(1))
            for par in range(2):
                ins = nc.gpsimd.memset(vb[par * SC:(par + 1) * SC, :, :, :, par * (dv + 1) + dv:par * (dv + 1) + dv + 1], 1.0)
                ins.then_inc(s("pool_steps").sem, 1)
                pool.wait_ge(s("pool_steps").sem, s("pool_steps").at(2 + par))

            def add_bias(j):
                pool.wait_ge(s("ln_out").sem, s("ln_out").at(j + 1))
                x4 = tile4(x_sb, j)
                nc.gpsimd.tensor_tensor(x4, x4, bo[:].unsqueeze(1).broadcast_to([P, TPI, P]), ALU.add)\
                    .then_inc(s("bias_added").sem, 1)

            def front(j, q, first=False):
                pool.wait_ge(s("kv_proj").sem, s("kv_proj").at(j))
                nc.gpsimd.tensor_copy(cb[:].rearrange("p b k -> p (b k)"), ctxT[:, bass.ds(j * (BPI * P), BPI * P)])\
                    .then_inc(s("ctx_ready").sem, 1)
                layernorm_pool(pr, pool, j + 1, w)
                if not first:
                    add_bias(j)
                pool.wait_ge(s("kv_ready").sem, s("kv_ready").at(j + 1))
                pool.wait_ge(s("scores").sem, s("scores").at((j - 1) * TPI))
                nc.gpsimd.tensor_tensor(kTl[:], kT[:], kTh[:], ALU.subtract).then_inc(s("k_split").sem, 1)
                pool.wait_ge(s("k_split").sem, s("k_split").at(j + 1))
                for part, khat in ((kTl, khatl),) if first else ((kTh, khath), (kTl, khatl)):
                    for b in range(BPI):
                        ins = spread_keys(nc.gpsimd, part, khat, q, b)
                ins.then_inc(s("khat_ready").sem, 1)
                if first:
                    add_bias(j)
            front(0, 0, True)
            front(1, 1)
            with pool.Fori(1, ITERS // 2) as i:
                front(2 * i, 0)
                front(2 * i + 1, 1)
            ahead.split(pr, pool)

        @block.scalar
        def _(act):
            act.wait_ge(s("pool_steps").sem, s("pool_steps").at(3))

            def front_kv(j, q):
                act.wait_ge(s("kv_proj").sem, s("kv_proj").at(j + 1))
                act.wait_ge(s("khat_ready").sem, s("khat_ready").at(j))
                act.wait_ge(s("heads_out").sem, s("heads_out").at((j - 1) * TPI))
                for b in range(BPI):
                    for part in (kT, kTh):
                        nc.scalar.activation(part[:, b, :], psF[1][:, 2 * b * P:2 * b * P + SC], ACT.Identity, bias=cols[:, 1:2])
                    v = psF[1][:, (2 * b + 1) * P:(2 * b + 2) * P].rearrange("p (q a d) -> p q a d", a=2, d=dv)
                    for par in range(2):
                        r = slice(par * SC, (par + 1) * SC)
                        ins = nc.scalar.activation(vb[r, q, b, :, par * (dv + 1):par * (dv + 1) + dv], v[r, :, par, :], ACT.Copy)
                ins.then_inc(s("kv_ready").sem, 1)

            def front_x(j):
                act.wait_ge(s("ln_T").sem, s("ln_T").at(j + 1))
                nc.scalar.activation(xT[:], psF[0][:], ACT.Copy).then_inc(s("xT_ready").sem, 1)

            def front_q(j, q):
                act.wait_ge(s("q_proj").sem, s("q_proj").at(j + 1))
                act.wait_ge(s("scores").sem, s("scores").at((j - 1) * TPI))
                nc.scalar.activation(qh[:, q, :], psF[1][:], ACT.Identity, bias=cols[:, 0:1]).then_inc(s("q_ready").sem, 1)

            def exp(n, g):
                act.wait_ge(s("shifted_T").sem, s("shifted_T").at(n + 1))
                act.wait_ge(s("heads_out").sem, s("heads_out").at(n - 1))
                nc.scalar.activation(probs[:, g % 2, :], psS[g % 2][:], ACT.Exp, scale=float(dv) ** -0.5)\
                    .then_inc(s("probs").sem, 1)

            def store_heads(n, g):
                act.wait_ge(s("heads_T").sem, s("heads_T").at(n + 1))
                nc.scalar.activation(headsT[:, g % 2, :], psC[g % 2][:, 256:256 + P], ACT.Identity, bias=cols[:, 2:3])\
                    .then_inc(s("headsT_ready").sem, 1)

            def body(i, first, last):
                for g in range(BODY):
                    n, c, p = i * BODY + g, g % TPI, g // TPI
                    j = 2 * i + p
                    exp(n, g)
                    if not (last and p):
                        if c == 0:
                            front_kv(j + 1, 1 - p)
                            front_x(j + 1)
                        elif c == 1:
                            front_q(j + 1, 1 - p)
                    if g or not first:
                        store_heads(n - 1, g - 1)
            front_kv(0, 0)
            front_x(0)
            front_q(0, 0)
            run_bodies(act, body)
            store_heads(TILES - 1, TILES - 1)
            ahead.convert(pr, act)

        @block.tensor
        def _(pe):

            def front_kv(j):
                pe.wait_ge(s("ctx_ready").sem, s("ctx_ready").at(j + 1))
                pe.wait_ge(s("q_split").sem, s("q_split").at(j))
                for b in range(BPI):
                    nc.tensor.matmul(psF[1][:, 2 * b * P:2 * b * P + SC], wk, cb[:, b, 0:SC], start=True, stop=True)
                    ins = nc.tensor.matmul(psF[1][:, (2 * b + 1) * P:(2 * b + 2) * P], cb[:, b, :], wv, start=True, stop=True)
                ins.then_inc(s("kv_proj").sem, 1)

            def front_x(j):
                pe.wait_ge(s("xT_ready").sem, s("xT_ready").at(j))
                pe.wait_ge(s("ln_out").sem, s("ln_out").at(j + 1))
                for c in range(TPI):
                    ins = nc.tensor.transpose(psF[0][:, c * P:(c + 1) * P], xn[:, c, :], ident[:])
                ins.then_inc(s("ln_T").sem, 1)

            def front_q(j):
                pe.wait_ge(s("kv_ready").sem, s("kv_ready").at(j + 1))
                pe.wait_ge(s("xT_ready").sem, s("xT_ready").at(j + 1))
                nc.tensor.matmul(psF[1][:], wq, xT[:], start=True, stop=True).then_inc(s("q_proj").sem, 1)

            def scores(n, g):
                c, p = g % TPI, g // TPI % 2
                pe.wait_ge(s("probs").sem, s("probs").at(n - 1))
                for h in range(2):
                    out = psS[g % 2][:, h * 512:(h + 1) * 512]
                    if masked:
                        nc.tensor.matmul(out, common["identb"][:], maskb[:, p, c, :].unsqueeze(1).broadcast_to([P, 8, SC]),
                                         start=True, stop=False)
                    for m, (q_part, k_part) in enumerate(((ql, khath), (qh, khatl), (qh, khath))):
                        ins = nc.tensor.matmul(out, q_part[:, p, c * P:(c + 1) * P], k_part[:, p, c // 2, 8 * h:8 * h + 8, :],
                                               start=m == 0 and not masked, stop=m == 2)
                ins.then_inc(s("scores").sem, 1)

            def front_done(j):
                pe.wait_ge(s("q_split").sem, s("q_split").at(j + 1))
                pe.wait_ge(s("khat_ready").sem, s("khat_ready").at(j + 1))
                if masked:
                    pe.wait_ge(s("mask_ready").sem, s("mask_ready").at(j + 1))

            def shifted_T(n, g):
                pe.wait_ge(s("shifted").sem, s("shifted").at(n + 1))
                for k in range(PAIRS):
                    ins = nc.tensor.transpose(psS[g % 2][:, k * P:(k + 1) * P], shifted[:, g % 2, k * P:(k + 1) * P], ident[:])
                ins.then_inc(s("shifted_T").sem, 1)

            def heads_out(n, g):
                pe.wait_ge(s("probs").sem, s("probs").at(n + 1))
                pe.wait_ge(s("x_added").sem, s("x_added").at(n - 1))
                for k in range(PAIRS):
                    ins = nc.tensor.matmul(psC[g % 2][:, k * vw:(k + 1) * vw], probs[:, g % 2, k * P:(k + 1) * P],
                                           vb[:, g // TPI, g % TPI // 2, k, :], start=True, stop=True)
                ins.then_inc(s("heads_out").sem, 1)

            def heads_T(n, g):
                pe.wait_ge(s("heads_norm").sem, s("heads_norm").at(n + 1))
                nc.tensor.transpose(psC[g % 2][:, 256:256 + P], heads[:, g % 2, :], ident[:]).then_inc(s("heads_T").sem, 1)

            def project(n, g):
                pe.wait_ge(s("headsT_ready").sem, s("headsT_ready").at(n + 1))
                nc.tensor.matmul(psC[g % 2][:, 384:384 + P], headsT[:, g % 2, :], wo, start=True, stop=True)\
                    .then_inc(s("attn_proj").sem, 1)

            def body(i, first, last):
                for g in range(BODY):
                    n, c, p = i * BODY + g, g % TPI, g // TPI
                    j = 2 * i + p
                    front = not (last and p)
                    shifted_T(n, g)
                    if g > 1 or not first:
                        project(n - 2, g - 2)
                    if g or not first:
                        heads_out(n - 1, (g - 1) % BODY)
                    if front and c == 0:
                        front_kv(j + 1)
                        front_x(j + 1)
                    if front and c == 1:
                        front_q(j + 1)
                    if front and c == 2:
                        front_done(j + 1)
                    if front or c < 2:
                        scores(n + 2, (g + 2) % BODY)
                    if g or not first:
                        heads_T(n - 1, g - 1)
            front_kv(0)
            front_x(0)
            front_q(0)
            front_done(0)
            pe.wait_ge(s("khat_first").sem, s("khat_first").at(1))
            scores(0, 0)
            scores(1, 1)
            run_bodies(pe, body)
            n = TILES - 1
            project(n - 1, n - 1)
            heads_out(n, n % BODY)
            heads_T(n, n)
            project(n, n)

        @block.vector
        def _(dve):
            def front_ln(j):
                steps = Steps(dve, s("dve_steps"), j, LN_STEPS)
                layernorm_vector(pr, dve, steps, j, w, tile4(x_sb, j), xn)
                steps.end()

            def front_mask(j, q):
                dve.wait_ge(s("wraw").sem, s("wraw").at((j + 1) * 16))
                dve.wait_ge(s("scores").sem, s("scores").at((j - 1) * TPI))
                nc.vector.tensor_scalar(maskb[:, q, :, :], maskf[:], 0.0, NEG, ALU.is_equal, ALU.mult)\
                    .then_inc(s("mask_ready").sem, 1)

            def front_xn(j):
                dve.wait_ge(s("ln_rstd").sem, s("ln_rstd").at(j + 1))
                dve.wait_ge(s("ln_T").sem, s("ln_T").at(j))
                layernorm_apply(pr, dve, w, tile4(x_sb, j), xn).then_inc(s("ln_out").sem, 1)

            def front_q(j, q):
                dve.wait_ge(s("q_ready").sem, s("q_ready").at(j + 1))
                nc.vector.scalar_tensor_tensor(ql[:, q, :], psF[1][:], cols[:, 0:1], qh[:, q, :], ALU.add, ALU.subtract)\
                    .then_inc(s("q_split").sem, 1)

            def largest(n, g):
                dve.wait_ge(s("scores").sem, s("scores").at(n + 1))
                nc.vector.tensor_reduce(smax[:, g % 2, :], by_head(psS[g % 2][:]), axis=AX.X, op=ALU.max)\
                    .then_inc(s("maxed").sem, 1)

            def shift(n, g):
                dve.wait_ge(s("maxed").sem, s("maxed").at(n + 1))
                dve.wait_ge(s("shifted_T").sem, s("shifted_T").at(n - 1))
                nc.vector.tensor_tensor(by_head(shifted[:, g % 2, :]), by_head(psS[g % 2][:]),
                                        smax[:, g % 2, :].unsqueeze(2).broadcast_to([P, H, SC]), ALU.subtract)\
                    .then_inc(s("shifted").sem, 1)

            def normalise(n, g):
                dve.wait_ge(s("heads_out").sem, s("heads_out").at(n + 1))
                o = psC[g % 2][:, 0:H * (dv + 1)].rearrange("p (h d) -> p h d", h=H)
                nc.vector.reciprocal(rsum[:, g % 2, :], o[:, :, dv]).then_inc(s("sums_inverted").sem, 1)
                dve.wait_ge(s("sums_inverted").sem, s("sums_inverted").at(n + 1))
                nc.vector.tensor_tensor(heads[:, g % 2, :].rearrange("p (h d) -> p h d", h=H), o[:, :, 0:dv],
                                        rsum[:, g % 2, :].unsqueeze(2).broadcast_to([P, H, dv]), ALU.mult)\
                    .then_inc(s("heads_norm").sem, 1)

            def add(n, g):
                dve.wait_ge(s("attn_proj").sem, s("attn_proj").at(n + 1))
                xc = x_sb[:, bass.ds(n, 1), :].rearrange("p a d -> p (a d)")
                nc.vector.tensor_tensor(xc, xc, psC[g % 2][:, 384:384 + P], ALU.add).then_inc(s("x_added").sem, 1)

            def body(i, first, last):
                for g in range(BODY):
                    n, c, p = i * BODY + g, g % TPI, g // TPI
                    j = 2 * i + p
                    if not (last and g == BODY - 1):
                        largest(n + 1, g + 1)
                    if g > 1 or not first:
                        if c == 2:
                            dve.wait_ge(s("bias_added").sem, s("bias_added").at(j + 1))
                        add(n - 2, g - 2)
                    if not (last and g == BODY - 1):
                        shift(n + 1, g + 1)
                    if g or not first:
                        normalise(n - 1, g - 1)
                    if c == 1 and not (last and p):
                        front_q(j + 1, 1 - p)
                    if masked and c == 0 and not (last and p):
                        front_mask(j + 1, 1 - p)
                    if not last and c == 2:
                        front_ln(j + 2)
                    if not last and c == 3:
                        front_xn(j + 2)
            for j in range(2):
                front_ln(j)
                if masked and not j:
                    front_mask(0, 0)
                front_xn(j)
                if not j:
                    dve.wait_ge(s("kv_ready").sem, s("kv_ready").at(1))
                    for b in range(BPI):
                        ins = spread_keys(nc.vector, kTh, khath, 0, b)
                    ins.then_inc(s("khat_first").sem, 1)
                    front_q(0, 0)
            largest(0, 0)
            shift(0, 0)
            run_bodies(dve, body)
            n = TILES - 1
            add(n - 1, n - 1)
            normalise(n, n)
            add(n, n)

    n4, n1 = ITERS * TPI, ITERS
    counts = dict(**ahead.counts, kv_proj=n1, ctx_ready=n1, ln_var=n1, ln_rstd=n1, kv_ready=n1, ln_out=n1, bias_added=n1,
                  ln_T=n1, xT_ready=n1, q_proj=n1, khat_first=1, q_ready=n1, q_split=n1, k_split=n1, khat_ready=n1, scores=n4, maxed=n4, shifted=n4, shifted_T=n4,
                  probs=n4, heads_out=n4, sums_inverted=n4, heads_norm=n4, heads_T=n4, headsT_ready=n4, attn_proj=n4,
                  x_added=n4, pool_steps=3, dve_steps=n1 * LN_STEPS)
    if masked:
        counts.update(mask_ready=n1, wraw=16 * n1)
    pr.end_block(counts)


def first_max(nc, steps, src, onehot, top, scratch, desc):
    shape = list(src.shape)
    steps.done(nc.vector.tensor_reduce(top, src, axis=AX.X, op=ALU.max))
    steps.done(nc.vector.tensor_tensor(scratch, src, top.unsqueeze(2).broadcast_to(shape), ALU.is_equal))
    steps.done(nc.vector.tensor_tensor(scratch, scratch, desc.unsqueeze(1).broadcast_to(shape), ALU.mult))
    steps.done(nc.vector.tensor_reduce(top, scratch, axis=AX.X, op=ALU.max))
    steps.done(nc.vector.tensor_tensor(onehot, desc.unsqueeze(1).broadcast_to(shape), top.unsqueeze(2).broadcast_to(shape),
                                       ALU.is_equal))


def three_parts(nc, steps, src, parts, hi, rest, mid, n):
    steps.done(nc.vector.tensor_copy(hi, src))
    nc.vector.tensor_copy(parts[:, :, 0:n], hi)
    steps.done(nc.vector.tensor_tensor(rest, src, hi, ALU.subtract))
    steps.done(nc.vector.tensor_copy(mid, rest))
    nc.vector.tensor_copy(parts[:, :, n:2 * n], mid)
    return nc.vector.tensor_tensor(parts[:, :, 2 * n:3 * n], rest, mid, ALU.subtract)


def layer0_ffn_weights(nc, ctx, dram):
    sb = buffers(nc, ctx, "f0w")
    E, CH = 8, 4
    t = dict(wd=sb("wd", [P, CH * P]), wu=sb("wu", [P, CH, P]), wr=sb("wr", [P, E]), br=sb("br", [P, E]),
             bup=sb("bup", [E, P]), cols=sb("cols", [P, 6 + CH]), desc=sb("desc", [P, E]))
    return Ahead(t, [(t["wd"][:], dram["F0_wd"]), (t["wu"][:], dram["F0_wu"]), (t["wr"][:], dram["F0_wr"]),
                     (t["cols"][:], dram["F0_cols"]), (t["bup"][:], dram["F0_bup"]),
                     (t["br"][:], dram["F0_br"].partition_broadcast(P)), (t["desc"][:], dram["desc8"].partition_broadcast(P))])


def layer0_ffn(pr, x_sb, common, wt):
    nc, s = pr.nc, pr.sig
    E, CH = 8, 4
    T4 = TPI * P
    with ExitStack() as ctx:
        def sb(name, shape, dt=F32):
            return ctx.enter_context(nc.sbuf_tensor(f"{name}_f0", shape, dt))
        ident = common["ident"]
        wd, wu, wr, br, bup, cols, desc = (wt[k] for k in ("wd", "wu", "wr", "br", "bup", "cols", "desc"))
        bn = sb("bn", [P, 4])
        xn, zT = sb("xn", [P, TILES, P]), sb("zT", [P, TILES * P])
        zsum, zs, zbn = sb("zsum", [P, TILES]), sb("zs", [P, B]), sb("zbn", [P, B, P])
        lg, ex, oh, tmp = (sb(n, [P, B, E]) for n in ("lg", "ex", "oh", "tmp"))
        top, gsum, gate = (sb(n, [P, B]) for n in ("top", "gsum", "gate"))
        sel, bsel = sb("sel", [P, B, CH]), sb("bsel", [P, B, CH])
        gd, gb, ones = sb("gd", [E, B]), sb("gb", [E, B, P]), sb("ones8", [E, P])
        hT = sb("hT", [P, 2, CH, S])
        w = all_ln_buffers(sb)
        psH = [ctx.enter_context(nc.psum_tensor(f"psH{c}_f0", [P, CH * S], F32)) for c in range(2)]
        psO = [ctx.enter_context(nc.psum_tensor(f"psO{c}_f0", [P, 512], F32)) for c in range(2)]
        psT = [ctx.enter_context(nc.psum_tensor(f"psT{c}_f0", [P, T4], F32)) for c in range(2)]
        NST = 4 + 4 + 1 + 2 + 2 + 5 + 1 + 2
        block = ctx.enter_context(nc.Block())

        @block.gpsimd
        def _(pool):
            nc.gpsimd.memset(ones[:], 1.0)
            all_ln_pool(pr, pool, w)
            pool.wait_ge(s("act_steps").sem, s("act_steps").at(1))
            nc.gpsimd.tensor_tensor(bn[:, 1:2], bn[:, 0:1], common["mhalf"][:, 0:1], ALU.pow).then_inc(s("pool_steps").sem, 1)
            all_rstd(pr, pool, w, 2)

        @block.scalar
        def _(act):
            nc.scalar.activation(bn[:, 0:1], cols[:, 0:1], ACT.Copy, bias=EPS).then_inc(s("act_steps").sem, 1)
            for i in range(ITERS):
                act.wait_ge(s("ln_T").sem, s("ln_T").at(i + 1))
                for c in range(TPI):
                    n = i * TPI + c
                    ins = nc.scalar.activation(zT[:, n * P:(n + 1) * P], psT[i % 2][:, c * P:(c + 1) * P], ACT.Identity,
                                               scale=cols[:, 4:5], bias=cols[:, 5:6], accum_out=zsum[:, n:n + 1])
                ins.then_inc(s("z_ready").sem, 1)
            act.wait_ge(s("gate_logits").sem, s("gate_logits").at(2))
            nc.scalar.activation(ex[:], lg[:], ACT.Exp).then_inc(s("gate_exp").sem, 1)
            act.wait_ge(s("gate_ready").sem, s("gate_ready").at(1))

            def relu(b, k):
                act.wait_ge(s("ffn_out").sem, s("ffn_out").at(b - 1))
                act.wait_ge(s("hidden").sem, s("hidden").at(b + 1))
                for j in range(CH):
                    col = [t[:, bass.ds(b, 1), j:j + 1].rearrange("p a j -> p (a j)") for t in (sel, bsel)]
                    ins = nc.scalar.activation(hT[:, k, j, :], psH[k][:, j * S:(j + 1) * S], ACT.Relu, scale=col[0], bias=col[1])
                ins.then_inc(s("hidden_ready").sem, 1)
            with act.Fori(0, B // 2) as i:
                relu(2 * i, 0)
                relu(2 * i + 1, 1)

        @block.tensor
        def _(pe):
            for i in range(ITERS):
                pe.wait_ge(s("ln_out").sem, s("ln_out").at(i + 1))
                pe.wait_ge(s("z_ready").sem, s("z_ready").at(i - 1))
                for c in range(TPI):
                    ins = nc.tensor.transpose(psT[i % 2][:, c * P:(c + 1) * P], xn[:, i * TPI + c, :], ident[:])
                ins.then_inc(s("ln_T").sem, 1)
            pe.wait_ge(s("scaled").sem, s("scaled").at(1))
            for b in range(B):
                ins = nc.tensor.matmul(psO[0][:, b * E:(b + 1) * E], zbn[:, b, :], wr[:], start=True, stop=True)
            ins.then_inc(s("gate_logits").sem, 1)

            def hidden(b, k):
                pe.wait_ge(s("hidden_ready").sem, s("hidden_ready").at(b - 1))
                for j in range(CH):
                    ins = nc.tensor.matmul(psH[k][:, j * S:(j + 1) * S], wd[:, j * P:(j + 1) * P], zT[:, bass.ds(b * S, S)],
                                           start=True, stop=True)
                ins.then_inc(s("hidden").sem, 1)

            def up(b, k):
                pe.wait_ge(s("hidden_ready").sem, s("hidden_ready").at(b + 1))
                pe.wait_ge(s("x_added").sem, s("x_added").at(b - 1))
                for t in range(S // P):
                    out = psO[k][:, t * P:(t + 1) * P]
                    for j in range(CH):
                        nc.tensor.matmul(out, hT[:, k, j, t * P:(t + 1) * P], wu[:, j, :], start=j == 0, stop=False)
                    ins = nc.tensor.matmul(out, ones[:], gb[:, bass.ds(b, 1), :].rearrange("e a d -> e (a d)"), start=False, stop=True)
                ins.then_inc(s("ffn_out").sem, 1)
            hidden(0, 0)
            pe.wait_ge(s("gate_ready").sem, s("gate_ready").at(1))
            with pe.Fori(0, B // 2 - 1) as i:
                for k in range(2):
                    hidden(2 * i + k + 1, 1 - k)
                    up(2 * i + k, k)
            hidden(B - 1, 1)
            up(B - 2, 0)
            up(B - 1, 1)

        @block.vector
        def _(dve):
            st = Steps(dve, s("dve_steps"), 0, NST)
            all_ln_vector(pr, dve, st.done, w, x_sb)
            for n in range(TILES):
                wait_rstd(pr, dve, n)
                ins = nc.vector.tensor_scalar(xn[:, n, :], x_sb[:, n, :], w["mean"][:, n:n + 1], w["rstd"][:, n:n + 1],
                                              ALU.subtract, ALU.mult)
            st.done(ins)
            all_ln_vector(pr, dve, st.done, w, xn, 2)
            dve.wait_ge(s("pool_steps").sem, s("pool_steps").at(2))
            st.done(nc.vector.tensor_tensor(bn[:, 1:2], bn[:, 1:2], cols[:, 1:2], ALU.mult))
            nc.vector.tensor_scalar(bn[:, 2:3], bn[:, 1:2], 1.0 / S, None, ALU.mult)
            st.done(nc.vector.tensor_tensor(bn[:, 3:4], bn[:, 1:2], cols[:, 3:4], ALU.mult))
            st.done(nc.vector.tensor_tensor(bn[:, 3:4], cols[:, 2:3], bn[:, 3:4], ALU.subtract))
            for n in range(TILES):
                wait_rstd(pr, dve, n, 2)
                ins = nc.vector.tensor_scalar(xn[:, n, :], xn[:, n, :], w["mean"][:, n:n + 1], w["rstd"][:, n:n + 1],
                                              ALU.subtract, ALU.mult)
                if n % TPI == TPI - 1:
                    ins.then_inc(s("ln_out").sem, 1)
            dve.wait_ge(s("z_ready").sem, s("z_ready").at(ITERS))
            z2 = zsum[:].rearrange("p (b t) -> p b t", t=2)
            st.done(nc.vector.tensor_tensor(zs[:], z2[:, :, 0], z2[:, :, 1], ALU.add))
            nc.vector.tensor_scalar(zbn[:], zs[:].unsqueeze(2).broadcast_to([P, B, P]), bn[:, 2:3], bn[:, 3:4],
                                    ALU.mult, ALU.add).then_inc(s("scaled").sem, 1)
            full = [P, B, E]
            dve.wait_ge(s("gate_logits").sem, s("gate_logits").at(1))
            lps = psO[0][:, 0:B * E].rearrange("p (b e) -> p b e", e=E)
            st.done(nc.vector.tensor_tensor(lg[:], lps, br[:].unsqueeze(1).broadcast_to(full), ALU.add))
            st.done(nc.vector.tensor_reduce(top[:], lg[:], axis=AX.X, op=ALU.max))
            nc.vector.tensor_tensor(lg[:], lg[:], top[:].unsqueeze(2).broadcast_to(full), ALU.subtract)\
                .then_inc(s("gate_logits").sem, 1)
            dve.wait_ge(s("gate_logits").sem, s("gate_logits").at(2))
            dve.wait_ge(s("gate_exp").sem, s("gate_exp").at(1))
            st.done(nc.vector.tensor_reduce(gsum[:], ex[:], axis=AX.X, op=ALU.add))
            st.done(nc.vector.reciprocal(gate[:], gsum[:]))
            first_max(nc, st, lg[:], oh[:], top[:], tmp[:], desc[:])
            st.done(nc.vector.tensor_tensor(oh[:], oh[:], gate[:].unsqueeze(2).broadcast_to(full), ALU.mult))
            ohp = oh[:].rearrange("p b (j a) -> p b j a", a=2)
            nc.vector.tensor_copy(sel[0:64, :, :], ohp[0:64, :, :, 0])
            nc.vector.tensor_tensor(tmp[0:E, :, :], oh[0:E, :, :], ident[0:E, 0:E].unsqueeze(1).broadcast_to([E, B, E]), ALU.mult)
            st.done(nc.vector.tensor_copy(sel[64:128, :, :], ohp[64:128, :, :, 1]))
            nc.vector.tensor_tensor(bsel[:], sel[:], cols[:, 6:6 + CH].unsqueeze(1).broadcast_to([P, B, CH]), ALU.mult)
            st.done(nc.vector.tensor_reduce(gd[:], tmp[0:E, :, :], axis=AX.X, op=ALU.add))
            nc.vector.tensor_tensor(gb[:], bup[:].unsqueeze(1).broadcast_to([E, B, P]), gd[:].unsqueeze(2).broadcast_to([E, B, P]),
                                    ALU.mult).then_inc(s("gate_ready").sem, 1)
            st.end()
            with dve.Fori(0, B // 2) as i:
                for k in range(2):
                    b = 2 * i + k
                    dve.wait_ge(s("ffn_out").sem, s("ffn_out").at(b + 1))
                    x2 = x_sb[:, bass.ds(b * 2, 2), :]
                    nc.vector.tensor_tensor(x2, x2, psO[k][:, 0:S].rearrange("p (c d) -> p c d", d=P), ALU.add)\
                        .then_inc(s("x_added").sem, 1)

    pr.end_block(dict(act_steps=1, pool_steps=2, dve_steps=NST, ln_var=2, ln_rstd=2 * RSTD_PARTS, stats_ready=2,
                      ln_out=ITERS, ln_T=ITERS, z_ready=ITERS, scaled=1, gate_logits=2, gate_exp=1, gate_ready=1,
                      hidden=B, hidden_ready=B, ffn_out=B, x_added=B))


def layer1_ffn_weights(nc, ctx, dram):
    sb = buffers(nc, ctx, "f1w")
    E, NE, CH = L1_E, L1_E + 1, L1_CH
    t = dict(w1=sb("w1", [P, L1_ALL]), w3=sb("w3", [P, L1_ALL]), w2=sb("w2", [P, CH, P]), cols=sb("cols", [P, 2 * CH]),
             gw=sb("gw", [P, E]), gb=sb("gb", [P, E]), desc=sb("desc", [P, E]), b2=sb("b2", [3 * NE, P]),
             self32=sb("self32", [3 * NE, L1_ALL]), selb=sb("selb", [3 * NE, L1_ALL], BF16))
    for k in ("w1", "w3"):
        t[k + "h"], t[k + "l"] = sb(k + "h", [P, L1_ALL], F32R), sb(k + "l", [P, L1_ALL], F32R)
    return Ahead(t, [(t["gw"][:], dram["F1_gw"]), (t["gb"][:], dram["F1_gb"].partition_broadcast(P)),
                     (t["desc"][:], dram["desc8"].partition_broadcast(P)), (t["cols"][:], dram["F1_cols"]),
                     (t["b2"][:], dram["F1_b2"]), (t["self32"][:], dram["F1_sel"]), (t["w1"][:], dram["F1_w1"]),
                     (t["w3"][:], dram["F1_w3"]), (t["w2"][:], dram["F1_w2"])],
                 [(t["selb"][:], t["self32"][:])], [(t[k][:], t[k + "h"][:], t[k + "l"][:]) for k in ("w1", "w3")])


def layer1_ffn(pr, x_sb, common, wt):
    nc, s = pr.nc, pr.sig
    E, NE, CH = L1_E, L1_E + 1, L1_CH
    T4 = TPI * P
    with ExitStack() as ctx:
        def sb(name, shape, dt=F32):
            return ctx.enter_context(nc.sbuf_tensor(f"{name}_f1", shape, dt))
        w = dict(common)
        ident = common["ident"]
        w1h, w1l, w3h, w3l, w2, cols, gw, gb, desc, b2, selb = (wt[k] for k in ("w1h", "w1l", "w3h", "w3l", "w2", "cols", "gw", "gb", "desc", "b2", "selb"))
        xn, xT = sb("xn", [P, TPI, P]), sb("xT", [P, 2, T4])
        xh, xl = sb("xh", [P, 2, T4], F32R), sb("xl", [P, 2, T4], F32R)
        lg, ex, bi, oh, oh2, tmp = (sb(n, [P, TPI, E]) for n in ("lg", "ex", "bi", "oh", "oh2", "tmp"))
        top, gs = sb("top", [P, TPI]), sb("gs", [P, TPI])
        rw, rest = sb("rw", [P, TPI, NE]), sb("rest", [P, TPI, NE])
        hi, mid = sb("hi", [P, TPI, NE], BF16), sb("mid", [P, TPI, NE], BF16)
        parts = sb("parts", [P, TPI, 3 * NE])
        rwT, rwTb = sb("rwT", [3 * NE, 2, T4]), sb("rwTb", [3 * NE, 2, T4], BF16)
        t3, g_, act_h, h = (sb(n, [P, 2, T4]) for n in ("t3", "g", "act_h", "h"))
        oT = sb("oT", [P, T4])
        w.update(ln_buffers(sb))
        psU = [ctx.enter_context(nc.psum_tensor(f"psU{k}_f1", [P, 2, T4], F32)) for k in range(2)]
        psR = [ctx.enter_context(nc.psum_tensor(f"psR{k}_f1", [P, T4], F32)) for k in range(2)]
        psO = ctx.enter_context(nc.psum_tensor("psO_f1", [P, T4], F32))
        psM = ctx.enter_context(nc.psum_tensor("psM_f1", [P, T4], F32))
        NST = LN_STEPS + 1 + 1 + 1 + 1 + 1 + 5 + 1 + 5 + 1 + 1 + 3
        rows = [min(P, L1_ALL - k * P) for k in range(CH)]
        block = ctx.enter_context(nc.Block())

        BODY = 2 * CH

        def run_bodies(eng, body):
            body(0, True, False)
            with eng.Fori(1, ITERS // 2 - 1) as i:
                body(i, False, False)
            body(ITERS // 2 - 1, False, True)

        @block.gpsimd
        def _(pool):
            nc.gpsimd.memset(rw[:], 1.0).then_inc(s("pool_steps").sem, 1)
            with pool.Fori(0, ITERS) as i:
                layernorm_pool(pr, pool, i + 1, w)

        @block.scalar
        def _(act):

            def front_x(j, q):
                act.wait_ge(s("ln_T").sem, s("ln_T").at(j + 1))
                nc.scalar.activation(xh[:, q, :], psM[:], ACT.Copy)
                nc.scalar.activation(xT[:, q, :], psM[:], ACT.Copy).then_inc(s("xT_ready").sem, 1)

            def front_exp(j):
                act.wait_ge(s("gate_logits").sem, s("gate_logits").at(2 * j + 2))
                nc.scalar.activation(ex[:], lg[:], ACT.Exp).then_inc(s("gate_exp").sem, 1)

            def front_parts(j, q):
                act.wait_ge(s("gate_T").sem, s("gate_T").at(j + 1))
                nc.scalar.activation(rwT[:, q, :], psM[0:3 * NE, :], ACT.Copy)
                nc.scalar.activation(rwTb[:, q, :], psM[0:3 * NE, :], ACT.Copy).then_inc(s("gate_parts").sem, 1)

            def bias(n, g):
                r = slice(0, rows[g % CH])
                act.wait_ge(s("hidden").sem, s("hidden").at(n + 1))
                nc.scalar.activation(t3[r, g % 2, :], psU[g % 2][r, 1, :], ACT.Identity, bias=cols[r, CH + g % CH:CH + g % CH + 1])\
                    .then_inc(s("hidden_b").sem, 1)

            def silu(n, g):
                r = slice(0, rows[g % CH])
                act.wait_ge(s("hidden_mul").sem, s("hidden_mul").at(n + 1))
                nc.scalar.activation(act_h[r, g % 2, :], g_[r, g % 2, :], ACT.Silu).then_inc(s("hidden_act").sem, 1)

            def store_out(j):
                act.wait_ge(s("ffn_out").sem, s("ffn_out").at(j + 1))
                act.wait_ge(s("ffn_outT_ready").sem, s("ffn_outT_ready").at(j))
                nc.scalar.activation(oT[:], psO[:], ACT.Copy).then_inc(s("ffn_outT").sem, 1)

            def body(i, first, last):
                for p in range(2):
                    j = 2 * i + p
                    for k in range(CH):
                        g = p * CH + k
                        bias(i * BODY + g, g)
                        if g or not first:
                            silu(i * BODY + g - 1, (g - 1) % BODY)
                        if k == 1 and not (first and p == 0):
                            store_out(j - 1)
                        if not (last and p):
                            if k == 2:
                                front_x(j + 1, 1 - p)
                            if k == 5:
                                front_exp(j + 1)
                            if k == 11:
                                front_parts(j + 1, 1 - p)
            front_x(0, 0)
            front_exp(0)
            front_parts(0, 0)
            run_bodies(act, body)
            silu(ITERS * CH - 1, BODY - 1)
            store_out(ITERS - 1)

        @block.tensor
        def _(pe):
            pe.wait_ge(s("pool_steps").sem, s("pool_steps").at(1))

            def front_x(j):
                pe.wait_ge(s("ln_out").sem, s("ln_out").at(j + 1))
                for c in range(TPI):
                    ins = nc.tensor.transpose(psM[:, c * P:(c + 1) * P], xn[:, c, :], ident[:])
                ins.then_inc(s("ln_T").sem, 1)

            def front_logits(j, q):
                pe.wait_ge(s("xT_ready").sem, s("xT_ready").at(j + 1))
                for c in range(TPI):
                    ins = nc.tensor.matmul(psM[:, c * E:(c + 1) * E], xT[:, q, c * P:(c + 1) * P], gw[:], start=True, stop=True)
                ins.then_inc(s("gate_logits").sem, 1)

            def front_parts(j):
                pe.wait_ge(s("gate_ready").sem, s("gate_ready").at(j + 1))
                for c in range(TPI):
                    ins = nc.tensor.transpose(psM[0:3 * NE, c * P:(c + 1) * P], parts[:, c, :], ident[:])
                ins.then_inc(s("gate_T").sem, 1)

            def up(n, g):
                k, q = g % CH, g // CH % 2
                cs, r = slice(k * P, k * P + rows[k]), slice(0, rows[k])
                pe.wait_ge(s("hidden_mul").sem, s("hidden_mul").at(n - 1))
                for half, hi, lo in ((1, w3h, w3l), (0, w1h, w1l)):
                    for m, (wt_part, x_part) in enumerate(((lo, xh), (hi, xl), (hi, xh))):
                        ins = nc.tensor.matmul(psU[g % 2][r, half, :], wt_part[:, cs], x_part[:, q, :], start=m == 0, stop=m == 2)
                ins.then_inc(s("hidden").sem, 1)

            def spread(n, g):
                k, q = g % CH, g // CH
                pe.wait_ge(s("hidden_ready").sem, s("hidden_ready").at(n - 1))
                nc.tensor.matmul(psR[g % 2][0:rows[k], :], selb[:, k * P:k * P + rows[k]], rwTb[:, q, :], start=True, stop=True)\
                    .then_inc(s("gate_bcast").sem, 1)

            def down(n, g, j):
                k, q = g % CH, g // CH
                if k == 0:
                    pe.wait_ge(s("ffn_outT").sem, s("ffn_outT").at(j))
                    nc.tensor.matmul(psO[:], b2[:], rwT[:, q, :], start=True, stop=False)
                pe.wait_ge(s("hidden_ready").sem, s("hidden_ready").at(n + 1))
                ins = nc.tensor.matmul(psO[:], w2[0:rows[k], k, :], h[0:rows[k], g % 2, :], start=False, stop=k == CH - 1)
                if k == CH - 1:
                    ins.then_inc(s("ffn_out").sem, 1)

            def out_T(j):
                pe.wait_ge(s("ffn_outT").sem, s("ffn_outT").at(j + 1))
                for c in range(TPI):
                    ins = nc.tensor.transpose(psM[:, c * P:(c + 1) * P], oT[:, c * P:(c + 1) * P], ident[:])
                ins.then_inc(s("ffn_outT_ready").sem, 1)

            def body(i, first, last):
                for p in range(2):
                    j = 2 * i + p
                    front = not (last and p)
                    for k in range(CH):
                        g = p * CH + k
                        n = i * BODY + g
                        if not (last and g == BODY - 1):
                            if k == CH - 1:
                                pe.wait_ge(s("x_split").sem, s("x_split").at(j + 2))
                            up(n + 1, (g + 1) % BODY)
                        if front and k == 2:
                            front_x(j + 1)
                        if front and k == 4:
                            front_logits(j + 1, 1 - p)
                        if k == 7 and not (first and p == 0):
                            if front:
                                pe.wait_ge(s("gate_logits").sem, s("gate_logits").at(2 * j + 4))
                            out_T(j - 1)
                        if front and k == 11:
                            if not (first and p == 0):
                                pe.wait_ge(s("x_added").sem, s("x_added").at(j * TPI))
                            front_parts(j + 1)
                        if g > 1 or not first:
                            down(n - 2, (g - 2) % BODY, j - 1 if k < 2 else j)
                        if k == 0:
                            pe.wait_ge(s("gate_parts").sem, s("gate_parts").at(j + 1))
                        spread(n, g)
            front_x(0)
            front_logits(0, 0)
            pe.wait_ge(s("x_split").sem, s("x_split").at(1))
            up(0, 0)
            front_parts(0)
            run_bodies(pe, body)
            for back in (2, 1):
                down(ITERS * CH - back, BODY - back, ITERS - 1)
            pe.wait_ge(s("x_added").sem, s("x_added").at((ITERS - 1) * TPI))
            out_T(ITERS - 1)

        @block.vector
        def _(dve):
            dve.wait_ge(s("pool_steps").sem, s("pool_steps").at(1))
            g4 = [P, TPI, E]

            def front_steps(j, k0):
                st = Steps(dve, s("dve_steps"), j, NST)
                st.k = k0
                return st

            def front_ln(j):
                steps = front_steps(j, 0)
                layernorm_vector(pr, dve, steps, j, w, tile4(x_sb, j), xn)
                return steps

            def front_xn(j):
                dve.wait_ge(s("ln_rstd").sem, s("ln_rstd").at(j + 1))
                layernorm_apply(pr, dve, w, tile4(x_sb, j), xn).then_inc(s("ln_out").sem, 1)

            def front_split(j, q):
                dve.wait_ge(s("xT_ready").sem, s("xT_ready").at(j + 1))
                nc.vector.tensor_tensor(xl[:, q, :], xT[:, q, :], xh[:, q, :], ALU.subtract).then_inc(s("x_split").sem, 1)

            def front_shift(j, steps):
                dve.wait_ge(s("gate_logits").sem, s("gate_logits").at(2 * j + 1))
                lps = psM[:, 0:TPI * E].rearrange("p (c e) -> p c e", e=E)
                steps.done(nc.vector.tensor_reduce(top[:], lps, axis=AX.X, op=ALU.max))
                nc.vector.tensor_tensor(lg[:], lps, top[:].unsqueeze(2).broadcast_to(g4), ALU.subtract)\
                    .then_inc(s("gate_logits").sem, 1)

            def front_scores(j, steps):
                dve.wait_ge(s("gate_exp").sem, s("gate_exp").at(j + 1))
                steps.done(nc.vector.tensor_reduce(gs[:], ex[:], axis=AX.X, op=ALU.add))
                steps.done(nc.vector.reciprocal(gs[:], gs[:]))
                steps.done(nc.vector.tensor_tensor(ex[:], ex[:], gs[:].unsqueeze(2).broadcast_to(g4), ALU.mult))
                steps.done(nc.vector.tensor_tensor(bi[:], ex[:], gb[:].unsqueeze(1).broadcast_to(g4), ALU.add))

            def front_best(steps):
                first_max(nc, steps, bi[:], oh[:], top[:], tmp[:], desc[:])

            def front_second(steps):
                steps.done(nc.vector.scalar_tensor_tensor(bi[:], oh[:], -1e30, bi[:], ALU.mult, ALU.add))
                first_max(nc, steps, bi[:], oh2[:], top[:], tmp[:], desc[:])

            def front_parts(steps):
                steps.done(nc.vector.tensor_tensor(oh[:], oh[:], oh2[:], ALU.add))
                steps.done(nc.vector.tensor_tensor(rw[:, :, 0:E], oh[:], ex[:], ALU.mult))
                three_parts(nc, steps, rw[:], parts[:], hi[:], rest[:], mid[:], NE).then_inc(s("gate_ready").sem, 1)
                steps.end()

            def multiply(n, g):
                k = g % CH
                r = slice(0, rows[k])
                dve.wait_ge(s("hidden_b").sem, s("hidden_b").at(n + 1))
                nc.vector.scalar_tensor_tensor(g_[r, g % 2, :], psU[g % 2][r, 0, :], cols[r, k:k + 1], t3[r, g % 2, :],
                                               ALU.add, ALU.mult).then_inc(s("hidden_mul").sem, 1)

            def weigh(n, g):
                r = slice(0, rows[g % CH])
                dve.wait_ge(s("hidden_act").sem, s("hidden_act").at(n + 1))
                dve.wait_ge(s("gate_bcast").sem, s("gate_bcast").at(n + 1))
                nc.vector.tensor_tensor(h[r, g % 2, :], act_h[r, g % 2, :], psR[g % 2][r, :], ALU.mult)\
                    .then_inc(s("hidden_ready").sem, 1)

            def add(j):
                dve.wait_ge(s("ffn_outT_ready").sem, s("ffn_outT_ready").at(j + 1))
                x4 = tile4(x_sb, j)
                nc.vector.tensor_tensor(x4, x4, psM[:].rearrange("p (c d) -> p c d", d=P), ALU.add)\
                    .then_inc(s("x_added").sem, TPI)

            def body(i, first, last):
                for p in range(2):
                    j = 2 * i + p
                    front = not (last and p)
                    for k in range(CH):
                        g = p * CH + k
                        n = i * BODY + g
                        multiply(n, g)
                        if g or not first:
                            weigh(n - 1, (g - 1) % BODY)
                        if k == 8 and not (first and p == 0):
                            add(j - 1)
                        if front:
                            if k == 0:
                                steps = front_ln(j + 1)
                            elif k == 1:
                                front_xn(j + 1)
                            elif k == 5:
                                front_split(j + 1, 1 - p)
                                front_shift(j + 1, steps)
                            elif k == 6:
                                front_scores(j + 1, steps)
                            elif k == 7:
                                front_best(steps)
                            elif k == 8:
                                front_second(steps)
                            elif k == 9:
                                front_parts(steps)
            steps = front_ln(0)
            front_xn(0)
            front_split(0, 0)
            front_shift(0, steps)
            front_scores(0, steps)
            front_best(steps)
            front_second(steps)
            front_parts(steps)
            run_bodies(dve, body)
            weigh(ITERS * CH - 1, BODY - 1)
            add(ITERS - 1)

    n1, n4 = ITERS, ITERS * TPI
    pr.end_block(dict(pool_steps=1, x_split=n1, dve_steps=NST * n1, ln_var=n1, ln_rstd=n1, ln_out=n1, ln_T=n1, xT_ready=n1,
                      gate_logits=2 * n1, gate_exp=n1, gate_ready=n1, gate_T=n1, gate_parts=n1, hidden=n1 * CH, hidden_b=n1 * CH,
                      hidden_mul=n1 * CH, hidden_act=n1 * CH, hidden_ready=n1 * CH, gate_bcast=n1 * CH, ffn_out=n1, ffn_outT=n1,
                      ffn_outT_ready=n1, x_added=n4))


def layer2_ffn_weights(nc, ctx, dram):
    sb = buffers(nc, ctx, "f2w")
    E = L2_E
    t = {k: sb(k, [P, E, P]) for k in ("wq", "wk", "wv", "wo")}
    t.update(sim=sb("sim", [P, E]), ones=sb("ones", [P, P]), sg=sb("sg", [P, E]), desc=sb("desc", [P, E]),
             tri32=sb("tri32", [P, P]), tri=sb("tri", [P, P], BF16), self32=sb("self32", [3 * E, E * P]),
             selb=sb("selb", [3 * E, E * P], BF16))
    for k in ("wq", "wk", "wv"):
        t[k + "h"], t[k + "l"] = sb(k + "h", [P, E, P], F32R), sb(k + "l", [P, E, P], F32R)
    return Ahead(t, [(t["sim"][:], dram["F2_sim"]), (t["sg"][:], dram["F2_gates"].partition_broadcast(P)),
                     (t["desc"][:], dram["desc16"].partition_broadcast(P)), (t["ones"][:], dram["ones"]),
                     (t["tri32"][:], dram["tri"]), (t["self32"][:], dram["F2_sel"])] +
                    [(t[k][:], dram["F2_" + k]) for k in ("wq", "wk", "wv", "wo")],
                 [(t["selb"][:], t["self32"][:]), (t["tri"][:], t["tri32"][:])],
                 [(t[k][:], t[k + "h"][:], t[k + "l"][:]) for k in ("wq", "wk", "wv")])


def layer2_ffn(pr, x_sb, common, wt):
    nc, s = pr.nc, pr.sig
    E = L2_E
    T4 = TPI * P
    with ExitStack() as ctx:
        def sb(name, shape, dt=F32):
            return ctx.enter_context(nc.sbuf_tensor(f"{name}_f2", shape, dt))
        w = dict(common)
        ident = common["ident"]
        wq, wk, wv, wo, sim, ones, sg, tri, desc, selb = (wt[k] for k in ("wq", "wk", "wv", "wo", "sim", "ones", "sg", "tri",
                                                                         "desc", "selb"))
        whl = [(wt[k + "h"], wt[k + "l"]) for k in ("wq", "wk", "wv")]
        simsq = sb("simsq", [P, E])
        simn = sb("simn", [P, 2, E])
        xn, xT = sb("xn", [P, TPI, P]), sb("xT", [P, 2, T4])
        sq, ssq, rn = sb("sq", [P, TPI, P]), sb("ssq", [P, TPI]), sb("rn", [P, TPI])
        lg, ex, gated, oh, oh2, tmp, mask, rest = (sb(n, [P, TPI, E]) for n in ("lg", "ex", "gated", "oh", "oh2", "tmp", "mask", "rest"))
        top, gs, inact = sb("top", [P, TPI]), sb("gs", [P, TPI]), sb("inact", [P, TPI])
        hi, mid = sb("hi", [P, TPI, E], BF16), sb("mid", [P, TPI, E], BF16)
        parts, rwTb = sb("parts", [P, TPI, P]), sb("rwTb", [3 * E, 2, T4], BF16)
        rwTo = sb("rwTo", [3 * E, T4], BF16)
        RING = 4
        xs = sb("xs", [P, RING, T4])
        xsh, xsl = sb("xsh", [P, RING, T4], F32R), sb("xsl", [P, RING, T4], F32R)
        qkvT = sb("qkvT", [P, 3, T4])
        v = sb("v", [P, TPI, P])
        nmax, rs = sb("nmax", [P, TPI]), sb("rs", [P, TPI])
        p, pT = sb("p", [P, TPI, S]), sb("pT", [P, TPI, S])
        aoT, oT = sb("aoT", [P, 2, T4]), sb("oT", [P, T4])
        w.update(ln_buffers(sb))
        psR = [ctx.enter_context(nc.psum_tensor(f"psR{k}_f2", [P, T4], F32)) for k in range(2)]
        psQKV = [ctx.enter_context(nc.psum_tensor(f"psQ{k}_f2", [P, T4], F32)) for k in range(3)]
        psM = ctx.enter_context(nc.psum_tensor("psM_f2", [P, T4], F32))
        psX = ctx.enter_context(nc.psum_tensor("psX_f2", [P, T4], F32))
        psY = ctx.enter_context(nc.psum_tensor("psY_f2", [P, T4], F32))
        psA = psQKV + [psY]
        NST = LN_STEPS + 1 + 1 + 2 + 5 + 1 + 5 + 1 + 1 + 1 + 1 + 1 + 1 + 1 + 3
        block = ctx.enter_context(nc.Block())

        def qn(j, e):
            return e if isinstance(j, int) and j == 0 else 2 * E * j - E + e

        def on(j, e):
            return 2 * E * j + e - (E if isinstance(j, int) and j == ITERS else 0)

        def split_no(j, e):
            return (E - 1) * j + e - 1

        def run_mains(eng, main):
            main(0, 0)
            main(1, 1)
            with eng.Fori(1, ITERS // 2 - 1) as i:
                main(2 * i, 0)
                main(2 * i + 1, 1)
            main(ITERS - 2, 0)
            main(ITERS - 1, 1)

        def is_first(j, n):
            return isinstance(j, int) and j < n

        def is_last(j):
            return isinstance(j, int) and j == ITERS - 1

        def has_second_next(j):
            return not isinstance(j, int) or j + 2 < ITERS

        @block.gpsimd
        def _(pool):
            nc.gpsimd.memset(parts[:], 0.0).then_inc(s("pool_steps").sem, 1)
            pool.wait_ge(s("gate_ready").sem, s("gate_ready").at(1))
            nc.gpsimd.tensor_tensor(simn[:, 1, :], simn[:, 0, :], common["mhalf"][:, 0:E], ALU.pow)\
                .then_inc(s("pool_steps").sem, 1)

            def front(j):
                layernorm_pool(pr, pool, j + 1, w)
                pool.wait_ge(s("quant").sem, s("quant").at(j + 1))
                nc.gpsimd.tensor_tensor(rn[:], ssq[:], common["mhalf"][:, 0:TPI], ALU.pow).then_inc(s("pool_steps").sem, 1)

            def keep_routes(j, q):
                pool.wait_ge(s("gate_bcast").sem, s("gate_bcast").at(2 * E * j + E))
                pool.wait_ge(s("gate_parts").sem, s("gate_parts").at(j + 1))
                nc.gpsimd.tensor_tensor(rwTo[:].rearrange("e (c t) -> e c t", t=P), rwTb[:, q, :].rearrange("e (c t) -> e c t", t=P),
                                        ones[0:3 * E, :].unsqueeze(1).broadcast_to([3 * E, TPI, P]), ALU.mult)\
                    .then_inc(s("routes_kept").sem, 1)

            def main(j, q):
                if has_second_next(j):
                    front(j + 2)
                keep_routes(j, q)
            front(0)
            front(1)
            run_mains(pool, main)

        @block.scalar
        def _(act):
            nc.scalar.activation(simsq[:], sim[:], ACT.Square).then_inc(s("act_steps").sem, 1)
            nc.scalar.activation(sg[:], sg[:], ACT.Exp, scale=-1.0).then_inc(s("act_steps").sem, 1)

            def front_squares(j):
                act.wait_ge(s("ln_out").sem, s("ln_out").at(j + 1))
                for c in range(TPI):
                    ins = nc.scalar.activation(sq[:, c, :], xn[:, c, :], ACT.Square, accum_out=ssq[:, c:c + 1])
                ins.then_inc(s("absmax").sem, 1)

            def front_x(j, q):
                act.wait_ge(s("ln_T").sem, s("ln_T").at(j + 1))
                nc.scalar.activation(xT[:, q, :], psM[:], ACT.Copy).then_inc(s("xT_ready").sem, 1)

            def front_exp(j):
                act.wait_ge(s("gate_exp").sem, s("gate_exp").at(2 * j + 1))
                nc.scalar.activation(ex[:], lg[:], ACT.Exp).then_inc(s("gate_exp").sem, 1)

            def front_parts(j, q):
                act.wait_ge(s("gate_T").sem, s("gate_T").at(j + 1))
                if not is_first(j, 2):
                    act.wait_ge(s("routes_kept").sem, s("routes_kept").at(j - 1))
                nc.scalar.activation(rwTb[:, q, :], psM[0:3 * E, :], ACT.Copy).then_inc(s("gate_parts").sem, 1)

            def store_o(j):
                act.wait_ge(s("hidden").sem, s("hidden").at(on(j, E)))
                act.wait_ge(s("ffn_outT_ready").sem, s("ffn_outT_ready").at(j - 1))
                nc.scalar.activation(oT[:], psX[:], ACT.Copy).then_inc(s("ffn_outT").sem, 1)

            def main(j, q):
                for e in range(1, E):
                    act.wait_ge(s("scaled").sem, s("scaled").at(qn(j, e + 1)))
                    nc.scalar.activation(xsh[:, e % RING, :], xs[:, e % RING, :], ACT.Copy).then_inc(s("x_high").sem, 1)
                    if not is_last(j):
                        if e == 4:
                            front_x(j + 1, 1 - q)
                        elif e == 10:
                            front_exp(j + 1)
                        elif e == 15:
                            front_parts(j + 1, 1 - q)
                act.wait_ge(s("hidden").sem, s("hidden").at(qn(j, E)))
                nc.scalar.activation(qkvT[:, 0, :], psQKV[0][:], ACT.Copy, scale=float(P) ** -0.5)
                nc.scalar.activation(qkvT[:, 1, :], psQKV[1][:], ACT.Copy).then_inc(s("qkv_ready").sem, 1)
                nc.scalar.activation(qkvT[:, 2, :], psQKV[2][:], ACT.Copy).then_inc(s("qkv_ready").sem, 1)
                for c in range(TPI):
                    nk = P * (c % 2 + 1)
                    act.wait_ge(s("maxed").sem, s("maxed").at(j * TPI + c + 1))
                    nc.scalar.activation(p[:, c, 0:nk], psA[c][:, 0:nk], ACT.Exp, bias=nmax[:, c:c + 1],
                                         accum_out=rs[:, c:c + 1]).then_inc(s("probs").sem, 1)
                act.wait_ge(s("vT").sem, s("vT").at(j + 1))
                nc.scalar.activation(v[:].rearrange("p c d -> p (c d)"), psM[:], ACT.Copy).then_inc(s("v_ready").sem, 1)
                for c in range(TPI):
                    nk = P * (c % 2 + 1)
                    act.wait_ge(s("pT").sem, s("pT").at(j * TPI + c + 1))
                    nc.scalar.activation(pT[:, c, 0:nk], psA[c][:, S:S + nk], ACT.Copy).then_inc(s("pT_ready").sem, 1)
                act.wait_ge(s("ao").sem, s("ao").at(j + 1))
                nc.scalar.activation(aoT[:, q, :], psM[:], ACT.Copy).then_inc(s("ao_ready").sem, 1)
                if has_second_next(j):
                    front_squares(j + 2)
                if not is_first(j, 1):
                    store_o(j)
            front_squares(0)
            front_x(0, 0)
            front_exp(0)
            front_parts(0, 0)
            front_squares(1)
            run_mains(act, main)
            store_o(ITERS)

        @block.tensor
        def _(pe):
            pe.wait_ge(s("pool_steps").sem, s("pool_steps").at(1))
            pe.wait_ge(s("act_steps").sem, s("act_steps").at(1))
            nc.tensor.matmul(psM[:, 0:E], ones[:], simsq[:], start=True, stop=True).then_inc(s("gate_logits").sem, 1)
            pe.wait_ge(s("gate_ready").sem, s("gate_ready").at(2))

            def front_x(j):
                pe.wait_ge(s("ln_out").sem, s("ln_out").at(j + 1))
                for c in range(TPI):
                    ins = nc.tensor.transpose(psM[:, c * P:(c + 1) * P], xn[:, c, :], ident[:])
                ins.then_inc(s("ln_T").sem, 1)

            def front_logits(j, q):
                pe.wait_ge(s("xT_ready").sem, s("xT_ready").at(j + 1))
                for c in range(TPI):
                    ins = nc.tensor.matmul(psM[:, c * E:(c + 1) * E], xT[:, q, c * P:(c + 1) * P], simn[:, 0, :], start=True, stop=True)
                ins.then_inc(s("gate_logits").sem, 1)

            def front_parts(j):
                pe.wait_ge(s("gate_ready").sem, s("gate_ready").at(j + 3))
                for c in range(TPI):
                    ins = nc.tensor.transpose(psM[:, c * P:(c + 1) * P], parts[:, c, :], ident[:])
                ins.then_inc(s("gate_T").sem, 1)

            def out_T(j):
                pe.wait_ge(s("ffn_outT").sem, s("ffn_outT").at(j + 1))
                for c in range(TPI):
                    ins = nc.tensor.transpose(psM[:, c * P:(c + 1) * P], oT[:, c * P:(c + 1) * P], ident[:])
                ins.then_inc(s("ffn_outT_ready").sem, 1)

            def spread(n, e, weights):
                pe.wait_ge(s("scaled").sem, s("scaled").at(n - 1))
                nc.tensor.matmul(psR[e % 2][:], selb[:, e * P:(e + 1) * P], weights, start=True, stop=True)\
                    .then_inc(s("gate_bcast").sem, 1)

            def v_to_tokens(j):
                pe.wait_ge(s("qkv_ready").sem, s("qkv_ready").at(2 * j + 2))
                for c in range(TPI):
                    ins = nc.tensor.transpose(psM[:, c * P:(c + 1) * P], qkvT[:, 2, c * P:(c + 1) * P], ident[:])
                ins.then_inc(s("vT").sem, 1)

            def scores(j):
                pe.wait_ge(s("qkv_ready").sem, s("qkv_ready").at(2 * j + 2))
                for c in range(TPI):
                    t, b = c % 2, c // 2
                    nk = P * (t + 1)
                    nc.tensor.matmul(psA[c][:, 0:nk], qkvT[:, 0, c * P:(c + 1) * P], qkvT[:, 1, b * S:b * S + nk], start=True, stop=False)
                    nc.tensor.matmul(psA[c][:, t * P:nk], common["identb"][:], tri[:], start=False, stop=True).then_inc(s("scores").sem, 1)

            def probs_T(j, c):
                pe.wait_ge(s("heads_norm").sem, s("heads_norm").at(j * TPI + c + 1))
                for k in range(c % 2 + 1):
                    ins = nc.tensor.transpose(psA[c][:, S + k * P:S + (k + 1) * P], p[:, c, k * P:(k + 1) * P], ident[:])
                ins.then_inc(s("pT").sem, 1)

            def attend(j):
                pe.wait_ge(s("v_ready").sem, s("v_ready").at(j + 1))
                for c in range(TPI):
                    pe.wait_ge(s("pT_ready").sem, s("pT_ready").at(j * TPI + c + 1))
                    for k in range(c % 2 + 1):
                        ins = nc.tensor.matmul(psM[:, c * P:(c + 1) * P], v[:, c - c % 2 + k, :], pT[:, c, k * P:(k + 1) * P],
                                               start=k == 0, stop=k == c % 2)
                ins.then_inc(s("ao").sem, 1)

            def mix_o(j, attention):
                pe.wait_ge(s("routes_kept").sem, s("routes_kept").at(j))
                spread(on(j, 0), 0, rwTo[:])
                spread(on(j, 1), 1, rwTo[:])
                pe.wait_ge(s("ffn_outT").sem, s("ffn_outT").at(j - 1))
                for e in range(E):
                    if e + 2 < E:
                        spread(on(j, e + 2), e + 2, rwTo[:])
                    if e in attention:
                        attention[e]()
                    pe.wait_ge(s("scaled").sem, s("scaled").at(on(j, e + 1)))
                    nc.tensor.matmul(psX[:], wo[:, e, :], xs[:, e % RING, :], start=e == 0, stop=e == E - 1)\
                        .then_inc(s("hidden").sem, 1)

            def main(j, q):
                pe.wait_ge(s("gate_parts").sem, s("gate_parts").at(j + 1))
                spread(qn(j, 0), 0, rwTb[:, q, :])
                spread(qn(j, 1), 1, rwTb[:, q, :])
                for e in range(E):
                    if e + 2 < E:
                        spread(qn(j, e + 2), e + 2, rwTb[:, q, :])
                    if e == 0:
                        pe.wait_ge(s("pT_ready").sem, s("pT_ready").at(j * TPI))
                    r = e % RING
                    if e == 0:
                        pe.wait_ge(s("scaled").sem, s("scaled").at(qn(j, 1)))
                        for n, w32 in enumerate((wq, wk, wv)):
                            ins = nc.tensor.matmul(psQKV[n][:], w32[:, e, :], xs[:, r, :], start=True, stop=False)
                    else:
                        pe.wait_ge(s("x_split").sem, s("x_split").at(split_no(j, e) + 1))
                        for n, (hi_w, lo_w) in enumerate(whl):
                            for m, (wp, xp) in enumerate(((lo_w, xsh), (hi_w, xsl), (hi_w, xsh))):
                                ins = nc.tensor.matmul(psQKV[n][:], wp[:, e, :], xp[:, r, :], start=False, stop=e == E - 1 and m == 2)
                    ins.then_inc(s("hidden").sem, 1)
                    if e == 0:
                        pe.wait_ge(s("ao_ready").sem, s("ao_ready").at(j))
                    if e == 10 and not is_first(j, 2):
                        if not is_last(j):
                            pe.wait_ge(s("gate_exp").sem, s("gate_exp").at(2 * j + 3))
                        out_T(j - 2)
                    if not is_last(j):
                        if e == 2:
                            front_x(j + 1)
                        elif e == 4:
                            front_logits(j + 1, 1 - q)
                        elif e == 14:
                            if not is_first(j, 2):
                                pe.wait_ge(s("x_added").sem, s("x_added").at((j - 1) * TPI))
                            front_parts(j + 1)
                if is_last(j):
                    pe.wait_ge(s("x_added").sem, s("x_added").at((j - 1) * TPI))
                else:
                    pe.wait_ge(s("gate_parts").sem, s("gate_parts").at(j + 2))
                stages = {1: lambda: scores(j), 2: lambda: v_to_tokens(j), 5: lambda: (probs_T(j, 0), probs_T(j, 1)),
                          7: lambda: (probs_T(j, 2), probs_T(j, 3)), 9: lambda: attend(j)}
                if is_first(j, 1):
                    for stage in stages.values():
                        stage()
                else:
                    mix_o(j, stages)
            front_x(0)
            front_logits(0, 0)
            front_parts(0)
            run_mains(pe, main)
            pe.wait_ge(s("ao_ready").sem, s("ao_ready").at(ITERS))
            out_T(ITERS - 2)
            mix_o(ITERS, {})
            pe.wait_ge(s("x_added").sem, s("x_added").at((ITERS - 1) * TPI))
            out_T(ITERS - 1)

        @block.vector
        def _(dve):
            setup = Steps(dve, s("dve_steps"), 0, 2)
            dve.wait_ge(s("gate_logits").sem, s("gate_logits").at(1))
            nc.vector.tensor_scalar(simn[:, 0, :], psM[:, 0:E], 1e-12, None, ALU.add).then_inc(s("gate_ready").sem, 1)
            dve.wait_ge(s("pool_steps").sem, s("pool_steps").at(2))
            nc.vector.tensor_tensor(simn[:, 0, :], sim[:], simn[:, 1, :], ALU.mult).then_inc(s("gate_ready").sem, 1)
            dve.wait_ge(s("act_steps").sem, s("act_steps").at(2))
            setup.done(nc.vector.tensor_scalar(sg[:], sg[:], 1.0, None, ALU.add))
            setup.done(nc.vector.reciprocal(sg[:], sg[:]))
            setup.end()
            g4 = [P, TPI, E]

            def front_ln(j):
                steps = Steps(dve, s("dve_steps"), j, NST)
                steps.k = 2
                layernorm_vector(pr, dve, steps, j, w, tile4(x_sb, j), xn)

            def gate_steps(j):
                steps = Steps(dve, s("dve_steps"), j, NST)
                steps.k = 2 + LN_STEPS
                return steps

            def front_xn(j):
                dve.wait_ge(s("ln_rstd").sem, s("ln_rstd").at(j + 1))
                dve.wait_ge(s("ln_T").sem, s("ln_T").at(j))
                layernorm_apply(pr, dve, w, tile4(x_sb, j), xn).then_inc(s("ln_out").sem, 1)

            def front_norm(j):
                dve.wait_ge(s("absmax").sem, s("absmax").at(j + 1))
                nc.vector.tensor_scalar(ssq[:], ssq[:], 1e-12, None, ALU.add).then_inc(s("quant").sem, 1)

            def front_gate(j, steps):
                dve.wait_ge(s("pool_steps").sem, s("pool_steps").at(3 + j))
                dve.wait_ge(s("gate_logits").sem, s("gate_logits").at(j + 2))
                lps = psM[:, 0:TPI * E].rearrange("p (c e) -> p c e", e=E)
                steps.done(nc.vector.tensor_tensor(lg[:], lps, rn[:].unsqueeze(2).broadcast_to(g4), ALU.mult))
                steps.done(nc.vector.tensor_tensor(lg[:], lg[:], sg[:].unsqueeze(1).broadcast_to(g4), ALU.subtract))
                nc.vector.tensor_scalar(gated[:], lg[:], 0.0, None, ALU.max)
                nc.vector.tensor_scalar(mask[:], lg[:], 0.0, None, ALU.is_gt)

            def front_best(steps):
                first_max(nc, steps, lg[:], oh[:], gs[:], tmp[:], desc[:])

            def front_second(steps):
                steps.done(nc.vector.tensor_reduce(top[:], gated[:], axis=AX.X, op=ALU.max))
                steps.done(nc.vector.tensor_scalar(inact[:], top[:], 0.0, None, ALU.is_le))
                steps.done(nc.vector.scalar_tensor_tensor(lg[:], oh[:], -1e30, lg[:], ALU.mult, ALU.add))
                first_max(nc, steps, lg[:], oh2[:], gs[:], tmp[:], desc[:])

            def front_mask(steps):
                nc.vector.tensor_tensor(lg[:], gated[:], top[:].unsqueeze(2).broadcast_to(g4), ALU.subtract)\
                    .then_inc(s("gate_exp").sem, 1)
                steps.done(nc.vector.tensor_tensor(oh[:], oh[:], oh2[:], ALU.add))
                steps.done(nc.vector.tensor_tensor(oh[:], oh[:], inact[:].unsqueeze(2).broadcast_to(g4), ALU.mult))
                steps.done(nc.vector.tensor_tensor(mask[:], mask[:], oh[:], ALU.add))

            def front_weights(j, steps):
                dve.wait_ge(s("gate_exp").sem, s("gate_exp").at(2 * j + 2))
                steps.done(nc.vector.tensor_tensor(ex[:], ex[:], mask[:], ALU.mult))
                steps.done(nc.vector.tensor_reduce(gs[:], ex[:], axis=AX.X, op=ALU.add))
                steps.done(nc.vector.reciprocal(gs[:], gs[:]))
                steps.done(nc.vector.tensor_tensor(ex[:], ex[:], gs[:].unsqueeze(2).broadcast_to(g4), ALU.mult))

            def front_parts(steps):
                three_parts(nc, steps, ex[:], parts[:], hi[:], rest[:], mid[:], E).then_inc(s("gate_ready").sem, 1)
                steps.n += 2
                steps.end()

            def scale_by(n, e, src):
                dve.wait_ge(s("gate_bcast").sem, s("gate_bcast").at(n + 1))
                dve.wait_ge(s("hidden").sem, s("hidden").at(n + 1 - RING))
                nc.vector.tensor_tensor(xs[:, e % RING, :], src, psR[e % 2][:], ALU.mult).then_inc(s("scaled").sem, 1)

            def low_part(j, e):
                dve.wait_ge(s("x_high").sem, s("x_high").at(split_no(j, e) + 1))
                nc.vector.tensor_tensor(xsl[:, e % RING, :], xs[:, e % RING, :], xsh[:, e % RING, :], ALU.subtract)\
                    .then_inc(s("x_split").sem, 1)

            def maxima(j):
                for c in range(TPI):
                    nk = P * (c % 2 + 1)
                    dve.wait_ge(s("scores").sem, s("scores").at(j * TPI + c + 1))
                    nc.vector.tensor_reduce(nmax[:, c:c + 1], psA[c][:, 0:nk], axis=AX.X, op=ALU.max, negate=True)\
                        .then_inc(s("maxed").sem, 1)

            def normalise(j, c):
                nk = P * (c % 2 + 1)
                dve.wait_ge(s("probs").sem, s("probs").at(j * TPI + c + 1))
                nc.vector.reciprocal(rs[:, c:c + 1], rs[:, c:c + 1]).then_inc(s("sums_inverted").sem, 1)
                dve.wait_ge(s("sums_inverted").sem, s("sums_inverted").at(j * TPI + c + 1))
                nc.vector.tensor_scalar(p[:, c, 0:nk], p[:, c, 0:nk], rs[:, c:c + 1], None, ALU.mult)\
                    .then_inc(s("heads_norm").sem, 1)

            def add(j):
                dve.wait_ge(s("ffn_outT_ready").sem, s("ffn_outT_ready").at(j + 1))
                x4 = tile4(x_sb, j)
                nc.vector.tensor_tensor(x4, x4, psM[:].rearrange("p (c d) -> p c d", d=P), ALU.add)\
                    .then_inc(s("x_added").sem, TPI)

            def mix_o(j, q, attention):
                dve.wait_ge(s("ao_ready").sem, s("ao_ready").at(j))
                for e in range(E):
                    scale_by(on(j, e), e, aoT[:, q, :])
                    if e in attention:
                        attention[e]()

            def main(j, q):
                for e in range(E):
                    scale_by(qn(j, e), e, xT[:, q, :])
                    if e > 1:
                        low_part(j, e - 1)
                    if e == 12 and not is_first(j, 2):
                        add(j - 2)
                    if not is_last(j):
                        if e == 6:
                            steps = gate_steps(j + 1)
                            front_gate(j + 1, steps)
                        elif e == 7:
                            front_best(steps)
                        elif e == 8:
                            front_second(steps)
                        elif e == 9:
                            front_mask(steps)
                        elif e == 11:
                            front_weights(j + 1, steps)
                        elif e == 13:
                            front_parts(steps)
                low_part(j, E - 1)
                stages = {1: lambda: maxima(j), 3: lambda: (normalise(j, 0), normalise(j, 1)),
                          5: lambda: (normalise(j, 2), normalise(j, 3))}
                if has_second_next(j):
                    stages.update({10: lambda: front_ln(j + 2), 12: lambda: front_xn(j + 2), 14: lambda: front_norm(j + 2)})
                if is_first(j, 1):
                    for stage in stages.values():
                        stage()
                else:
                    mix_o(j, 1 - q, stages)
            front_ln(0)
            front_xn(0)
            front_norm(0)
            steps = gate_steps(0)
            front_gate(0, steps)
            front_best(steps)
            front_second(steps)
            front_mask(steps)
            front_weights(0, steps)
            front_parts(steps)
            front_ln(1)
            front_xn(1)
            front_norm(1)
            run_mains(dve, main)
            add(ITERS - 2)
            mix_o(ITERS, 1, {})
            add(ITERS - 1)

    n1, n4 = ITERS, ITERS * TPI
    pr.end_block(dict(x_high=(E - 1) * n1, x_split=(E - 1) * n1, pool_steps=2 + n1, act_steps=2, dve_steps=2 + NST * n1, ln_var=n1, ln_rstd=n1, ln_out=n1,
                      ln_T=n1, xT_ready=n1, gate_logits=n1 + 1, gate_ready=n1 + 2, gate_exp=2 * n1, gate_T=n1, gate_parts=n1,
                      absmax=n1, quant=n1, gate_bcast=2 * E * n1, scaled=2 * E * n1, hidden=2 * E * n1,
                      routes_kept=n1, sums_inverted=n4,
                      qkv_ready=2 * n1, vT=n1, v_ready=n1, scores=n4, maxed=n4, probs=n4, heads_norm=n4, pT=n4, pT_ready=n4,
                      ao=n1, ao_ready=n1, ffn_outT=n1, ffn_outT_ready=n1, x_added=n4))


def rows_in_steps(eng, rows, depth, step):
    for r in range(depth):
        step(r, r)
    with eng.Fori(1, rows // depth) as i:
        for k in range(depth):
            step(i * depth + k, k)
    for r in range(rows, rows + depth):
        step(r, r - rows)


def layer3_ffn_weights(nc, ctx, dram):
    wraw = buffers(nc, ctx, "f3w")("wraw", [P, 3, L3_I])
    return Ahead(dict(wraw=wraw), [(wraw[:], dram["F3_w"])])


def layer3_ffn(pr, x_sb, common, wt):
    nc, s = pr.nc, pr.sig
    T4 = TPI * P
    NI = L3_I // P
    ROWS = ITERS * NI
    QMAX = 32767.0
    with ExitStack() as ctx:
        def sb(name, shape, dt=F32):
            return ctx.enter_context(nc.sbuf_tensor(f"{name}_f3", shape, dt))
        ident = common["ident"]
        up, gt = sb("up", [P, NI, ITERS, T4]), sb("gt", [P, NI, ITERS, T4])
        wraw = wt["wraw"]
        wT = sb("wT", [P, 3, L3_I])
        ws, wi = sb("ws", [P, 3, L3_I // BLK]), sb("wi", [P, 3, L3_I // BLK])
        xT = sb("xT", [P, ITERS, T4])
        xq = sb("xq", [P, 2, NI, T4])
        gq, sig, uq = xT[:, 0:4, :], xT[:, 4:8, :], xq[:].rearrange("p a n t -> p (a n) t")[:, 0:4, :]
        am = sb("am", [P, 5, ROWS])
        amr, gm = sb("amr", [P, 5]), sb("gm", [P, 5])
        scale, inv, fac = sb("scale", [P, 5]), sb("inv", [P, 5]), sb("fac", [P, 5])
        magic = sb("magic", [P, 1])
        w = all_ln_buffers(sb)
        mean, rstd = w["mean"], w["rstd"]
        PS = [ctx.enter_context(nc.psum_tensor(f"ps{c}_f3", [P, T4], F32)) for c in range(8)]
        X, U, G, GS, O = range(5)
        SC_STEPS = 4
        upf, gtf = up[:].rearrange("p n i t -> p (n i) t"), gt[:].rearrange("p n i t -> p (n i) t")

        def part(t, r):
            return t[:, bass.ds(r, 1), :].rearrange("p a t -> p (a t)")

        def scale_vector(dve, done, k, n, width, factor=None):
            col = slice(k, k + 1)
            nc.vector.tensor_reduce(amr[:, col], am[:, k, 0:width], axis=AX.X, op=ALU.max).then_inc(s("absmax").sem, 1)
            dve.wait_ge(s("gmax").sem, s("gmax").at(n))
            f = 1.0 if factor is None else factor
            done(nc.vector.tensor_scalar(scale[:, col], gm[:, col], f, 1.0 / QMAX, ALU.mult, ALU.mult))
            done(nc.vector.tensor_scalar(scale[:, col], scale[:, col], 1e-12, None, ALU.max))
            done(nc.vector.reciprocal(inv[:, col], scale[:, col]))
            done(nc.vector.tensor_scalar(inv[:, col], inv[:, col], f, None, ALU.mult))

        def gmax_pool(pool, k, n):
            pool.wait_ge(s("absmax").sem, s("absmax").at(n))
            nc.gpsimd.partition_all_reduce(gm[:, k:k + 1], amr[:, k:k + 1], P, bass.bass_isa.ReduceOp.max)\
                .then_inc(s("gmax").sem, 1)

        NW = 2 + 6 + SC_STEPS
        with nc.Block() as block:
            @block.gpsimd
            def _(pool):
                nc.gpsimd.memset(magic[:], MAGIC)
                all_ln_pool(pr, pool, w)
                gmax_pool(pool, X, 1)

            @block.scalar
            def _(act):
                for k in range(3):
                    act.wait_ge(s("vT").sem, s("vT").at(k + 1))
                    nc.scalar.activation(wT[:, k, :], PS[5 + k][:, 0:L3_I], ACT.Copy).then_inc(s("v_ready").sem, 1)
                for i in range(ITERS):
                    act.wait_ge(s("ln_T").sem, s("ln_T").at(i + 1))
                    nc.scalar.activation(xT[:, i, :], PS[i % 2][:], ACT.Copy).then_inc(s("xT_ready").sem, 1)

            @block.tensor
            def _(pe):
                pe.wait_ge(s("quant").sem, s("quant").at(1))
                for k in range(3):
                    for j in range(NI):
                        ins = nc.tensor.transpose(PS[5 + k][:, j * P:(j + 1) * P], wraw[:, k, j * P:(j + 1) * P], ident[:])
                    ins.then_inc(s("vT").sem, 1)
                for i in range(ITERS):
                    pe.wait_ge(s("ln_out").sem, s("ln_out").at(i + 1))
                    pe.wait_ge(s("xT_ready").sem, s("xT_ready").at(i - 1))
                    for c in range(TPI):
                        ins = nc.tensor.transpose(PS[i % 2][:, c * P:(c + 1) * P], xq[:, i % 2, 0, c * P:(c + 1) * P], ident[:])
                    ins.then_inc(s("ln_T").sem, 1)

            @block.vector
            def _(dve):
                st = Steps(dve, s("dve_steps"), 0, NW)
                all_ln_vector(pr, dve, st.done, w, x_sb)
                wb = wraw[:].rearrange("p k (n b) -> p (k n) b", b=BLK)
                wsf, wif = ws[:].rearrange("p k n -> p (k n)"), wi[:].rearrange("p k n -> p (k n)")
                full = list(wb.shape)
                st.done(nc.vector.tensor_reduce(wsf, wb, axis=AX.X, op=ALU.max, apply_absolute_value=True))
                st.done(nc.vector.tensor_scalar(wsf, wsf, 1.0 / 7.0, 1e-12, ALU.mult, ALU.max))
                st.done(nc.vector.reciprocal(wif, wsf))
                st.done(nc.vector.tensor_tensor(wb, wb, wif.unsqueeze(2).broadcast_to(full), ALU.mult))
                st.done(nc.vector.tensor_scalar(wraw[:], wraw[:], MAGIC, -MAGIC, ALU.add, ALU.add))
                st.done(nc.vector.tensor_scalar(wraw[:], wraw[:], 7.0, -8.0, ALU.min, ALU.max))
                nc.vector.tensor_tensor(wb, wb, wsf.unsqueeze(2).broadcast_to(full), ALU.mult).then_inc(s("quant").sem, 1)

                def largest(i):
                    dve.wait_ge(s("ln_out").sem, s("ln_out").at(i + 1))
                    nc.vector.tensor_reduce(am[:, X, i:i + 1], xq[:, i % 2, 0, :], axis=AX.X, op=ALU.max,
                                            apply_absolute_value=True).then_inc(s("maxed").sem, 1)
                for i in range(ITERS):
                    dve.wait_ge(s("ln_T").sem, s("ln_T").at(i - 1))
                    dve.wait_ge(s("maxed").sem, s("maxed").at(i - 1))
                    wait_rstd(pr, dve, i * TPI)
                    for c in range(TPI):
                        n = i * TPI + c
                        ins = nc.vector.tensor_scalar(xq[:, i % 2, 0, c * P:(c + 1) * P], x_sb[:, n, :], mean[:, n:n + 1],
                                                      rstd[:, n:n + 1], ALU.subtract, ALU.mult)
                    ins.then_inc(s("ln_out").sem, 1)
                    if i:
                        largest(i - 1)
                largest(ITERS - 1)
                dve.wait_ge(s("maxed").sem, s("maxed").at(ITERS))
                scale_vector(dve, st.done, X, 1, ITERS)
                st.end()
        pr.end_block(dict(ln_var=1, ln_rstd=RSTD_PARTS, absmax=1, gmax=1, vT=3, v_ready=3, ln_T=ITERS, xT_ready=ITERS,
                          quant=1, ln_out=ITERS, maxed=ITERS, dve_steps=NW, stats_ready=1, pool_steps=1))

        with nc.Block() as block:
            NP = 2 * NI

            @block.gpsimd
            def _(pool):
                gmax_pool(pool, U, 1)
                gmax_pool(pool, G, 2)

            @block.tensor
            def _(pe):
                def project(i, k):
                    pe.wait_ge(s("quant").sem, s("quant").at(i + 1))
                    for n in range(NP):
                        pe.wait_ge(s("hidden_b").sem, s("hidden_b").at((i - 1) * NP + n + 1))
                        nc.tensor.matmul(PS[n][:], wT[:, n // NI, (n % NI) * P:(n % NI + 1) * P], xq[:, k, 0, :],
                                         start=True, stop=True).then_inc(s("hidden").sem, 1)
                with pe.Fori(0, ITERS // 2) as i:
                    project(2 * i, 0)
                    project(2 * i + 1, 1)

            @block.scalar
            def _(act):
                with act.Fori(0, ITERS) as i:
                    for n in range(NP):
                        act.wait_ge(s("hidden").sem, s("hidden").at(i * NP + n + 1))
                        kept = (gt if n < NI else up)[:, n % NI, bass.ds(i, 1), :].rearrange("p a t -> p (a t)")
                        nc.scalar.activation(kept, PS[n][:], ACT.Copy, scale=scale[:, X:X + 1]).then_inc(s("hidden_b").sem, 1)

            @block.vector
            def _(dve):
                def quantise(i, k):
                    dve.wait_ge(s("hidden").sem, s("hidden").at((i - 1) * NP))
                    nc.vector.tensor_scalar(xq[:, k, 0, :], part(xT, i), inv[:, X:X + 1], MAGIC, ALU.mult, ALU.add)\
                        .then_inc(s("scaled").sem, 1)
                    dve.wait_ge(s("scaled").sem, s("scaled").at(i + 1))
                    nc.vector.tensor_scalar(xq[:, k, 0, :], xq[:, k, 0, :], -MAGIC, None, ALU.add).then_inc(s("quant").sem, 1)

                def largest(i):
                    for k, kept in ((G, gt), (U, up)):
                        dve.wait_ge(s("hidden_b").sem, s("hidden_b").at(i * NP + (NI if k == G else NP)))
                        nc.vector.tensor_reduce(am[:, k, bass.ds(i, 1)], kept[:, :, bass.ds(i, 1), :].rearrange("p n a t -> p (n a) t"),
                                                axis=AX.XY, op=ALU.max, apply_absolute_value=True).then_inc(s("maxed").sem, 1)
                quantise(0, 0)
                quantise(1, 1)
                with dve.Fori(0, ITERS // 2 - 1) as i:
                    for k in range(2):
                        largest(2 * i + k)
                        quantise(2 * i + k + 2, k)
                largest(ITERS - 2)
                largest(ITERS - 1)
                st = Steps(dve, s("dve_steps"), 0, 2 * SC_STEPS)
                dve.wait_ge(s("maxed").sem, s("maxed").at(ITERS * 2))
                scale_vector(dve, st.done, U, 1, ITERS)
                scale_vector(dve, st.done, G, 2, ITERS)
        pr.end_block(dict(absmax=2, gmax=2, quant=ITERS, scaled=ITERS, hidden=ITERS * NP, hidden_b=ITERS * NP, maxed=ITERS * 2,
                          dve_steps=2 * SC_STEPS))

        DEPTH = 4
        with nc.Block() as block:
            @block.gpsimd
            def _(pool):
                def step(r, k):
                    if has(r - 1, ROWS):
                        pool.wait_ge(s("hidden_ready").sem, s("hidden_ready").at(r))
                        nc.gpsimd.tensor_tensor(part(gtf, r - 1), gq[:, (k - 1) % DEPTH, :], sig[:, (k - 1) % DEPTH, :], ALU.mult)\
                            .then_inc(s("hidden_mul").sem, 1)
                rows_in_steps(pool, ROWS, DEPTH, step)
                gmax_pool(pool, GS, 1)

            @block.scalar
            def _(act):
                def step(r, k):
                    if has(r, ROWS):
                        act.wait_ge(s("hidden_mul").sem, s("hidden_mul").at(r + 1 - DEPTH))
                        act.wait_ge(s("up_ready").sem, s("up_ready").at(r + 1 - DEPTH))
                        nc.scalar.activation(gq[:, k, :], part(gtf, r), ACT.Identity, bias=magic[:], scale=inv[:, G:G + 1])\
                            .then_inc(s("scaled").sem, 1)
                        nc.scalar.activation(uq[:, k, :], part(upf, r), ACT.Identity, bias=magic[:], scale=inv[:, U:U + 1])\
                            .then_inc(s("up_scaled").sem, 1)
                    if has(r - 1, ROWS):
                        q = (k - 1) % DEPTH
                        act.wait_ge(s("quant").sem, s("quant").at(r))
                        nc.scalar.activation(sig[:, q, :], gq[:, q, :], ACT.Sigmoid, scale=scale[:, G:G + 1])\
                            .then_inc(s("hidden_act").sem, 1)
                rows_in_steps(act, ROWS, DEPTH, step)

            @block.vector
            def _(dve):
                def step(r, k):
                    if has(r, ROWS):
                        dve.wait_ge(s("scaled").sem, s("scaled").at(r + 1))
                        nc.vector.tensor_scalar(gq[:, k, :], gq[:, k, :], -MAGIC, None, ALU.add).then_inc(s("quant").sem, 1)
                    if has(r - 1, ROWS):
                        dve.wait_ge(s("hidden_act").sem, s("hidden_act").at(r))
                        sg = sig[:, (k - 1) % DEPTH, :]
                        nc.vector.tensor_scalar(sg, sg, 65536.0, 65535.0, ALU.mult, ALU.min).then_inc(s("hidden").sem, 1)
                    if has(r - 3, ROWS):
                        dve.wait_ge(s("hidden_mul").sem, s("hidden_mul").at(r - 2))
                        nc.vector.tensor_reduce(am[:, GS, bass.ds(r - 3, 1)], part(gtf, r - 3), axis=AX.X, op=ALU.max,
                                                apply_absolute_value=True).then_inc(s("maxed").sem, 1)
                    if has(r - 1, ROWS):
                        dve.wait_ge(s("up_scaled").sem, s("up_scaled").at(r))
                        nc.vector.tensor_scalar(part(upf, r - 1), uq[:, (k - 1) % DEPTH, :], -MAGIC, None, ALU.add)\
                            .then_inc(s("up_ready").sem, 1)
                        dve.wait_ge(s("hidden").sem, s("hidden").at(r))
                        nc.vector.tensor_scalar(sg, sg, MAGIC, -MAGIC, ALU.add, ALU.add).then_inc(s("hidden_ready").sem, 1)
                rows_in_steps(dve, ROWS, DEPTH, step)
                st = Steps(dve, s("dve_steps"), 0, SC_STEPS + 1)
                dve.wait_ge(s("maxed").sem, s("maxed").at(ROWS))
                st.done(nc.vector.tensor_scalar(fac[:, GS:GS + 1], scale[:, G:G + 1], 1.0 / 65536.0, None, ALU.mult))
                scale_vector(dve, st.done, GS, 1, ROWS, fac[:, GS:GS + 1])
        pr.end_block(dict(absmax=1, gmax=1, quant=ROWS, scaled=ROWS, up_scaled=ROWS, up_ready=ROWS, hidden_act=ROWS, hidden=ROWS,
                          hidden_ready=ROWS, hidden_mul=ROWS, maxed=ROWS, dve_steps=SC_STEPS + 1))

        with nc.Block() as block:
            @block.gpsimd
            def _(pool):
                gmax_pool(pool, O, 1)

            @block.scalar
            def _(act):
                with act.Fori(0, ROWS) as r:
                    nc.scalar.activation(part(gtf, r), part(gtf, r), ACT.Identity, bias=magic[:], scale=inv[:, GS:GS + 1])\
                        .then_inc(s("scaled").sem, 1)

            @block.vector
            def _(dve):
                def step(r, k):
                    if has(r, ROWS):
                        dve.wait_ge(s("scaled").sem, s("scaled").at(r + 1))
                        nc.vector.scalar_tensor_tensor(part(gtf, r), part(gtf, r), -MAGIC, part(upf, r), ALU.add, ALU.mult)\
                            .then_inc(s("quant").sem, 1)
                    if has(r - 1, ROWS):
                        dve.wait_ge(s("quant").sem, s("quant").at(r))
                        nc.vector.tensor_reduce(am[:, O, bass.ds(r - 1, 1)], part(gtf, r - 1), axis=AX.X, op=ALU.max,
                                                apply_absolute_value=True).then_inc(s("maxed").sem, 1)
                rows_in_steps(dve, ROWS, DEPTH, step)
                st = Steps(dve, s("dve_steps"), 0, SC_STEPS + 1)
                dve.wait_ge(s("maxed").sem, s("maxed").at(ROWS))
                st.done(nc.vector.tensor_tensor(fac[:, O:O + 1], scale[:, GS:GS + 1], scale[:, U:U + 1], ALU.mult))
                scale_vector(dve, st.done, O, 1, ROWS, fac[:, O:O + 1])
        pr.end_block(dict(absmax=1, gmax=1, scaled=ROWS, quant=ROWS, maxed=ROWS, dve_steps=SC_STEPS + 1))

        with nc.Block() as block:
            @block.tensor
            def _(pe):
                def down(i, k):
                    pe.wait_ge(s("quant").sem, s("quant").at(i + 1))
                    pe.wait_ge(s("x_added").sem, s("x_added").at(i - 1))
                    for c in range(TPI):
                        for n in range(NI):
                            ins = nc.tensor.matmul(PS[k][:, c * P:(c + 1) * P], xq[:, k, n, c * P:(c + 1) * P],
                                                   wT[:, 2, n * P:(n + 1) * P], start=n == 0, stop=n == NI - 1)
                    ins.then_inc(s("ffn_out").sem, 1)
                with pe.Fori(0, ITERS // 2) as i:
                    down(2 * i, 0)
                    down(2 * i + 1, 1)

            @block.scalar
            def _(act):
                def quantise(i, k):
                    act.wait_ge(s("ffn_out").sem, s("ffn_out").at(i - 1))
                    nc.scalar.activation(xq[:, k, :, :], gt[:, :, bass.ds(i, 1), :].rearrange("p n a t -> p (n a) t"),
                                         ACT.Identity, bias=magic[:], scale=inv[:, O:O + 1]).then_inc(s("scaled").sem, 1)
                with act.Fori(0, ITERS // 2) as i:
                    quantise(2 * i, 0)
                    quantise(2 * i + 1, 1)

            @block.vector
            def _(dve):
                def integers(i, k):
                    dve.wait_ge(s("scaled").sem, s("scaled").at(i + 1))
                    nc.vector.tensor_scalar(xq[:, k, :, :], xq[:, k, :, :], -MAGIC, None, ALU.add).then_inc(s("quant").sem, 1)

                def add(i, k):
                    dve.wait_ge(s("ffn_out").sem, s("ffn_out").at(i + 1))
                    x4 = tile4(x_sb, i)
                    nc.vector.scalar_tensor_tensor(x4, PS[k][:].rearrange("p (c d) -> p c d", d=P), scale[:, O:O + 1], x4,
                                                   ALU.mult, ALU.add).then_inc(s("x_added").sem, 1)
                integers(0, 0)
                with dve.Fori(0, ITERS // 2 - 1) as i:
                    for k in range(2):
                        integers(2 * i + k + 1, 1 - k)
                        add(2 * i + k, k)
                integers(ITERS - 1, 1)
                add(ITERS - 2, 0)
                add(ITERS - 1, 1)
        pr.end_block(dict(scaled=ITERS, quant=ITERS, ffn_out=ITERS, x_added=ITERS))


def build(nc, dram, out):
    with ExitStack() as ctx:
        pr = Program(nc, ctx)
        for name in SIGNALS:
            pr.sig(name)
        x_sb = ctx.enter_context(nc.sbuf_tensor("x_sb", [P, TILES, P], F32))
        common = {}

        def csb(name, shape, dt=F32):
            common[name] = ctx.enter_context(nc.sbuf_tensor(name, shape, dt))
            return common[name]
        csb("ident", [P, P]), csb("identb", [P, P], BF16), csb("ctxT", [P, B * P]), csb("headmask", [P, H])
        csb("mhalf", [P, 16])
        later = Ahead({}, [], [(common["identb"][:], common["ident"][:])])
        for layer in range(1, 4):
            later = later + narrow_attention_weights(nc, ctx, dram, layer)
        with ExitStack() as first:
            sb0 = buffers(nc, first, "a0w")
            wide = {k: sb0(k, [P, PAIRS, P]) for k in ("wqT", "wkT", "wvT", "wo")}
            wide["bo"] = sb0("bo", [P, P])
            with nc.Block() as block:
                @block.sync
                def _(sp):
                    load(sp, pr.sig("x_loaded"), [(x_sb[:], dram["x"])])
                    load(sp, pr.sig("weights_qk"), [(wide[k][:], dram["L0_" + k]) for k in ("wqT", "wkT")])
                    load(sp, pr.sig("inputs"), [(wide["wvT"][:], dram["L0_wvT"]), (wide["wo"][:], dram["L0_wo"]),
                                                (common["ident"][:], dram["ident"]), (common["ctxT"][:], dram["ctxT"]),
                                                (common["headmask"][:], dram["headmask"]),
                                                (wide["bo"][:], dram["L0_bo"].partition_broadcast(P))])

                @block.gpsimd
                def _(pool):
                    for g in pr.named.values():
                        pool.sem_inc(g.sem, Signal.PRIME)
                    nc.gpsimd.memset(common["mhalf"][:], -0.5)
            ffn0 = layer0_ffn_weights(nc, first, dram)
            wide_attention(pr, x_sb, common, wide, ffn0 + later)
            if N_SUBLAYERS > 1:
                layer0_ffn(pr, x_sb, common, ffn0.tensors)
        ffns = [(layer1_ffn_weights, layer1_ffn), (layer2_ffn_weights, layer2_ffn), (layer3_ffn_weights, layer3_ffn)]
        for layer, (weights, ffn) in enumerate(ffns, 1):
            if N_SUBLAYERS <= 2 * layer:
                break
            with ExitStack() as scope:
                wt = weights(nc, scope, dram)
                narrow_attention(pr, x_sb, common, dram, layer, later.tensors, wt)
                if N_SUBLAYERS > 2 * layer + 1:
                    ffn(pr, x_sb, common, wt.tensors)
        with nc.Block() as block:
            @block.sync
            def _(sp):
                sp.dma_start(out, x_sb[:]).then_inc(pr.sig("out_stored").sem, 16)
                sp.wait_ge(pr.sig("out_stored").sem, pr.sig("out_stored").at(16))


def laid_out(inp):
    import numpy as np
    f = {k: np.asarray(v) for k, v in inp.items()}

    def rows(a):
        return a.reshape(-1, P, a.shape[-1]).transpose(1, 0, 2)

    d = {}
    d["x"] = rows(f["x"].reshape(B * S, P))
    ct = f["ctx_1024"].transpose(2, 0, 1)
    d["ctxT"] = np.concatenate([ct, ct], axis=2).reshape(P, B * P)
    d["mask"] = f["mask_Bx1xSxS2_ik1"].reshape(TILES, P, SC).transpose(1, 0, 2)
    d["ident"] = np.eye(P, dtype=np.float32)
    d["headmask"] = np.kron(np.eye(H, dtype=np.float32), np.ones((P // H, 1), np.float32))
    d["L0_wqT"], d["L0_wkT"] = rows(f["L0_xattn_Wq"].T), rows(f["L0_xattn_Wk"].T)
    d["L0_wvT"], d["L0_wo"] = rows(f["L0_xattn_Wv"].T), rows(f["L0_xattn_Wo"])
    d["L0_bo"] = f["L0_xattn_bo"]
    zero = np.zeros(P, np.float32)
    eye = np.eye(P, dtype=np.float32)
    d["L1_w4"] = np.stack([eye, eye, eye, f["L1_xattn_w_proj"].T], axis=1)
    d["L1_cols"] = np.stack([zero, zero, zero], axis=1)
    d["L1_bo"] = f["L1_xattn_b_proj"]
    d["L2_w4"] = np.stack([f["L2_xattn_wq"], f["L2_xattn_wk"], f["L2_xattn_wv"], f["L2_xattn_wo"]], axis=1)
    d["L2_cols"] = np.stack([zero, zero, zero], axis=1)
    d["L2_bo"] = f["L2_xattn_bo"]
    d["L3_w4"] = np.stack([f["L3_xattn_Wq"].T, f["L3_xattn_Wk"].T, f["L3_xattn_Wv"].T, f["L3_xattn_Wo"].T], axis=1)
    d["L3_cols"] = np.stack([f["L3_xattn_bq"], f["L3_xattn_bk"], f["L3_xattn_bv"]], axis=1)
    d["L3_bo"] = f["L3_xattn_bo"]
    d["desc8"] = np.arange(8, 0, -1).astype(np.float32)
    d["F0_wd"] = f["L0_ffn_W_down"].transpose(1, 0, 2).reshape(P, 512)
    d["F0_wu"] = rows(f["L0_ffn_W_up"].reshape(512, P))
    d["F0_wr"], d["F0_br"], d["F0_bup"] = f["L0_ffn_Wr"], f["L0_ffn_br"], f["L0_ffn_b_up"]
    d["F0_cols"] = np.concatenate([np.stack([f["L0_ffn_" + k] for k in ("bn_var", "bn_g", "bn_b", "bn_mean", "ln_g", "ln_b")],
                                            axis=1), f["L0_ffn_b_down"].reshape(4, P).T], axis=1)

    def joined(a, b):
        return np.concatenate([a, b[None]], axis=0)

    def chunked(a):
        out = np.zeros((L1_CH * P, a.shape[1]), a.dtype)
        out[:L1_ALL] = a
        return rows(out)

    for k in ("w1", "w3"):
        d["F1_" + k] = joined(f["L1_ffn_" + k], f["L1_ffn_s" + k]).transpose(1, 0, 2).reshape(P, L1_ALL)
    d["F1_w2"] = chunked(joined(f["L1_ffn_w2"], f["L1_ffn_sw2"]).reshape(L1_ALL, P))
    d["F1_cols"] = np.concatenate([chunked(joined(f["L1_ffn_" + k], f["L1_ffn_s" + k]).reshape(L1_ALL, 1))[:, :, 0]
                                   for k in ("b1", "b3")], axis=1)
    d["F1_b2"] = np.concatenate([joined(f["L1_ffn_b2"], f["L1_ffn_sb2"])] * 3, axis=0)
    d["F1_gw"], d["F1_gb"] = f["L1_ffn_gate_w"].T, f["L1_ffn_gate_b"]
    d["F1_sel"] = np.concatenate([np.kron(np.eye(L1_E + 1, dtype=np.float32), np.ones((1, L1_H), np.float32))] * 3, axis=0)

    d["desc16"] = np.arange(L2_E, 0, -1).astype(np.float32)
    d["F2_sim"], d["F2_gates"] = f["L2_ffn_sim_matrix"], f["L2_ffn_gates"]
    d["ones"] = np.ones((P, P), np.float32)
    d["tri"] = np.triu(np.full((P, P), NEG, np.float32), 1)
    d["F2_sel"] = np.concatenate([np.kron(np.eye(L2_E, dtype=np.float32), np.ones((1, P), np.float32))] * 3, axis=0)
    for k in "qkvo":
        d["F2_w" + k] = f[f"L2_ffn_{k}_proj"].transpose(1, 0, 2)
    d["F3_w"] = np.stack([rows(f["L3_ffn_w_gate"]).reshape(P, L3_I), rows(f["L3_ffn_w_up"]).reshape(P, L3_I),
                          f["L3_ffn_w_down"]], axis=1)
    return d


def kernel(**inputs):
    import numpy as _np
    import concourse.bacc as _bacc
    from concourse import mybir as _mybir
    from concourse.bass_utils import run_bass_kernel_spmd as _run

    nc = _bacc.Bacc("TRN2", target_bir_lowering=False, num_devices=1)
    arrays, dram = {}, {}
    for name, a in laid_out(inputs).items():
        a = _np.ascontiguousarray(a)
        arrays[f"in_{name}"] = a
        dram[name] = nc.dram_tensor(f"in_{name}", a.shape, _mybir.dt.from_np(a.dtype), kind="ExternalInput").ap()
    out = nc.dram_tensor("out_0", (P, TILES, P), F32, kind="ExternalOutput").ap()
    build(nc, dram, out)
    r = _run(nc, [arrays], core_ids=[0])
    got = r.results[0]["out_0"]
    return _np.ascontiguousarray(got.transpose(1, 0, 2)).reshape(B, S, P)
```
